# Optimizing a Trainium2 kernel written in Bass

```python
import numpy as np
import jax
import jax.numpy as jnp

def _softmax(x, axis=-1):
    return jax.nn.softmax(x, axis=axis)

def _gelu(x):
    return jax.nn.gelu(x, approximate=True)

def _silu(x):
    return jax.nn.silu(x)

def _sigmoid(x):
    return jax.nn.sigmoid(x)

def _layernorm(x, axis=-1, eps=1e-05):
    m = jnp.mean(x, axis=axis, keepdims=True)
    v = jnp.var(x, axis=axis, keepdims=True)
    return (x - m) / jnp.sqrt(v + eps)

def _scatter_add(tgt, idx, src, axis=0):
    return tgt.at[idx].add(src)

def _segment_sum(src, seg, n):
    return jax.ops.segment_sum(src, seg, n)
kernel_name = 'mk_seq_postln_d2_jaxref_r4_0f5034'

def setup_inputs(seed: int=0):
    np.random.seed(seed)
    _w = jnp.asarray

    def _L0_attn_setup():
        import jax, jax.numpy as jnp
        import numpy as np
        import math
        from jax import lax
        B, L, D = (8, 1024, 256)
        FILTER_ORDER = 64
        EMB_DIM = 3
        SHIFT = 0.05
        KSIZE = 3

        def _implicit_filter(f_w1, f_b1, freq1, f_w2, f_b2, freq2, f_w3, f_b3, freq3, f_wout):
            t = jnp.linspace(0.0, 1.0, L)
            t_resc = jnp.linspace(0.0, L - 1.0, L)
            w = 2.0 * jnp.pi * t_resc / L
            bands = (EMB_DIM - 1) // 2
            f = jnp.linspace(0.0001, bands - 1.0, bands)
            fw = f[None, :] * w[:, None]
            z = jnp.concatenate([t[:, None], jnp.cos(fw), -jnp.sin(fw)], axis=-1)
            h = jnp.sin(freq1 * (z @ f_w1 + f_b1))
            h = jnp.sin(freq2 * (h @ f_w2 + f_b2))
            h = jnp.sin(freq3 * (h @ f_w3 + f_b3))
            h = h @ f_wout
            max_decay = math.log(0.01) / 0.3
            min_decay = math.log(0.01) / 1.5
            deltas = jnp.linspace(min_decay, max_decay, D)
            decay = jnp.exp(-t[:, None] * jnp.abs(deltas)[None, :])
            return h * (decay + SHIFT)
        key = jax.random.key(seed)
        ks = jax.random.split(key, 12)
        s = 0.02
        return {'u': jax.random.normal(ks[0], (B, L, D), jnp.float32), 'w_in': jax.random.normal(ks[1], (D, 3 * D), jnp.float32) * s, 'b_in': jnp.zeros((3 * D,), jnp.float32), 'sf_w': jax.random.normal(ks[2], (3 * D, KSIZE), jnp.float32) * 0.3, 'sf_b': jnp.zeros((3 * D,), jnp.float32), 'f_w1': jax.random.normal(ks[3], (EMB_DIM, FILTER_ORDER), jnp.float32) * 0.5, 'f_b1': jnp.zeros((FILTER_ORDER,), jnp.float32), 'freq1': jnp.ones((FILTER_ORDER,), jnp.float32), 'f_w2': jax.random.normal(ks[4], (FILTER_ORDER, FILTER_ORDER), jnp.float32) * 0.12, 'f_b2': jnp.zeros((FILTER_ORDER,), jnp.float32), 'freq2': jnp.ones((FILTER_ORDER,), jnp.float32), 'f_w3': jax.random.normal(ks[5], (FILTER_ORDER, FILTER_ORDER), jnp.float32) * 0.12, 'f_b3': jnp.zeros((FILTER_ORDER,), jnp.float32), 'freq3': jnp.ones((FILTER_ORDER,), jnp.float32), 'f_wout': jax.random.normal(ks[6], (FILTER_ORDER, D), jnp.float32) * s, 'filt_bias': jax.random.normal(ks[7], (D,), jnp.float32), 'w_out': jax.random.normal(ks[8], (D, D), jnp.float32) * s, 'b_out': jnp.zeros((D,), jnp.float32)}
    _L0_attn_in = _L0_attn_setup()

    def _L0_ffn_setup():
        import jax, jax.numpy as jnp
        import numpy as np
        D_MODEL = 256
        N_EXPERTS = 8
        TOP_K = 2
        key = jax.random.key(seed)
        k1, k2, k3, k4 = jax.random.split(key, 4)
        B, S, D, E = (4, 512, D_MODEL, N_EXPERTS)
        dff = 4 * D
        lim = float(np.sqrt(6.0 / (D + dff)))
        return {'x': jax.random.normal(k1, (B, S, D), dtype=jnp.float32), 'router_w': jax.random.normal(k2, (D, E), dtype=jnp.float32) * (1.0 / np.sqrt(D)), 'router_b': jnp.zeros((E,), dtype=jnp.float32), 'expert_up': jax.random.uniform(k3, (E, dff, D), dtype=jnp.float32, minval=-lim, maxval=lim), 'expert_down': jax.random.uniform(k4, (E, D, dff), dtype=jnp.float32, minval=-lim, maxval=lim)}
    _L0_ffn_in = _L0_ffn_setup()

    def _L1_attn_setup():
        import jax, jax.numpy as jnp
        import numpy as np
        DIM = 256
        H = 16
        D = DIM // H
        CS = 64
        SCALE = D ** (-0.5)
        key = jax.random.key(seed)
        k1, k2, k3 = jax.random.split(key, 3)
        B, N = (4, 1024)
        x = jax.random.normal(k1, (B, N, DIM), dtype=jnp.float32)
        W_qkv = jax.random.normal(k2, (DIM, 3 * DIM), dtype=jnp.float32) * DIM ** (-0.5)
        W_out = jax.random.normal(k3, (DIM, DIM), dtype=jnp.float32) * DIM ** (-0.5)
        return {'x': x, 'W_qkv': W_qkv, 'W_out': W_out}
    _L1_attn_in = _L1_attn_setup()

    def _L1_ffn_setup():
        import jax, jax.numpy as jnp
        import numpy as np
        DIM = 256
        DEPTH = 2
        HEADS = 8
        DIM_HEAD = 64
        WINDOW = 128
        INNER = HEADS * DIM_HEAD
        HID = int(DIM * 4 * 2 / 3)
        B, N = (2, 2048)
        QK_SCALE = 8.0

        def shift_token(t):
            t1, t2 = jnp.split(t, 2, axis=-1)
            t2 = jnp.pad(t2, ((0, 0), (1, 0), (0, 0)))[:, :-1]
            return jnp.concatenate([t1, t2], axis=-1)

        def l2norm(t):
            return t / jnp.clip(jnp.linalg.norm(t, axis=-1, keepdims=True), 1e-12)

        def rotate_half(x):
            x1, x2 = jnp.split(x, 2, axis=-1)
            return jnp.concatenate([-x2, x1], axis=-1)

        def rotary_xpos(q, k):
            n = q.shape[-2]
            half_idx = jnp.arange(0, DIM_HEAD, 2, dtype=jnp.float32)
            inv_freq = 1.0 / 10000.0 ** (half_idx / DIM_HEAD)
            t = jnp.arange(n, dtype=jnp.float32)
            freqs = t[:, None] * inv_freq[None, :]
            freqs = jnp.concatenate([freqs, freqs], axis=-1)
            base = (half_idx + 0.4 * DIM_HEAD) / (1.4 * DIM_HEAD)
            power = (t - n // 2) / float(WINDOW // 2)
            scale = base[None, :] ** power[:, None]
            scale = jnp.concatenate([scale, scale], axis=-1)
            cos, sin = (jnp.cos(freqs), jnp.sin(freqs))
            q = q * cos * scale + rotate_half(q) * sin * scale
            k = k * cos / scale + rotate_half(k) * sin / scale
            return (q, k)

        def local_attention(q, k, v):
            b, h, n, d = q.shape
            w = n // WINDOW
            bq = q.reshape(b, h, w, WINDOW, d) * QK_SCALE
            bk = k.reshape(b, h, w, WINDOW, d)
            bv = v.reshape(b, h, w, WINDOW, d)

            def look_around(t):
                p = jnp.pad(t, ((0, 0), (0, 0), (1, 0), (0, 0), (0, 0)))
                return jnp.concatenate([p[:, :, :w], p[:, :, 1:]], axis=3)
            bk, bv = (look_around(bk), look_around(bv))
            bt = jnp.arange(n).reshape(w, WINDOW)
            btp = jnp.pad(bt, ((1, 0), (0, 0)), constant_values=-1)
            btk = jnp.concatenate([btp[:w], btp[1:]], axis=1)
            sim = jnp.einsum('bhwid,bhwjd->bhwij', bq, bk)
            i = bt[:, :, None]
            j = btk[:, None, :]
            mask = (i < j) | (i > j + WINDOW) | (j == -1)
            sim = jnp.where(mask, -jnp.finfo(sim.dtype).max, sim)
            attn = jax.nn.softmax(sim, axis=-1)
            out = jnp.einsum('bhwij,bhwjd->bhwid', attn, bv)
            return out.reshape(b, h, n, d)

        def _layer(x, wqkv, qs, ksc, wo, lg, lb, w1, b1, w2, b2):
            b, n, _ = x.shape
            h = shift_token(x)
            qkv = h @ wqkv
            q, k, v = jnp.split(qkv, 3, axis=-1)
            to_heads = lambda t: t.reshape(b, n, HEADS, DIM_HEAD).transpose(0, 2, 1, 3)
            q, k, v = (to_heads(q), to_heads(k), to_heads(v))
            q = l2norm(q) * qs
            k = l2norm(k) * ksc
            q, k = rotary_xpos(q, k)
            o = local_attention(q, k, v)
            o = o.transpose(0, 2, 1, 3).reshape(b, n, INNER)
            x = x + o @ wo
            h = shift_token(x)
            mu = h.mean(-1, keepdims=True)
            var = h.var(-1, keepdims=True)
            h = (h - mu) / jnp.sqrt(var + 1e-05) * lg + lb
            h = h @ w1 + b1
            a, g = jnp.split(h, 2, axis=-1)
            h = a * jax.nn.gelu(g, approximate=False)
            x = x + h @ w2 + b2
            return x
        key = jax.random.key(seed)
        ks = jax.random.split(key, 6)
        return {'x': jax.random.normal(ks[0], (B, N, DIM), jnp.float32), 'wqkv': jax.random.normal(ks[1], (DEPTH, DIM, 3 * INNER), jnp.float32) * 0.02, 'q_scale': jnp.ones((DEPTH, DIM_HEAD), jnp.float32), 'k_scale': jnp.ones((DEPTH, DIM_HEAD), jnp.float32), 'wo': jax.random.normal(ks[2], (DEPTH, INNER, DIM), jnp.float32) * 0.02, 'ln_g': jnp.ones((DEPTH, DIM), jnp.float32), 'ln_b': jnp.zeros((DEPTH, DIM), jnp.float32), 'w1': jax.random.normal(ks[3], (DEPTH, DIM, 2 * HID), jnp.float32) * 0.02, 'b1': jnp.zeros((DEPTH, 2 * HID), jnp.float32), 'w2': jax.random.normal(ks[4], (DEPTH, HID, DIM), jnp.float32) * 0.02, 'b2': jnp.zeros((DEPTH, DIM), jnp.float32)}
    _L1_ffn_in = _L1_ffn_setup()
    _d = {'L0_attn_u': _L0_attn_in['u'], 'L0_attn_w_in': _L0_attn_in['w_in'], 'L0_attn_b_in': _L0_attn_in['b_in'], 'L0_attn_sf_w': _L0_attn_in['sf_w'], 'L0_attn_sf_b': _L0_attn_in['sf_b'], 'L0_attn_f_w1': _L0_attn_in['f_w1'], 'L0_attn_f_b1': _L0_attn_in['f_b1'], 'L0_attn_freq1': _L0_attn_in['freq1'], 'L0_attn_f_w2': _L0_attn_in['f_w2'], 'L0_attn_f_b2': _L0_attn_in['f_b2'], 'L0_attn_freq2': _L0_attn_in['freq2'], 'L0_attn_f_w3': _L0_attn_in['f_w3'], 'L0_attn_f_b3': _L0_attn_in['f_b3'], 'L0_attn_freq3': _L0_attn_in['freq3'], 'L0_attn_f_wout': _L0_attn_in['f_wout'], 'L0_attn_filt_bias': _L0_attn_in['filt_bias'], 'L0_attn_w_out': _L0_attn_in['w_out'], 'L0_attn_b_out': _L0_attn_in['b_out'], 'L0_ffn_router_w': _L0_ffn_in['router_w'], 'L0_ffn_router_b': _L0_ffn_in['router_b'], 'L0_ffn_expert_up': _L0_ffn_in['expert_up'], 'L0_ffn_expert_down': _L0_ffn_in['expert_down'], 'L1_attn_W_qkv': _L1_attn_in['W_qkv'], 'L1_attn_W_out': _L1_attn_in['W_out'], 'L1_ffn_wqkv': _L1_ffn_in['wqkv'], 'L1_ffn_q_scale': _L1_ffn_in['q_scale'], 'L1_ffn_k_scale': _L1_ffn_in['k_scale'], 'L1_ffn_wo': _L1_ffn_in['wo'], 'L1_ffn_ln_g': _L1_ffn_in['ln_g'], 'L1_ffn_ln_b': _L1_ffn_in['ln_b'], 'L1_ffn_w1': _L1_ffn_in['w1'], 'L1_ffn_b1': _L1_ffn_in['b1'], 'L1_ffn_w2': _L1_ffn_in['w2'], 'L1_ffn_b2': _L1_ffn_in['b2']}
    _x0 = _d['L0_attn_u']
    _d['L0_attn_u'] = jax.random.normal(jax.random.fold_in(jax.random.key(seed), 1), (1, 4096, 256), dtype=_x0.dtype)
    del _x0
    return _d

def reference(L0_attn_u, L0_attn_w_in, L0_attn_b_in, L0_attn_sf_w, L0_attn_sf_b, L0_attn_f_w1, L0_attn_f_b1, L0_attn_freq1, L0_attn_f_w2, L0_attn_f_b2, L0_attn_freq2, L0_attn_f_w3, L0_attn_f_b3, L0_attn_freq3, L0_attn_f_wout, L0_attn_filt_bias, L0_attn_w_out, L0_attn_b_out, L0_ffn_router_w, L0_ffn_router_b, L0_ffn_expert_up, L0_ffn_expert_down, L1_attn_W_qkv, L1_attn_W_out, L1_ffn_wqkv, L1_ffn_q_scale, L1_ffn_k_scale, L1_ffn_wo, L1_ffn_ln_g, L1_ffn_ln_b, L1_ffn_w1, L1_ffn_b1, L1_ffn_w2, L1_ffn_b2):

    def _L0_attn_ref(u, w_in, b_in, sf_w, sf_b, f_w1, f_b1, freq1, f_w2, f_b2, freq2, f_w3, f_b3, freq3, f_wout, filt_bias, w_out, b_out):
        import jax, jax.numpy as jnp
        import numpy as np
        import math
        from jax import lax
        B, L, D = (8, 1024, 256)
        FILTER_ORDER = 64
        EMB_DIM = 3
        SHIFT = 0.05
        KSIZE = 3

        def _implicit_filter(f_w1, f_b1, freq1, f_w2, f_b2, freq2, f_w3, f_b3, freq3, f_wout):
            t = jnp.linspace(0.0, 1.0, L)
            t_resc = jnp.linspace(0.0, L - 1.0, L)
            w = 2.0 * jnp.pi * t_resc / L
            bands = (EMB_DIM - 1) // 2
            f = jnp.linspace(0.0001, bands - 1.0, bands)
            fw = f[None, :] * w[:, None]
            z = jnp.concatenate([t[:, None], jnp.cos(fw), -jnp.sin(fw)], axis=-1)
            h = jnp.sin(freq1 * (z @ f_w1 + f_b1))
            h = jnp.sin(freq2 * (h @ f_w2 + f_b2))
            h = jnp.sin(freq3 * (h @ f_w3 + f_b3))
            h = h @ f_wout
            max_decay = math.log(0.01) / 0.3
            min_decay = math.log(0.01) / 1.5
            deltas = jnp.linspace(min_decay, max_decay, D)
            decay = jnp.exp(-t[:, None] * jnp.abs(deltas)[None, :])
            return h * (decay + SHIFT)
        b, l, d = u.shape
        up = (u @ w_in + b_in).transpose(0, 2, 1)
        uc = lax.conv_general_dilated(up, sf_w[:, None, :], (1,), [(KSIZE - 1, KSIZE - 1)], feature_group_count=3 * d, dimension_numbers=('NCH', 'OIH', 'NCH'))[..., :l] + sf_b[None, :, None]
        x0, x1, v = jnp.split(uc, 3, axis=1)
        k = _implicit_filter(f_w1, f_b1, freq1, f_w2, f_b2, freq2, f_w3, f_b3, freq3, f_wout).T
        v = v * x1
        n = 2 * l
        y = jnp.fft.irfft(jnp.fft.rfft(v, n=n) * jnp.fft.rfft(k, n=n), n=n)[..., :l]
        v = y + v * filt_bias[None, :, None]
        out = (v * x0).transpose(0, 2, 1)
        return out @ w_out + b_out

    def _L0_ffn_ref(x, router_w, router_b, expert_up, expert_down):
        import jax, jax.numpy as jnp
        import numpy as np
        D_MODEL = 256
        N_EXPERTS = 8
        TOP_K = 2
        B, S, D = x.shape
        E = expert_up.shape[0]
        x_flat = x.reshape(-1, D)
        logits = x_flat @ router_w + router_b
        probs = jax.nn.softmax(logits, axis=-1)
        top_w, top_idx = jax.lax.top_k(probs, TOP_K)
        comb = jnp.sum(top_w[..., None] * jax.nn.one_hot(top_idx, E, dtype=x.dtype), axis=1)
        output = jnp.zeros_like(x_flat)
        for e in range(E):
            h = jax.nn.gelu(x_flat @ expert_up[e].T, approximate=False)
            out_e = h @ expert_down[e].T
            output = output + comb[:, e:e + 1] * out_e
        return output.reshape(B, S, D)

    def _L1_attn_ref(x, W_qkv, W_out):
        import jax, jax.numpy as jnp
        import numpy as np
        DIM = 256
        H = 16
        D = DIM // H
        CS = 64
        SCALE = D ** (-0.5)
        B, N, C = x.shape
        qkv = (x @ W_qkv).reshape(B, N, 3, H, D)
        qkv = jnp.transpose(qkv, (2, 0, 3, 1, 4))
        q, k, v = (qkv[0], qkv[1], qkv[2])
        nc = N // CS
        q = q.reshape(B, H, nc, CS, D)
        k = k.reshape(B, H, nc, CS, D)
        v = v.reshape(B, H, nc, CS, D)
        attn = jnp.einsum('bhcqd,bhckd->bhcqk', q, k) * SCALE
        mask = jnp.triu(jnp.ones((CS, CS), dtype=bool), k=1)
        attn = jnp.where(mask, jnp.float32(-65000.0), attn)
        attn = jax.nn.softmax(attn, axis=-1)
        out_local = jnp.einsum('bhcqk,bhckd->bhcqd', attn, v)
        chunk_k = k.mean(axis=3)
        chunk_v = v.mean(axis=3)
        cum_k = jnp.cumsum(chunk_k, axis=2)
        cum_v = jnp.cumsum(chunk_v, axis=2)
        zeros = jnp.zeros((B, H, 1, D), dtype=x.dtype)
        cum_k = jnp.concatenate([zeros, cum_k[:, :, :-1]], axis=2)
        cum_v = jnp.concatenate([zeros, cum_v[:, :, :-1]], axis=2)
        cross = jax.nn.sigmoid(jnp.einsum('bhcsd,bhcd->bhcs', q, cum_k) * SCALE)
        out = out_local + cross[..., None] * cum_v[:, :, :, None, :] * 0.5
        out = out.reshape(B, H, N, D)
        out = jnp.transpose(out, (0, 2, 1, 3)).reshape(B, N, C)
        return out @ W_out

    def _L1_ffn_ref(x, wqkv, q_scale, k_scale, wo, ln_g, ln_b, w1, b1, w2, b2):
        import jax, jax.numpy as jnp
        import numpy as np
        DIM = 256
        DEPTH = 2
        HEADS = 8
        DIM_HEAD = 64
        WINDOW = 128
        INNER = HEADS * DIM_HEAD
        HID = int(DIM * 4 * 2 / 3)
        B, N = (2, 2048)
        QK_SCALE = 8.0

        def shift_token(t):
            t1, t2 = jnp.split(t, 2, axis=-1)
            t2 = jnp.pad(t2, ((0, 0), (1, 0), (0, 0)))[:, :-1]
            return jnp.concatenate([t1, t2], axis=-1)

        def l2norm(t):
            return t / jnp.clip(jnp.linalg.norm(t, axis=-1, keepdims=True), 1e-12)

        def rotate_half(x):
            x1, x2 = jnp.split(x, 2, axis=-1)
            return jnp.concatenate([-x2, x1], axis=-1)

        def rotary_xpos(q, k):
            n = q.shape[-2]
            half_idx = jnp.arange(0, DIM_HEAD, 2, dtype=jnp.float32)
            inv_freq = 1.0 / 10000.0 ** (half_idx / DIM_HEAD)
            t = jnp.arange(n, dtype=jnp.float32)
            freqs = t[:, None] * inv_freq[None, :]
            freqs = jnp.concatenate([freqs, freqs], axis=-1)
            base = (half_idx + 0.4 * DIM_HEAD) / (1.4 * DIM_HEAD)
            power = (t - n // 2) / float(WINDOW // 2)
            scale = base[None, :] ** power[:, None]
            scale = jnp.concatenate([scale, scale], axis=-1)
            cos, sin = (jnp.cos(freqs), jnp.sin(freqs))
            q = q * cos * scale + rotate_half(q) * sin * scale
            k = k * cos / scale + rotate_half(k) * sin / scale
            return (q, k)

        def local_attention(q, k, v):
            b, h, n, d = q.shape
            w = n // WINDOW
            bq = q.reshape(b, h, w, WINDOW, d) * QK_SCALE
            bk = k.reshape(b, h, w, WINDOW, d)
            bv = v.reshape(b, h, w, WINDOW, d)

            def look_around(t):
                p = jnp.pad(t, ((0, 0), (0, 0), (1, 0), (0, 0), (0, 0)))
                return jnp.concatenate([p[:, :, :w], p[:, :, 1:]], axis=3)
            bk, bv = (look_around(bk), look_around(bv))
            bt = jnp.arange(n).reshape(w, WINDOW)
            btp = jnp.pad(bt, ((1, 0), (0, 0)), constant_values=-1)
            btk = jnp.concatenate([btp[:w], btp[1:]], axis=1)
            sim = jnp.einsum('bhwid,bhwjd->bhwij', bq, bk)
            i = bt[:, :, None]
            j = btk[:, None, :]
            mask = (i < j) | (i > j + WINDOW) | (j == -1)
            sim = jnp.where(mask, -jnp.finfo(sim.dtype).max, sim)
            attn = jax.nn.softmax(sim, axis=-1)
            out = jnp.einsum('bhwij,bhwjd->bhwid', attn, bv)
            return out.reshape(b, h, n, d)

        def _layer(x, wqkv, qs, ksc, wo, lg, lb, w1, b1, w2, b2):
            b, n, _ = x.shape
            h = shift_token(x)
            qkv = h @ wqkv
            q, k, v = jnp.split(qkv, 3, axis=-1)
            to_heads = lambda t: t.reshape(b, n, HEADS, DIM_HEAD).transpose(0, 2, 1, 3)
            q, k, v = (to_heads(q), to_heads(k), to_heads(v))
            q = l2norm(q) * qs
            k = l2norm(k) * ksc
            q, k = rotary_xpos(q, k)
            o = local_attention(q, k, v)
            o = o.transpose(0, 2, 1, 3).reshape(b, n, INNER)
            x = x + o @ wo
            h = shift_token(x)
            mu = h.mean(-1, keepdims=True)
            var = h.var(-1, keepdims=True)
            h = (h - mu) / jnp.sqrt(var + 1e-05) * lg + lb
            h = h @ w1 + b1
            a, g = jnp.split(h, 2, axis=-1)
            h = a * jax.nn.gelu(g, approximate=False)
            x = x + h @ w2 + b2
            return x
        for l in range(DEPTH):
            x = _layer(x, wqkv[l], q_scale[l], k_scale[l], wo[l], ln_g[l], ln_b[l], w1[l], b1[l], w2[l], b2[l])
        return x
    x = L0_attn_u
    x = _layernorm(x + _L0_attn_ref(x, L0_attn_w_in, L0_attn_b_in, L0_attn_sf_w, L0_attn_sf_b, L0_attn_f_w1, L0_attn_f_b1, L0_attn_freq1, L0_attn_f_w2, L0_attn_f_b2, L0_attn_freq2, L0_attn_f_w3, L0_attn_f_b3, L0_attn_freq3, L0_attn_f_wout, L0_attn_filt_bias, L0_attn_w_out, L0_attn_b_out), axis=-1)
    x = _layernorm(x + _L0_ffn_ref(x, L0_ffn_router_w, L0_ffn_router_b, L0_ffn_expert_up, L0_ffn_expert_down), axis=-1)
    x = _layernorm(x + _L1_attn_ref(x, L1_attn_W_qkv, L1_attn_W_out), axis=-1)
    x = _layernorm(x + _L1_ffn_ref(x, L1_ffn_wqkv, L1_ffn_q_scale, L1_ffn_k_scale, L1_ffn_wo, L1_ffn_ln_g, L1_ffn_ln_b, L1_ffn_w1, L1_ffn_b1, L1_ffn_w2, L1_ffn_b2), axis=-1)
    return x

_drawn_inputs = setup_inputs


def setup_inputs(seed=0):
    import zlib

    import numpy as np

    out = dict(_drawn_inputs(seed))
    spreads = {'L0_attn_b_in': (0.0, 0.1),
     'L0_attn_sf_b': (0.0, 0.1),
     'L0_attn_f_b1': (0.0, 0.8),
     'L0_attn_freq1': (1.0, 0.6),
     'L0_attn_f_b2': (0.0, 0.628),
     'L0_attn_freq2': (1.0, 0.6),
     'L0_attn_f_b3': (0.0, 0.431),
     'L0_attn_freq3': (1.0, 0.6),
     'L0_attn_b_out': (0.0, 0.1),
     'L0_ffn_router_b': (0.0, 0.1),
     'L1_ffn_q_scale': (1.0, 0.6),
     'L1_ffn_k_scale': (1.0, 0.6),
     'L1_ffn_ln_g': (1.0, 0.6),
     'L1_ffn_ln_b': (0.0, 0.8),
     'L1_ffn_b1': (0.0, 0.8),
     'L1_ffn_b2': (0.0, 0.1)}
    factors = {'L0_attn_w_in': 5.089, 'L0_attn_filt_bias': 8.0}
    for name, (base, spread) in spreads.items():
        noise = np.random.default_rng([zlib.crc32(name.encode()), seed]).standard_normal(out[name].shape)
        drawn = base * np.exp(spread * noise) if base else spread * noise
        out[name] = jnp.asarray(drawn.astype(out[name].dtype))
    for name, factor in factors.items():
        out[name] = (out[name] * factor).astype(out[name].dtype)
    return out
```

```python
from contextlib import ExitStack

import numpy as np

import concourse.bass as bass
import concourse.mybir as mybir

F32 = mybir.dt.float32
I32 = mybir.dt.int32
U32 = mybir.dt.uint32
ALU = mybir.AluOpType
ACT = mybir.ActivationFunctionType
AX_X = mybir.AxisListType.X

P = 128
TOKENS = 4096
DIM = 256
TILES = TOKENS // P
KT = DIM // P
EPS = 1e-5
DMA = 16


class Count:

    def __init__(self, sem, per_tile=1, by=1):
        self.sem = sem
        self.n, self.by = per_tile, by

    def prime(self, engine):
        engine.sem_inc(self.sem, 2 * self.n * self.by)

    def at(self, tile, k=None):
        return ((tile + 2) * self.n + (self.n if k is None else k)) * self.by


def wait(engine, count, tile, k=None):
    engine.wait_ge(count.sem, count.at(tile, k))


class Scope:

    def __init__(self, nc, stack, phase):
        self.nc, self.stack, self.phase, self.sems = nc, stack, phase, []
        stack.callback(self.release)

    def release(self):
        self.nc.clear_and_free_semaphores(self.sems)
        self.nc.all_engine_barrier()

    def sbuf(self, name, shape, dtype=F32):
        return self.stack.enter_context(self.nc.sbuf_tensor(f"{self.phase}_{name}", shape, dtype))

    def psum(self, name, shape, dtype=F32):
        return self.stack.enter_context(self.nc.psum_tensor(f"{self.phase}_{name}", shape, dtype))

    def sem(self, name):
        self.sems.append(self.nc.alloc_semaphore(f"{self.phase}_{name}"))
        return self.sems[-1]

    def count(self, name, per_tile=1, by=1):
        return Count(self.sem(name), per_tile, by)


def tile_pairs(engine, pairs, body):
    for u in (0, 1):
        body(u, u, 0, True)
    with engine.Fori(1, pairs - 1) as i:
        for u in (0, 1):
            body(i * 2 + u, u, i, True)
    for u in (0, 1):
        body(2 * (pairs - 1) + u, u, pairs - 1, u == 0)


def first(tile):
    return isinstance(tile, int) and tile == 0


def last(tile):
    return isinstance(tile, int) and tile == TILES - 1
HEADS = 8
HEAD_DIM = 64
INNER = HEADS * HEAD_DIM
PAIRS = HEADS // 2
NEG = -1e25


def window_attention(nc, layer, x_in, x_out, wqkv, qk_scale, wo, rotary, ident_dram, mask_dram):
    with ExitStack() as stack:
        s = Scope(nc, stack, f"win{layer}")
        w_qkv = s.sbuf("w_qkv", [P, KT, 3 * INNER])
        w_o = s.sbuf("w_o", [P, INNER // P, DIM])
        ident = s.sbuf("ident", [P, P])
        mask = s.sbuf("mask", [P, 3, 2, P])
        scales = s.sbuf("scales", [P, 4, HEAD_DIM])
        minus_half = s.sbuf("minus_half", [P, 2 * HEADS])
        x = [s.sbuf(f"x{u}", [P, DIM]) for u in (0, 1)]
        x_res = [s.sbuf(f"x_res{u}", [P, DIM]) for u in (0, 1)]
        x_shift = [s.sbuf(f"x_shift{u}", [P, P]) for u in (0, 1)]
        rot = [s.sbuf(f"rot{u}", [P, 4, HEAD_DIM]) for u in (0, 1)]
        rot_s = [s.sbuf(f"rot_s{u}", [P, 4, HEAD_DIM]) for u in (0, 1)]
        hT = s.sbuf("hT", [P, KT, P])
        squares = s.sbuf("squares", [P, 2, INNER])
        norm2 = s.sbuf("norm2", [P, 2, HEADS])
        inv_norm = s.sbuf("inv_norm", [P, 2, HEADS])
        q_gain = [s.sbuf(f"q_gain{u}", [P, HEADS]) for u in (0, 1)]
        by_cos = s.sbuf("by_cos", [P, 2, HEADS, HEAD_DIM])
        by_sin = s.sbuf("by_sin", [P, 2, HEADS, HEAD_DIM])
        turned = s.sbuf("turned", [P, 2, HEADS, HEAD_DIM])
        k_turned = s.sbuf("k_turned", [P, HEADS, HEAD_DIM])
        qT = s.sbuf("qT", [P, PAIRS, P])
        kT = s.sbuf("kT", [P, PAIRS, 2, 2, P])
        v = s.sbuf("v", [P, 2, INNER])
        masked = s.sbuf("masked", [P, 2, 2, 2 * P])
        top = s.sbuf("top", [P, PAIRS, 2])
        bias = s.sbuf("bias", [P, PAIRS, 2])
        probs = s.sbuf("probs", [P, 2, 2, 2 * P])
        spare = s.sbuf("spare", [P, 2])
        total = s.sbuf("total", [P, HEADS])
        inv_total = s.sbuf("inv_total", [P, HEADS])
        pT = s.sbuf("pT", [P, 2, 4, P])
        o = s.sbuf("o", [P, INNER])
        oT = s.sbuf("oT", [P, INNER // P, P])
        y = [s.sbuf(f"y{u}", [P, DIM]) for u in (0, 1)]

        ps_qk = s.psum("ps_qk", [P, 2, INNER])
        ps_v = s.psum("ps_v", [P, INNER])
        ps_T = s.psum("ps_T", [P, 2, 4, P])
        ps_s = s.psum("ps_s", [P, 2, 2, 2 * P])
        ps_o = s.psum("ps_o", [P, INNER])

        weights_in = s.sem("weights_in")
        const_in = s.sem("const_in")
        consts_set = s.sem("consts_set")
        x_loaded = [s.sem(f"x_loaded{u}") for u in (0, 1)]
        res_loaded = [s.sem(f"res_loaded{u}") for u in (0, 1)]
        y_stored = [s.sem(f"y_stored{u}") for u in (0, 1)]
        c = lambda name, n=1: s.count(name, n)
        hT_ps, hT_sb, qk_ps, v_ps, v_sb = c("hT_ps"), c("hT_sb"), c("qk_ps"), c("v_ps"), c("v_sb")
        rot_ready, squared, normed2 = c("rot_ready"), c("squared"), c("normed2")
        norm_floor, norm_inv, gain = c("norm_floor"), c("norm_inv"), c("gain")
        cos_done, sin_done, turned_done, k_done = c("cos_done"), c("sin_done", 2), c("turned_done"), c("k_done")
        qT_ps, kT_ps, qT_sb, kT_sb = c("qT_ps"), c("kT_ps"), c("qT_sb"), c("kT_sb", 2)
        s_ps, s_masked, bias_done = c("s_ps", PAIRS), c("s_masked", HEADS), c("bias_done", PAIRS)
        exp_done, pT_ps, pT_sb, pv_done = c("exp_done", HEADS), c("pT_ps", PAIRS), c("pT_sb", PAIRS), c("pv_done", PAIRS)
        inv_done, o_done, oT_ps, oT_sb = c("inv_done"), c("o_done"), c("oT_ps"), c("oT_sb")
        y_ps, y_done = c("y_ps"), c("y_done")

        with nc.Block() as block:

            @block.sync
            def _(sp):
                sp.dma_start(ident[:, :], ident_dram).then_inc(const_in, DMA)
                sp.dma_start(mask[:, :, :, :], mask_dram).then_inc(const_in, DMA)
                for n in range(4):
                    sp.dma_start(scales[:, n, :], qk_scale[n:n + 1, :].to_broadcast([P, HEAD_DIM])).then_inc(const_in, DMA)

                def load(t, u):
                    sp.dma_start(x[u][:, :], x_in[bass.ds(t * P + 1, P), :]).then_inc(x_loaded[u], DMA)
                    sp.dma_start(x_shift[u][:, :], x_in[bass.ds(t * P, P), P:DIM]).then_inc(x_loaded[u], DMA)
                    sp.dma_start(rot[u][:, :, :], rotary[bass.ds(t * P, P), :, :]).then_inc(x_loaded[u], DMA)

                def load_res(t, u):
                    sp.dma_start(x_res[u][:, :], x_in[bass.ds(t * P + 1, P), :]).then_inc(res_loaded[u], DMA)

                for u in (0, 1):
                    sp.sem_inc(y_stored[u], DMA)
                    load(u, u)
                sp.dma_start(w_qkv[:, :, :], wqkv.rearrange("(k p) n -> p k n", p=P)).then_inc(weights_in, DMA)
                sp.dma_start(w_o[:, :, :], wo.rearrange("(k p) n -> p k n", p=P)).then_inc(weights_in, DMA)
                for u in (0, 1):
                    load_res(u, u)

                def store(t, u):
                    wait(sp, y_done, t)
                    sp.dma_start(x_out[bass.ds(t * P + 1, P), :], y[u][:, :]).then_inc(y_stored[u], DMA)

                with sp.Fori(0, TILES // 2 - 1) as i:
                    for u in (0, 1):
                        wait(sp, hT_ps, i * 2 + u)
                        wait(sp, rot_ready, i * 2 + u)
                        load(i * 2 + u + 2, u)
                        store(i * 2 + u, u)
                        load_res(i * 2 + u + 2, u)
                for u in (0, 1):
                    store(TILES - 2 + u, u)
                for u in (0, 1):
                    sp.wait_ge(y_stored[u], DMA * (TILES // 2 + 1))

            @block.gpsimd
            def _(pool):
                for q in (rot_ready, norm_inv):
                    q.prime(pool)
                pool.memset(minus_half[:, :], -0.5).then_inc(consts_set, 1)
                pool.memset(kT[:, :, :, :, :], 0.0).then_inc(consts_set, 1)
                pool.memset(v[:, :, :], 0.0).then_inc(consts_set, 1)
                pool.wait_ge(consts_set, 3)
                pool.wait_ge(const_in, 6 * DMA)
                with pool.Fori(0, TILES // 2) as i:
                    for u in (0, 1):
                        t = i * 2 + u
                        pool.wait_ge(x_loaded[u], (i + 1) * 3 * DMA)
                        wait(pool, sin_done, t - 2)
                        pool.tensor_tensor(rot_s[u][:, :, :], rot[u][:, :, :], scales[:, :, :], ALU.mult)\
                            .then_inc(rot_ready.sem, 1)
                        wait(pool, norm_floor, t)
                        wait(pool, k_done, t - 1)
                        pool.tensor_tensor(inv_norm[:, :, :], norm2[:, :, :],
                                           minus_half[:, :].rearrange("p (a h) -> p a h", a=2), ALU.pow)\
                            .then_inc(norm_inv.sem, 1)

            @block.scalar
            def _(act):
                for q in (hT_sb, v_sb, squared, qT_sb, exp_done, pT_sb, oT_sb):
                    q.prime(act)

                def turned_h(t):
                    wait(act, hT_ps, t)
                    wait(act, v_ps, t - 1)
                    act.copy(hT[:, :, :], ps_T[:, 1, 0:KT, :]).then_inc(hT_sb.sem, 1)

                def square(t):
                    wait(act, qk_ps, t)
                    wait(act, normed2, t - 1)
                    act.activation(squares[:, :, :], ps_qk[:, :, :], ACT.Square).then_inc(squared.sem, 1)

                def turned_q(t):
                    wait(act, qT_ps, t)
                    wait(act, s_ps, t - 1)
                    act.copy(qT[:, :, :], ps_T[:, 1, :, :]).then_inc(qT_sb.sem, 1)

                def turned_o(t):
                    wait(act, oT_ps, t)
                    wait(act, y_ps, t - 1)
                    act.copy(oT[:, :, :], ps_T[:, 0, :, :]).then_inc(oT_sb.sem, 1)

                def keep_v(t, u):
                    wait(act, v_ps, t)
                    wait(act, pv_done, t - 1)
                    act.copy(v[:, u, :], ps_v[:, :]).then_inc(v_sb.sem, 1)

                def exps(t, u, p):
                    wait(act, bias_done, t, p + 1)
                    if p < 2:
                        wait(act, pT_ps, t - 1, p + 3)
                    else:
                        wait(act, pT_ps, t, p - 1)
                    for j in (0, 1):
                        h = 2 * p + j
                        act.activation(probs[:, p % 2, j, :], masked[:, p % 2, j, :], ACT.Exp,
                                       bias=bias[:, p, j:j + 1], scale=q_gain[u][:, h:h + 1],
                                       accum_out=total[:, h:h + 1]).then_inc(exp_done.sem, 1)

                def pT_copy(t, p):
                    wait(act, pT_ps, t, p + 1)
                    if p < 2:
                        wait(act, pv_done, t - 1, p + 3)
                    else:
                        wait(act, pv_done, t, p - 1)
                    act.copy(pT[:, p % 2, :, :], ps_T[:, int(p == 1), :, :]).then_inc(pT_sb.sem, 1)

                act.wait_ge(consts_set, 3)
                turned_h(0)
                square(0)
                turned_q(0)
                keep_v(0, 0)

                def tile(t, u, i, more):
                    if not first(t):
                        turned_o(t - 1)
                    wait(act, inv_done, t - 1)
                    exps(t, u, 0)
                    if more:
                        turned_h(t + 1)
                    exps(t, u, 1)
                    if more:
                        square(t + 1)
                    pT_copy(t, 0)
                    exps(t, u, 2)
                    pT_copy(t, 1)
                    exps(t, u, 3)
                    pT_copy(t, 2)
                    if more:
                        turned_q(t + 1)
                    pT_copy(t, 3)
                    if more:
                        keep_v(t + 1, 1 - u)

                tile_pairs(act, TILES // 2, tile)
                turned_o(TILES - 1)

            @block.vector
            def _(dve):
                for q in (normed2, norm_floor, gain, cos_done, sin_done, turned_done, k_done, kT_sb, s_masked, bias_done,
                          inv_done, o_done, y_done):
                    q.prime(dve)
                dve.wait_ge(const_in, 6 * DMA)
                dve.wait_ge(consts_set, 3)

                def rotate(t, u):
                    wait(dve, squared, t)
                    wait(dve, norm_inv, t - 1)
                    dve.reduce_sum(norm2[:, :, :].rearrange("p a h -> p (a h)"),
                                   squares[:, :, :].rearrange("p a (h d) -> p (a h) d", h=HEADS), axis=AX_X)\
                        .then_inc(normed2.sem, 1)
                    wait(dve, normed2, t)
                    dve.tensor_scalar(norm2[:, :, :], norm2[:, :, :], 1e-24, None, ALU.max).then_inc(norm_floor.sem, 1)
                    wait(dve, qk_ps, t)
                    wait(dve, rot_ready, t)
                    wait(dve, turned_done, t - 1)
                    q4 = ps_qk[:, :, :].rearrange("p a (h d) -> p a h d", h=HEADS)
                    H2 = HEAD_DIM // 2
                    tab = rot_s[u][:, :, :].rearrange("p (a b) d -> p a b d", a=2)
                    dve.tensor_tensor(by_cos[:, :, :, :], q4,
                                      tab[:, :, 0:1, :].to_broadcast([P, 2, HEADS, HEAD_DIM]), ALU.mult)\
                        .then_inc(cos_done.sem, 1)
                    for a, b in ((0, H2), (H2, 0)):
                        dve.tensor_tensor(by_sin[:, :, :, a:a + H2], q4[:, :, :, b:b + H2],
                                          tab[:, :, 1:2, a:a + H2].to_broadcast([P, 2, HEADS, H2]), ALU.mult)\
                            .then_inc(sin_done.sem, 1)
                    wait(dve, cos_done, t)
                    wait(dve, sin_done, t)
                    wait(dve, qT_ps, t - 1)
                    wait(dve, k_done, t - 1)
                    dve.tensor_tensor(turned[:, :, :, :], by_cos[:, :, :, :], by_sin[:, :, :, :], ALU.add)\
                        .then_inc(turned_done.sem, 1)

                def normalise_k(t, u):
                    wait(dve, norm_inv, t)
                    dve.tensor_scalar(q_gain[u][:, :], inv_norm[:, 0, :], 8.0, None, ALU.mult).then_inc(gain.sem, 1)
                    wait(dve, turned_done, t)
                    wait(dve, kT_ps, t - 1)
                    dve.tensor_tensor(k_turned[:, :, :], turned[:, 1, :, :],
                                      inv_norm[:, 1, :].unsqueeze(2).to_broadcast([P, HEADS, HEAD_DIM]), ALU.mult)\
                        .then_inc(k_done.sem, 1)

                def turned_k(t, u):
                    wait(dve, kT_ps, t)
                    wait(dve, s_ps, t - 1)
                    for j in (0, 1):
                        half = slice(j * HEAD_DIM, (j + 1) * HEAD_DIM)
                        dve.tensor_copy(kT[half, :, j, u, :], ps_T[half, 1, :, :]).then_inc(kT_sb.sem, 1)

                def mask_pair(t, u, i, p, which):
                    wait(dve, s_ps, t, p + 1)
                    if p < 2:
                        wait(dve, exp_done, t - 1, 2 * p + 6)
                    else:
                        wait(dve, exp_done, t, 2 * p - 2)
                    dve.memset(spare[:, :], 0.0)
                    for j in (0, 1):
                        dve.tensor_tensor_reduce(out=masked[:, p % 2, j, :], in0=ps_s[:, p % 2, j, :],
                                                 in1=mask[:, which, :, :].rearrange("p a k -> p (a k)"),
                                                 scale=1.0, scalar=-3e38, op0=ALU.add, op1=ALU.max,
                                                 accum_out=top[:, p, j:j + 1]).then_inc(s_masked.sem, 1)
                    wait(dve, s_masked, t, 2 * p + 2)
                    wait(dve, gain, t)
                    dve.scalar_tensor_tensor(out=bias[:, p, :], in0=top[:, p, :], scalar=-1.0,
                                             in1=q_gain[u][:, 2 * p:2 * p + 2], op0=ALU.mult, op1=ALU.mult)\
                        .then_inc(bias_done.sem, 1)

                def add_residual(t, u, pair):
                    wait(dve, y_ps, t)
                    dve.wait_ge(y_stored[u], (pair + 1) * DMA)
                    dve.wait_ge(res_loaded[u], (pair + 1) * DMA)
                    dve.tensor_tensor(y[u][:, :], ps_v[:, 0:DIM], x_res[u][:, :], ALU.add).then_inc(y_done.sem, 1)

                rotate(0, 0)
                normalise_k(0, 0)
                turned_k(0, 0)

                def tile(t, u, i, more):
                    which = 2 if first(t) else u
                    mask_pair(t, u, i, 0, which)
                    mask_pair(t, u, i, 1, which)
                    if not first(t):
                        add_residual(t - 1, 1 - u, i + u - 1)
                    mask_pair(t, u, i, 2, which)
                    if more:
                        rotate(t + 1, 1 - u)
                    mask_pair(t, u, i, 3, which)
                    if more:
                        normalise_k(t + 1, 1 - u)
                    wait(dve, exp_done, t)
                    dve.reciprocal(inv_total[:, :], total[:, :]).then_inc(inv_done.sem, 1)
                    if more:
                        turned_k(t + 1, 1 - u)
                    wait(dve, inv_done, t)
                    wait(dve, pv_done, t)
                    wait(dve, oT_ps, t - 1)
                    dve.tensor_tensor(o[:, :].rearrange("p (h d) -> p h d", h=HEADS),
                                      ps_o[:, :].rearrange("p (h d) -> p h d", h=HEADS),
                                      inv_total[:, :].unsqueeze(2).to_broadcast([P, HEADS, HEAD_DIM]), ALU.mult)\
                        .then_inc(o_done.sem, 1)

                tile_pairs(dve, TILES // 2, tile)
                add_residual(TILES - 1, 1, TILES // 2 - 1)

            @block.tensor
            def _(pe):
                for q in (hT_ps, qk_ps, v_ps, qT_ps, kT_ps, s_ps, pT_ps, pv_done, oT_ps, y_ps):
                    q.prime(pe)
                pe.wait_ge(const_in, 6 * DMA)

                def turn_x(t, u, i):
                    pe.wait_ge(x_loaded[u], (i + 1) * 3 * DMA)
                    wait(pe, kT_sb, t - 1)
                    pe.transpose(ps_T[:, 1, 0, :], x[u][:, 0:P], ident[:, :])
                    pe.transpose(ps_T[:, 1, 1, :], x_shift[u][:, :], ident[:, :]).then_inc(hT_ps.sem, 1)

                def project_qk(t):
                    wait(pe, hT_sb, t)
                    wait(pe, squared, t - 1)
                    wait(pe, sin_done, t - 1)
                    for a in (0, 1):
                        for k in range(KT):
                            mm = pe.matmul(ps_qk[:, a, :], hT[:, k, :], w_qkv[:, k, a * INNER:(a + 1) * INNER],
                                           start=(k == 0), stop=(k == KT - 1))
                    mm.then_inc(qk_ps.sem, 1)

                def project_v(t):
                    wait(pe, y_done, t - 2)
                    for k in range(KT):
                        mm = pe.matmul(ps_v[:, :], hT[:, k, :], w_qkv[:, k, 2 * INNER:3 * INNER],
                                       start=(k == 0), stop=(k == KT - 1))
                    mm.then_inc(v_ps.sem, 1)

                def turn_q(t):
                    wait(pe, turned_done, t)
                    if not first(t):
                        wait(pe, pT_sb, t - 1, 2)
                    else:
                        wait(pe, hT_sb, t)
                    for n in range(PAIRS):
                        mm = pe.transpose(ps_T[:, 1, n, :],
                                          turned[:, 0, 2 * n:2 * n + 2, :].rearrange("p h d -> p (h d)"), ident[:, :])
                    mm.then_inc(qT_ps.sem, 1)

                def turn_k(t):
                    wait(pe, k_done, t)
                    wait(pe, qT_sb, t)
                    for n in range(PAIRS):
                        mm = pe.transpose(ps_T[:, 1, n, :],
                                          k_turned[:, 2 * n:2 * n + 2, :].rearrange("p h d -> p (h d)"), ident[:, :])
                    mm.then_inc(kT_ps.sem, 1)

                def turn_o(t):
                    wait(pe, o_done, t)
                    wait(pe, pT_sb, t)
                    for n in range(INNER // P):
                        mm = pe.transpose(ps_T[:, 0, n, :], o[:, n * P:(n + 1) * P], ident[:, :])
                    mm.then_inc(oT_ps.sem, 1)

                def project_out(t):
                    wait(pe, oT_sb, t)
                    if not last(t):
                        wait(pe, v_sb, t + 1)
                    for n in range(INNER // P):
                        mm = pe.matmul(ps_v[:, 0:DIM], oT[:, n, :], w_o[:, n, :],
                                       start=(n == 0), stop=(n == INNER // P - 1))
                    mm.then_inc(y_ps.sem, 1)

                def scores(t, p):
                    if p < 2:
                        wait(pe, s_masked, t - 1, 2 * p + 6)
                    else:
                        wait(pe, s_masked, t, 2 * p - 2)
                    pe.matmul(ps_s[:, p % 2, :, :].rearrange("q j k -> q (j k)"), qT[:, p, :],
                              kT[:, p, :, :, :].rearrange("d j a k -> d (j a k)"), start=True, stop=True)\
                        .then_inc(s_ps.sem, 1)

                def pT_pair(t, p, more):
                    wait(pe, exp_done, t, 2 * p + 2)
                    if p == 0:
                        wait(pe, oT_sb, t - 1)
                    elif p == 1:
                        if more:
                            wait(pe, hT_sb, t + 1)
                        else:
                            wait(pe, kT_sb, t)
                    else:
                        wait(pe, pT_sb, t, (1, 3)[p - 2])
                    for n in range(4):
                        mm = pe.transpose(ps_T[:, int(p == 1), n, :], probs[:, p % 2, n // 2, (n % 2) * P:(n % 2 + 1) * P],
                                          ident[:, :])
                    mm.then_inc(pT_ps.sem, 1)

                def values(t, p):
                    wait(pe, pT_sb, t, p + 1)
                    if p == 0:
                        wait(pe, v_sb, t)
                        wait(pe, o_done, t - 1)
                    for j in (0, 1):
                        h = 2 * p + j
                        cols = slice(h * HEAD_DIM, (h + 1) * HEAD_DIM)
                        for a in (0, 1):
                            mm = pe.matmul(ps_o[:, cols], pT[:, p % 2, 2 * j + a, :], v[:, a, cols],
                                           start=(a == 0), stop=(a == 1))
                    mm.then_inc(pv_done.sem, 1)

                pe.wait_ge(consts_set, 3)
                turn_x(0, 0, 0)
                pe.wait_ge(weights_in, 2 * DMA)
                project_qk(0)
                project_v(0)
                turn_q(0)
                turn_k(0)

                def tile(t, u, i, more):
                    wait(pe, qT_sb, t)
                    wait(pe, kT_sb, t)
                    scores(t, 0)
                    scores(t, 1)
                    if not first(t):
                        turn_o(t - 1)
                    if more:
                        turn_x(t + 1, 1 - u, i + u)
                    scores(t, 2)
                    if not first(t):
                        project_out(t - 1)
                    if more:
                        project_qk(t + 1)
                    pT_pair(t, 0, more)
                    scores(t, 3)
                    pT_pair(t, 1, more)
                    values(t, 0)
                    if more:
                        project_v(t + 1)
                    pT_pair(t, 2, more)
                    values(t, 1)
                    if more:
                        turn_q(t + 1)
                    pT_pair(t, 3, more)
                    values(t, 2)
                    if more:
                        turn_k(t + 1)
                    values(t, 3)

                tile_pairs(pe, TILES // 2, tile)
                turn_o(TILES - 1)
                project_out(TILES - 1)
HIDDEN = DIM * 4 * 2 // 3
HT = -(-HIDDEN // P)
GROUP = 4
GT = GROUP * P
GROUPS = TOKENS // GT
PSUM_F32 = 512


def gated_ffn(nc, layer, x_in, x_out, w1, b1, w2, b2, ln_gain, ln_bias, ident_dram, x_block=None):
    final = x_block is not None
    loads = 3 if final else 2
    with ExitStack() as stack:
        s = Scope(nc, stack, f"ffn{layer}")
        w_up = s.sbuf("w_up", [P, KT, 2 * HIDDEN])
        w_down = s.sbuf("w_down", [P, HT, DIM])
        ident = s.sbuf("ident", [P, P])
        bias_up = s.sbuf("bias_up", [P, 2, HT])
        bias_down = s.sbuf("bias_down", [P, DIM])
        gain = s.sbuf("gain", [P, KT])
        offset = s.sbuf("offset", [P, KT])
        minus_half = s.sbuf("minus_half", [P, GROUP])
        x = [s.sbuf(f"x{u}", [P, GROUP, DIM]) for u in (0, 1)]
        x_shift = [s.sbuf(f"x_shift{u}", [P, GROUP, P]) for u in (0, 1)]
        x_outer = [s.sbuf(f"x_outer{u}", [P, GROUP, DIM]) for u in (0, 1)] if final else None
        spare = s.sbuf("spare", [P, 2])
        stats = s.sbuf("stats", [P, GROUP, 2, 6])
        mean_var = s.sbuf("mean_var", [P, GROUP, 2])
        var_eps = s.sbuf("var_eps", [P, GROUP])
        rstd = s.sbuf("rstd", [P, GROUP])
        normed = s.sbuf("normed", [P, GROUP, DIM])
        hT = s.sbuf("hT", [P, KT, GT])
        act_g = s.sbuf("act_g", [P, 2, GT])
        hidden = s.sbuf("hidden", [P, HT, GT])
        y = [s.sbuf(f"y{u}", [P, GROUP, DIM]) for u in (0, 1)]
        y_stats = s.sbuf("y_stats", [P, GROUP, 6])
        y_mean_var = s.sbuf("y_mean_var", [P, GROUP, 2])
        y_var_eps = s.sbuf("y_var_eps", [P, GROUP])
        y_rstd = s.sbuf("y_rstd", [P, GROUP])

        ps_T = s.psum("ps_T", [P, KT, GT])
        ps_a = s.psum("ps_a", [P, 2, GT])
        ps_g = s.psum("ps_g", [P, 2, GT])
        ps_y = s.psum("ps_y", [P, 2, PSUM_F32])

        weights_in = s.sem("weights_in")
        const_in = s.sem("const_in")
        consts_set = s.sem("consts_set")
        x_loaded = [s.sem(f"x_loaded{u}") for u in (0, 1)]
        y_stored = [s.sem(f"y_stored{u}") for u in (0, 1)]
        c = lambda name, n=1: s.count(name, n)
        stats_done, mean_done, eps_done, rstd_done = c("stats_done", 2 * GROUP), c("mean_done", GROUP), c("eps_done"), c("rstd_done")
        normed_done, hT_ps, hT_sb = c("normed_done", 2 * GROUP), c("hT_ps"), c("hT_sb", KT)
        up_ps, gelu_done, hidden_done = c("up_ps", HT), c("gelu_done", HT), c("hidden_done", HT)
        down_ps, y_done, x_biased = c("down_ps", 2), c("y_done", 2), c("x_biased", 2 if final else 1)
        y_stats_done, y_mean_done, y_eps_done = c("y_stats_done", GROUP), c("y_mean_done", GROUP), c("y_eps_done")
        y_rstd_done, y_normed = c("y_rstd_done"), c("y_normed", GROUP)

        def rows(f):
            return min(P, HIDDEN - f * P)

        with nc.Block() as block:

            @block.sync
            def _(sp):
                def load(g, u):
                    sp.dma_start(x[u][:, :, :], x_in[bass.ds(g * GT + 1, GT), :].rearrange("(n p) d -> p n d", p=P))\
                        .then_inc(x_loaded[u], DMA)
                    sp.dma_start(x_shift[u][:, :, :],
                                 x_in[bass.ds(g * GT, GT), P:DIM].rearrange("(n p) d -> p n d", p=P))\
                        .then_inc(x_loaded[u], DMA)
                    if final:
                        sp.dma_start(x_outer[u][:, :, :], x_block[bass.ds(g * GT + 1, GT), :].rearrange("(n p) d -> p n d", p=P))\
                            .then_inc(x_loaded[u], DMA)

                for u in (0, 1):
                    sp.sem_inc(y_stored[u], DMA)
                    load(u, u)
                sp.dma_start(ident[:, :], ident_dram).then_inc(const_in, DMA)
                sp.dma_start(gain[:, :], ln_gain).then_inc(const_in, DMA)
                sp.dma_start(offset[:, :], ln_bias).then_inc(const_in, DMA)
                sp.dma_start(bias_up[:, :, :], b1).then_inc(const_in, DMA)
                whole = (HT - 1) * P
                sp.dma_start(bias_down[:, :], b2.rearrange("(o d) -> o d", o=1).to_broadcast([P, DIM])).then_inc(const_in, DMA)
                sp.dma_start(w_up[:, :, :], w1.rearrange("(k p) n -> p k n", p=P)).then_inc(weights_in, DMA)
                sp.dma_start(w_down[:, 0:HT - 1, :], w2[0:whole, :].rearrange("(f p) d -> p f d", p=P)).then_inc(weights_in, DMA)
                sp.dma_start(w_down[0:rows(HT - 1), HT - 1, :], w2[whole:HIDDEN, :]).then_inc(weights_in, DMA)

                def store(g, u):
                    if final:
                        wait(sp, y_normed, g)
                        out = x_out[bass.ds(g * GT, GT), :]
                    else:
                        wait(sp, y_done, g)
                        out = x_out[bass.ds(g * GT + 1, GT), :]
                    sp.dma_start(out.rearrange("(n p) d -> p n d", p=P), y[u][:, :, :]).then_inc(y_stored[u], DMA)

                with sp.Fori(0, GROUPS // 2 - 1) as i:
                    for u in (0, 1):
                        store(i * 2 + u, u)
                        load(i * 2 + u + 2, u)
                for u in (0, 1):
                    store(GROUPS - 2 + u, u)
                for u in (0, 1):
                    sp.wait_ge(y_stored[u], DMA * (GROUPS // 2 + 1))

            @block.gpsimd
            def _(pool):
                for q in (rstd_done, x_biased) + ((y_rstd_done,) if final else ()):
                    q.prime(pool)
                pool.memset(minus_half[:, :], -0.5).then_inc(consts_set, 1)
                pool.wait_ge(consts_set, 1)
                pool.wait_ge(const_in, 5 * DMA)

                def whole_block_rstd(g):
                    wait(pool, y_eps_done, g)
                    wait(pool, y_normed, g - 1)
                    pool.tensor_tensor(y_rstd[:, :], y_var_eps[:, :], minus_half[:, :], ALU.pow)\
                        .then_inc(y_rstd_done.sem, 1)

                def group_rstd(g):
                    wait(pool, eps_done, g)
                    wait(pool, normed_done, g - 1)
                    pool.tensor_tensor(rstd[:, :], var_eps[:, :], minus_half[:, :], ALU.pow)\
                        .then_inc(rstd_done.sem, 1)

                group_rstd(0)

                def group(g, u, i, more):
                    wait(pool, normed_done, g)
                    pool.tensor_tensor(x[u][:, :, :], x[u][:, :, :],
                                       bias_down[:, :].unsqueeze(1).to_broadcast([P, GROUP, DIM]), ALU.add)\
                        .then_inc(x_biased.sem, 1)
                    if final:
                        wait(pool, x_biased, g, 1)
                        pool.tensor_tensor(x[u][:, :, :], x[u][:, :, :], x_outer[u][:, :, :], ALU.add)\
                            .then_inc(x_biased.sem, 1)
                    if more:
                        group_rstd(g + 1)
                    if final:
                        whole_block_rstd(g)

                tile_pairs(pool, GROUPS // 2, group)

            @block.scalar
            def _(act):
                for q in (hT_sb, gelu_done):
                    q.prime(act)
                act.wait_ge(const_in, 5 * DMA)

                def norm_affine(g):
                    wait(act, hT_ps, g)
                    wait(act, up_ps, g - 1)
                    for k in range(KT):
                        act.activation(hT[:, k, :], ps_T[:, k, :], ACT.Identity,
                                       bias=offset[:, k:k + 1], scale=gain[:, k:k + 1]).then_inc(hT_sb.sem, 1)

                norm_affine(0)

                def group(g, u, i, more):
                    for f in range(HT):
                        n = rows(f)
                        wait(act, up_ps, g, f + 1)
                        if f < 2:
                            wait(act, hidden_done, g - 1, f + HT - 1)
                        else:
                            wait(act, hidden_done, g, f - 1)
                        act.activation(act_g[0:n, f % 2, :], ps_g[0:n, f % 2, :], ACT.Gelu,
                                       bias=bias_up[0:n, 1, f:f + 1]).then_inc(gelu_done.sem, 1)
                    if more:
                        norm_affine(g + 1)

                tile_pairs(act, GROUPS // 2, group)

            @block.vector
            def _(dve):
                for q in (stats_done, mean_done, eps_done, normed_done, hidden_done, y_done) + \
                        ((y_stats_done, y_mean_done, y_eps_done, y_normed) if final else ()):
                    q.prime(dve)

                def statistics(g, u, i):
                    dve.wait_ge(x_loaded[u], (i + 1) * loads * DMA)
                    wait(dve, mean_done, g - 1)
                    for n in range(GROUP):
                        dve.bn_stats(stats[:, n, 0, :], x[u][:, n, 0:P]).then_inc(stats_done.sem, 1)
                        dve.bn_stats(stats[:, n, 1, :], x_shift[u][:, n, :]).then_inc(stats_done.sem, 1)
                    wait(dve, stats_done, g)
                    wait(dve, normed_done, g - 1)
                    dve.memset(spare[:, :], 0.0)
                    for n in range(GROUP):
                        dve.bn_aggr(mean_var[:, n, :], stats[:, n, :, :].rearrange("p a b -> p (a b)"))\
                            .then_inc(mean_done.sem, 1)
                    wait(dve, mean_done, g)
                    wait(dve, rstd_done, g - 1)
                    dve.tensor_scalar(var_eps[:, :], mean_var[:, :, 1], EPS, None, ALU.add).then_inc(eps_done.sem, 1)

                def normalise(g, u):
                    wait(dve, rstd_done, g)
                    wait(dve, hT_ps, g - 1)
                    for n in range(GROUP):
                        for k, src in ((0, x[u][:, n, 0:P]), (1, x_shift[u][:, n, :])):
                            dve.tensor_scalar(normed[:, n, k * P:(k + 1) * P], src, mean_var[:, n, 0:1], rstd[:, n:n + 1],
                                              ALU.subtract, ALU.mult).then_inc(normed_done.sem, 1)

                statistics(0, 0, 0)
                normalise(0, 0)

                def group(g, u, i, more):
                    if more:
                        statistics(g + 1, 1 - u, i + u)
                    for f in range(HT):
                        n = rows(f)
                        wait(dve, gelu_done, g, f + 1)
                        wait(dve, down_ps, g - 1)
                        dve.scalar_tensor_tensor(out=hidden[0:n, f, :], in0=ps_a[0:n, f % 2, :],
                                                 scalar=bias_up[0:n, 0, f:f + 1], in1=act_g[0:n, f % 2, :],
                                                 op0=ALU.add, op1=ALU.mult).then_inc(hidden_done.sem, 1)
                    if more:
                        normalise(g + 1, 1 - u)
                    wait(dve, x_biased, g)
                    dve.wait_ge(y_stored[u], (i + 1) * DMA)
                    for b in (0, 1):
                        wait(dve, down_ps, g, b + 1)
                        dve.tensor_tensor(y[u][:, 2 * b:2 * b + 2, :],
                                          ps_y[:, b, :].rearrange("p (n d) -> p n d", n=2),
                                          x[u][:, 2 * b:2 * b + 2, :], ALU.add).then_inc(y_done.sem, 1)
                    if final:
                        wait(dve, y_done, g)
                        wait(dve, y_mean_done, g - 1)
                        for n in range(GROUP):
                            dve.bn_stats(y_stats[:, n, :], y[u][:, n, :]).then_inc(y_stats_done.sem, 1)
                        wait(dve, y_stats_done, g)
                        wait(dve, y_normed, g - 1)
                        dve.memset(spare[:, :], 0.0)
                        for n in range(GROUP):
                            dve.bn_aggr(y_mean_var[:, n, :], y_stats[:, n, :]).then_inc(y_mean_done.sem, 1)
                        wait(dve, y_mean_done, g)
                        wait(dve, y_rstd_done, g - 1)
                        dve.tensor_scalar(y_var_eps[:, :], y_mean_var[:, :, 1], EPS, None, ALU.add)\
                            .then_inc(y_eps_done.sem, 1)
                        wait(dve, y_rstd_done, g)
                        for n in range(GROUP):
                            dve.tensor_scalar(y[u][:, n, :], y[u][:, n, :], y_mean_var[:, n, 0:1], y_rstd[:, n:n + 1],
                                              ALU.subtract, ALU.mult).then_inc(y_normed.sem, 1)

                tile_pairs(dve, GROUPS // 2, group)

            @block.tensor
            def _(pe):
                for q in (hT_ps, up_ps, down_ps):
                    q.prime(pe)
                pe.wait_ge(const_in, 5 * DMA)

                def transposed(g):
                    wait(pe, normed_done, g)
                    wait(pe, hT_sb, g - 1)
                    for k in range(KT):
                        for n in range(GROUP):
                            mm = pe.transpose(ps_T[:, k, n * P:(n + 1) * P], normed[:, n, k * P:(k + 1) * P], ident[:, :])
                    mm.then_inc(hT_ps.sem, 1)

                transposed(0)
                pe.wait_ge(weights_in, 3 * DMA)

                def group(g, u, i, more):
                    wait(pe, hT_sb, g)
                    for f in range(HT):
                        n = rows(f)
                        if f < 2:
                            wait(pe, hidden_done, g - 1, f + HT - 1)
                        else:
                            wait(pe, hidden_done, g, f - 1)
                        for a, bank in ((1, ps_g), (0, ps_a)):
                            for k in range(KT):
                                mm = pe.matmul(bank[0:n, f % 2, :], w_up[:, k, a * HIDDEN + f * P:a * HIDDEN + f * P + n],
                                               hT[:, k, :], start=(k == 0), stop=(k == KT - 1))
                        mm.then_inc(up_ps.sem, 1)
                    if more:
                        transposed(g + 1)
                    for b in (0, 1):
                        wait(pe, y_done, g - 1, b + 1)
                        for n in (2 * b, 2 * b + 1):
                            for f in range(HT):
                                wait(pe, hidden_done, g, f + 1)
                                mm = pe.matmul(ps_y[:, b, (n % 2) * DIM:(n % 2 + 1) * DIM],
                                               hidden[0:rows(f), f, n * P:(n + 1) * P], w_down[0:rows(f), f, :],
                                               start=(f == 0), stop=(f == HT - 1))
                        mm.then_inc(down_ps.sem, 1)

                tile_pairs(pe, GROUPS // 2, group)
C_HEADS = 16
C_DIM = 16
CHUNK = 64
CH = P // CHUNK
HH = P // C_DIM
C_SCALE = C_DIM ** -0.5


def chunk_attention(nc, x_in, x_out, w_qkv_dram, w_out_dram, ident_dram, causal_dram, head_mask_dram, cum_dram,
                    pair_dram):
    with ExitStack() as stack:
        s = Scope(nc, stack, "chunk")
        w_qkv = s.sbuf("w_qkv", [P, KT, 3 * DIM])
        w_out = s.sbuf("w_out", [P, KT, DIM])
        ident = s.sbuf("ident", [P, P])
        causal = s.sbuf("causal", [P, CHUNK])
        head_mask = s.sbuf("head_mask", [P, 2, HH])
        cum_w = s.sbuf("cum_w", [P, 2, P])
        pair_mask = s.sbuf("pair_mask", [P, 2, C_DIM])
        zero = s.sbuf("zero", [P, KT])
        minus_half = s.sbuf("minus_half", [P, 1])
        x = [s.sbuf(f"x{u}", [P, DIM]) for u in (0, 1)]
        x_res = [s.sbuf(f"x_res{u}", [P, DIM]) for u in (0, 1)]
        xT = s.sbuf("xT", [P, KT, P])
        xT_twice = s.sbuf("xT_twice", [P, KT, CH, 2, CHUNK])
        qT = s.sbuf("qT", [P, KT, P])
        kx = s.sbuf("kx", [P, KT, CH, HH, CHUNK])
        k_sum = s.sbuf("k_sum", [P, KT, CH])
        k_cum = s.sbuf("k_cum", [P, CH + 1, KT])
        k_mean = s.sbuf("k_mean", [P, KT, CH, HH])
        v = [s.sbuf(f"v{u}", [P, CH, DIM]) for u in (0, 1)]
        v_pairs = [s.sbuf(f"v_pairs{u}", [P, CH, HH, 2, C_DIM]) for u in (0, 1)]
        v_sum = [s.sbuf(f"v_sum{u}", [P, DIM]) for u in (0, 1)]
        v_add = s.sbuf("v_add", [P, DIM])
        scores = s.sbuf("scores", [P, C_HEADS, CHUNK])
        top = s.sbuf("top", [P, C_HEADS])
        probs = s.sbuf("probs", [P, C_HEADS, CHUNK])
        total = s.sbuf("total", [P, C_HEADS])
        inv_total = s.sbuf("inv_total", [P, C_HEADS])
        cross_e = s.sbuf("cross_e", [P, C_HEADS])
        cross_d = s.sbuf("cross_d", [P, C_HEADS])
        cross = s.sbuf("cross", [P, C_HEADS])
        pT = s.sbuf("pT", [P, HH, P])
        o_local = s.sbuf("o_local", [P, DIM])
        o_cross = s.sbuf("o_cross", [P, DIM])
        o = s.sbuf("o", [P, DIM])
        oT = s.sbuf("oT", [P, KT, P])
        res = s.sbuf("res", [P, DIM])
        stats = s.sbuf("stats", [P, 6])
        mean_var = s.sbuf("mean_var", [P, 2])
        var_eps = s.sbuf("var_eps", [P, 1])
        rstd = s.sbuf("rstd", [P, 1])
        spare = s.sbuf("spare", [P, 2])
        y = [s.sbuf(f"y{u}", [P, DIM]) for u in (0, 1)]

        ps_T = s.psum("ps_T", [P, 2, 4, P])
        ps_f = s.psum("ps_f", [P, 4, P])
        ps_v = s.psum("ps_v", [P, CH, DIM])
        ps_s = s.psum("ps_s", [P, KT, HH, CHUNK])
        ps_c = s.psum("ps_c", [P, PSUM_F32])
        ps_o = s.psum("ps_o", [P, PSUM_F32])

        in_sem = s.sem("const_in")
        consts_set = s.sem("consts_set")
        x_loaded = [s.sem(f"x_loaded{u}") for u in (0, 1)]
        res_loaded = [s.sem(f"res_loaded{u}") for u in (0, 1)]
        y_stored = [s.sem(f"y_stored{u}") for u in (0, 1)]
        c = lambda name, n=1: s.count(name, n)
        xT_ps, xT_sb, qk_ps, qT_sb, v_ps, v_sb = c("xT_ps"), c("xT_sb", 2), c("qk_ps"), c("qT_sb"), c("v_ps"), c("v_sb")
        kx_done, ksum_done, kcum_done, kmean_done = c("kx_done", KT), c("ksum_done"), c("kcum_done", 3), c("kmean_done")
        pairs_done, vadd_done, vsum_done = c("pairs_done"), c("vadd_done"), c("vsum_done")
        s_ps, z_ps, added, max_done, shifted = c("s_ps"), c("z_ps"), c("added"), c("max_done"), c("shifted")
        exp_done, cross_exp, sum_done, inv_done = c("exp_done"), c("cross_exp"), c("sum_done"), c("inv_done")
        cross_plus, cross_done = c("cross_plus"), c("cross_done")
        pT_ps, pT_sb, pv_ps, cumv_ps = c("pT_ps", 2), c("pT_sb", 2), c("pv_ps"), c("cumv_ps")
        local_done, crossed, o_done, oT_ps, oT_sb = c("local_done"), c("crossed"), c("o_done"), c("oT_ps"), c("oT_sb")
        y_ps, res_done, stats_done, mean_done = c("y_ps"), c("res_done"), c("stats_done"), c("mean_done")
        eps_done, rstd_done, y_done = c("eps_done"), c("rstd_done"), c("y_done")

        with nc.Block() as block:

            @block.sync
            def _(sp):
                def load(t, u):
                    sp.dma_start(x[u][:, :], x_in[bass.ds(t * P + 1, P), :]).then_inc(x_loaded[u], DMA)

                def load_res(t, u):
                    sp.dma_start(x_res[u][:, :], x_in[bass.ds(t * P + 1, P), :]).then_inc(res_loaded[u], DMA)

                for u in (0, 1):
                    sp.sem_inc(y_stored[u], DMA)
                    load(u, u)
                for dst, src in ((ident[:, :], ident_dram), (causal[:, :], causal_dram),
                                 (head_mask[:, :, :], head_mask_dram), (cum_w[:, :, :], cum_dram), (pair_mask[:, :, :], pair_dram),
                                 (w_qkv[:, :, :], w_qkv_dram.rearrange("(k p) n -> p k n", p=P)),
                                 (w_out[:, :, :], w_out_dram.rearrange("(k p) n -> p k n", p=P))):
                    sp.dma_start(dst, src).then_inc(in_sem, DMA)

                for u in (0, 1):
                    load_res(u, u)

                def store(t, u):
                    wait(sp, y_done, t)
                    sp.dma_start(x_out[bass.ds(t * P + 1, P), :], y[u][:, :]).then_inc(y_stored[u], DMA)

                with sp.Fori(0, TILES // 2 - 1) as i:
                    for u in (0, 1):
                        wait(sp, xT_ps, i * 2 + u)
                        load(i * 2 + u + 2, u)
                        store(i * 2 + u, u)
                        load_res(i * 2 + u + 2, u)
                for u in (0, 1):
                    store(TILES - 2 + u, u)
                for u in (0, 1):
                    sp.wait_ge(y_stored[u], DMA * (TILES // 2 + 1))

            @block.gpsimd
            def _(pool):
                for q in (kcum_done, kmean_done, pairs_done, vadd_done, vsum_done, rstd_done):
                    q.prime(pool)
                pool.memset(minus_half[:, :], -0.5).then_inc(consts_set, 1)
                pool.memset(k_cum[:, :, :], 0.0).then_inc(consts_set, 1)
                pool.memset(zero[:, :], 0.0).then_inc(consts_set, 1)
                for u in (0, 1):
                    pool.memset(v_sum[u][:, :], 0.0).then_inc(consts_set, 1)
                pool.wait_ge(consts_set, 5)
                pool.wait_ge(in_sem, 7 * DMA)

                def running_k(t):
                    wait(pool, kmean_done, t - 1)
                    pool.tensor_tensor(k_cum[:, 0, :], k_cum[:, CH, :], zero[:, :], ALU.add).then_inc(kcum_done.sem, 1)
                    wait(pool, ksum_done, t)
                    wait(pool, kcum_done, t, 1)
                    for n in range(CH):
                        pool.tensor_tensor(k_cum[:, n + 1, :], k_cum[:, n, :], k_sum[:, :, n], ALU.add)\
                            .then_inc(kcum_done.sem, 1)
                        wait(pool, kcum_done, t, n + 2)
                    wait(pool, z_ps, t - 1)
                    pool.tensor_tensor(k_mean[:, :, :, :],
                                       k_cum[:, 0:CH, :].rearrange("p c k -> p k c").unsqueeze(3)
                                       .to_broadcast([P, KT, CH, HH]),
                                       head_mask[:, 1:2, :].unsqueeze(1).to_broadcast([P, KT, CH, HH]), ALU.mult)\
                        .then_inc(kmean_done.sem, 1)

                def running_v(t, u):
                    wait(pool, v_sb, t)
                    wait(pool, pv_ps, t - 2)
                    pool.tensor_tensor(v_pairs[u][:, :, :, :, :].rearrange("p c n j d -> p (c n) j d"),
                                       v[u][:, :, :].rearrange("p c (n j d) -> p (c n) j d", j=2, d=C_DIM),
                                       pair_mask[:, :, :].unsqueeze(1).to_broadcast([P, CH * HH, 2, C_DIM]), ALU.mult)\
                        .then_inc(pairs_done.sem, 1)
                    wait(pool, vsum_done, t - 1)
                    pool.tensor_tensor(v_add[:, :], v[u][:, 0, :], v[u][:, 1, :], ALU.add).then_inc(vadd_done.sem, 1)
                    wait(pool, vadd_done, t)
                    wait(pool, cumv_ps, t - 1)
                    pool.tensor_tensor(v_sum[1 - u][:, :], v_sum[u][:, :], v_add[:, :], ALU.add)\
                        .then_inc(vsum_done.sem, 1)

                running_k(0)
                running_v(0, 0)

                def row_factor(t):
                    wait(pool, eps_done, t)
                    wait(pool, y_done, t - 1)
                    pool.tensor_tensor(rstd[:, :], var_eps[:, :], minus_half[:, :], ALU.pow).then_inc(rstd_done.sem, 1)

                def tile(t, u, i, more):
                    if not first(t):
                        row_factor(t - 1)
                    if more:
                        running_k(t + 1)
                        running_v(t + 1, 1 - u)

                tile_pairs(pool, TILES // 2, tile)
                row_factor(TILES - 1)

            @block.scalar
            def _(act):
                for q in (xT_sb, qT_sb, v_sb, exp_done, cross_exp, pT_sb, oT_sb):
                    q.prime(act)

                def turned_x(t):
                    wait(act, xT_ps, t)
                    wait(act, v_ps, t - 1)
                    act.copy(xT[:, :, :], ps_T[:, 0, 0:KT, :]).then_inc(xT_sb.sem, 1)
                    for k in range(KT):
                        last_copy = act.copy(xT_twice[:, k, :, :, :],
                                             ps_T[:, 0, k, :].rearrange("p (c t) -> p c t", c=CH).unsqueeze(2)
                                             .to_broadcast([P, CH, 2, CHUNK]))
                    last_copy.then_inc(xT_sb.sem, 1)

                def keep_qv(t, u):
                    wait(act, qk_ps, t)
                    wait(act, z_ps, t - 1)
                    act.copy(qT[:, :, :], ps_f[:, 0:KT, :]).then_inc(qT_sb.sem, 1)
                    wait(act, v_ps, t)
                    wait(act, cumv_ps, t - 2)
                    wait(act, vadd_done, t - 2)
                    act.copy(v[u][:, :, :], ps_v[:, :, :]).then_inc(v_sb.sem, 1)

                def turned_o(t):
                    wait(act, oT_ps, t)
                    wait(act, y_ps, t - 1)
                    act.copy(oT[:, :, :], ps_T[:, 1, 0:KT, :]).then_inc(oT_sb.sem, 1)

                turned_x(0)
                keep_qv(0, 0)

                def tile(t, u, i, more):
                    wait(act, z_ps, t)
                    wait(act, cross_plus, t - 1)
                    act.activation(cross_e[:, :], ps_c[:, 0:C_HEADS], ACT.Exp, scale=-C_SCALE).then_inc(cross_exp.sem, 1)
                    if not first(t):
                        turned_o(t - 1)
                    if more:
                        turned_x(t + 1)
                    wait(act, shifted, t)
                    wait(act, pT_ps, t - 1)
                    wait(act, sum_done, t - 1)
                    act.activation(probs[:, :, :], scores[:, :, :], ACT.Exp, scale=C_SCALE).then_inc(exp_done.sem, 1)
                    if more:
                        keep_qv(t + 1, 1 - u)
                    for b in (0, 1):
                        wait(act, pT_ps, t, b + 1)
                        wait(act, pv_ps, t - 1)
                        act.copy(pT[:, 4 * b:4 * b + 4, :], ps_T[:, b, :, :]).then_inc(pT_sb.sem, 1)

                tile_pairs(act, TILES // 2, tile)
                turned_o(TILES - 1)

            @block.vector
            def _(dve):
                for q in (kx_done, ksum_done, added, max_done, shifted, sum_done, inv_done, cross_plus, cross_done,
                          local_done, crossed, o_done, res_done, stats_done, mean_done, eps_done, y_done):
                    q.prime(dve)
                dve.wait_ge(in_sem, 7 * DMA)

                def spread_k(t):
                    wait(dve, qT_sb, t)
                    wait(dve, s_ps, t - 1)
                    for n in range(KT):
                        dve.tensor_tensor(kx[:, n, :, :, :],
                                          ps_f[:, KT + n, :].rearrange("p (c k) -> p c k", c=CH).unsqueeze(2)
                                          .to_broadcast([P, CH, HH, CHUNK]),
                                          head_mask[:, 0:1, :].unsqueeze(3).to_broadcast([P, CH, HH, CHUNK]), ALU.mult)\
                            .then_inc(kx_done.sem, 1)
                    wait(dve, kcum_done, t - 1)
                    dve.reduce_sum(k_sum[:, :, :].rearrange("p k c -> p (k c)"),
                                   ps_f[:, KT:2 * KT, :].rearrange("p k (c t) -> p (k c) t", c=CH), axis=AX_X)\
                        .then_inc(ksum_done.sem, 1)

                def statistics(t, u, pair):
                    wait(dve, y_ps, t)
                    dve.wait_ge(res_loaded[u], (pair + 1) * DMA)
                    dve.tensor_tensor(res[:, :], ps_o[:, DIM:2 * DIM], x_res[u][:, :], ALU.add).then_inc(res_done.sem, 1)
                    wait(dve, res_done, t)
                    dve.bn_stats(stats[:, :], res[:, :]).then_inc(stats_done.sem, 1)
                    wait(dve, stats_done, t)
                    dve.memset(spare[:, :], 0.0)
                    dve.bn_aggr(mean_var[:, :], stats[:, :]).then_inc(mean_done.sem, 1)
                    wait(dve, mean_done, t)
                    dve.tensor_scalar(var_eps[:, :], mean_var[:, 1:2], EPS, None, ALU.add).then_inc(eps_done.sem, 1)

                def normalise(t, u, pair):
                    wait(dve, rstd_done, t)
                    dve.wait_ge(y_stored[u], (pair + 1) * DMA)
                    dve.tensor_scalar(y[u][:, :], res[:, :], mean_var[:, 0:1], rstd[:, :], ALU.subtract, ALU.mult)\
                        .then_inc(y_done.sem, 1)

                spread_k(0)

                def tile(t, u, i, more):
                    wait(dve, s_ps, t)
                    wait(dve, exp_done, t - 1)
                    dve.tensor_tensor(scores[:, :, :], ps_s[:, :, :, :].rearrange("p a h k -> p (a h) k"),
                                      causal[:, :].unsqueeze(1).to_broadcast([P, C_HEADS, CHUNK]), ALU.add)\
                        .then_inc(added.sem, 1)
                    wait(dve, added, t)
                    dve.reduce_max(top[:, :], scores[:, :, :], axis=AX_X).then_inc(max_done.sem, 1)
                    wait(dve, max_done, t)
                    dve.tensor_tensor(scores[:, :, :], scores[:, :, :],
                                      top[:, :].unsqueeze(2).to_broadcast([P, C_HEADS, CHUNK]), ALU.subtract)\
                        .then_inc(shifted.sem, 1)
                    if not first(t):
                        statistics(t - 1, 1 - u, i + u - 1)
                    if more:
                        spread_k(t + 1)
                    wait(dve, exp_done, t)
                    dve.reduce_sum(total[:, :], probs[:, :, :], axis=AX_X).then_inc(sum_done.sem, 1)
                    if not first(t):
                        normalise(t - 1, 1 - u, i + u - 1)
                    wait(dve, sum_done, t)
                    dve.reciprocal(inv_total[:, :], total[:, :]).then_inc(inv_done.sem, 1)
                    wait(dve, cross_exp, t)
                    dve.tensor_scalar(cross_d[:, :], cross_e[:, :], 1.0, None, ALU.add).then_inc(cross_plus.sem, 1)
                    wait(dve, cross_plus, t)
                    dve.reciprocal(cross[:, :], cross_d[:, :]).then_inc(cross_done.sem, 1)
                    heads = lambda a: a.rearrange("p (h d) -> p h d", h=C_HEADS)
                    wide = lambda a: a.unsqueeze(2).to_broadcast([P, C_HEADS, C_DIM])
                    wait(dve, inv_done, t)
                    wait(dve, pv_ps, t)
                    dve.tensor_tensor(heads(o_local[:, :]), heads(ps_o[:, 0:DIM]), wide(inv_total[:, :]), ALU.mult)\
                        .then_inc(local_done.sem, 1)
                    wait(dve, cross_done, t)
                    wait(dve, cumv_ps, t)
                    dve.tensor_tensor(heads(o_cross[:, :]), heads(ps_c[:, DIM:2 * DIM]), wide(cross[:, :]), ALU.mult)\
                        .then_inc(crossed.sem, 1)
                    wait(dve, local_done, t)
                    wait(dve, crossed, t)
                    wait(dve, oT_ps, t - 1)
                    dve.tensor_tensor(o[:, :], o_local[:, :], o_cross[:, :], ALU.add).then_inc(o_done.sem, 1)
                tile_pairs(dve, TILES // 2, tile)
                statistics(TILES - 1, 1, TILES // 2 - 1)
                normalise(TILES - 1, 1, TILES // 2 - 1)

            @block.tensor
            def _(pe):
                for q in (xT_ps, qk_ps, v_ps, s_ps, z_ps, pT_ps, pv_ps, cumv_ps, oT_ps, y_ps):
                    q.prime(pe)
                pe.wait_ge(in_sem, 7 * DMA)

                def turn_x(t, u, i):
                    pe.wait_ge(x_loaded[u], (i + 1) * DMA)
                    wait(pe, pT_sb, t - 2, 1)
                    for k in range(KT):
                        mm = pe.transpose(ps_T[:, 0, k, :], x[u][:, k * P:(k + 1) * P], ident[:, :])
                    mm.then_inc(xT_ps.sem, 1)

                def project(t):
                    wait(pe, xT_sb, t)
                    wait(pe, ksum_done, t - 1)
                    for n in range(4):
                        for k in range(KT):
                            mm = pe.matmul(ps_f[:, n, :], w_qkv[:, k, n * P:(n + 1) * P], xT[:, k, :],
                                           start=(k == 0), stop=(k == KT - 1))
                    mm.then_inc(qk_ps.sem, 1)
                    wait(pe, v_sb, t - 1)
                    for ch in range(CH):
                        for k in range(KT):
                            mm = pe.matmul(ps_v[:, ch, :], xT_twice[:, k, ch, :, :].rearrange("p a t -> p (a t)"),
                                           w_qkv[:, k, 2 * DIM:3 * DIM],
                                           start=(k == 0), stop=(k == KT - 1))
                    mm.then_inc(v_ps.sem, 1)

                def turn_o(t):
                    wait(pe, o_done, t)
                    for k in range(KT):
                        mm = pe.transpose(ps_T[:, 1, k, :], o[:, k * P:(k + 1) * P], ident[:, :])
                    mm.then_inc(oT_ps.sem, 1)

                def project_out(t):
                    wait(pe, oT_sb, t)
                    for k in range(KT):
                        mm = pe.matmul(ps_o[:, DIM:2 * DIM], oT[:, k, :], w_out[:, k, :],
                                       start=(k == 0), stop=(k == KT - 1))
                    mm.then_inc(y_ps.sem, 1)

                pe.wait_ge(consts_set, 5)
                turn_x(0, 0, 0)
                project(0)

                def tile(t, u, i, more):
                    wait(pe, kx_done, t)
                    wait(pe, added, t - 1)
                    for n in range(KT):
                        for ch in range(CH):
                            q = slice(ch * CHUNK, (ch + 1) * CHUNK)
                            mm = pe.matmul(ps_s[q, n, :, :].rearrange("p h k -> p (h k)"), qT[:, n, q],
                                           kx[:, n, ch, :, :].rearrange("p h k -> p (h k)"), start=True, stop=True)
                    mm.then_inc(s_ps.sem, 1)
                    wait(pe, kmean_done, t)
                    wait(pe, crossed, t - 1)
                    for n in range(KT):
                        for ch in range(CH):
                            q = slice(ch * CHUNK, (ch + 1) * CHUNK)
                            mm = pe.matmul(ps_c[q, n * HH:(n + 1) * HH], qT[:, n, q], k_mean[:, n, ch, :],
                                           start=True, stop=True)
                    mm.then_inc(z_ps.sem, 1)
                    if not first(t):
                        turn_o(t - 1)
                    if more:
                        turn_x(t + 1, 1 - u, i + u)
                    if not first(t):
                        project_out(t - 1)
                    if more:
                        project(t + 1)
                    wait(pe, exp_done, t)
                    wait(pe, oT_sb, t - 1)
                    if more:
                        wait(pe, xT_sb, t + 1)
                    flat = probs[:, :, :].rearrange("p (n j) k -> p n (j k)", j=2)
                    for b in (0, 1):
                        for n in range(4):
                            mm = pe.transpose(ps_T[:, b, n, :], flat[:, 4 * b + n, :], ident[:, :])
                        mm.then_inc(pT_ps.sem, 1)
                    wait(pe, pairs_done, t)
                    wait(pe, res_done, t - 1)
                    for n in range(HH):
                        if n % 4 == 0:
                            wait(pe, pT_sb, t, n // 4 + 1)
                        for ch in range(CH):
                            q = slice(ch * CHUNK, (ch + 1) * CHUNK)
                            mm = pe.matmul(ps_o[q, n * 2 * C_DIM:(n + 1) * 2 * C_DIM], pT[:, n, q],
                                           v_pairs[u][:, ch, n, :, :].rearrange("p j d -> p (j d)"), start=True, stop=True)
                    mm.then_inc(pv_ps.sem, 1)
                    wait(pe, cross_exp, t)
                    wait(pe, vsum_done, t - 1)
                    pe.matmul(ps_c[:, DIM:2 * DIM], cum_w[:, 0, :], v_sum[u][:, :], start=True, stop=False)
                    pe.matmul(ps_c[:, DIM:2 * DIM], cum_w[:, 1, :], v[u][:, 0, :], start=False, stop=True)\
                        .then_inc(cumv_ps.sem, 1)

                tile_pairs(pe, TILES // 2, tile)
                turn_o(TILES - 1)
                project_out(TILES - 1)
FILTER = 1024
ORDER = 64
STEP = 64
STEPS = TOKENS // STEP
SPANS = FILTER // P + 1
PADDED = FILTER + 2 * P
STARTS = P + STEP
TWO_PI = (6.28125, 0.0019350051879882812, 3.0199157663446385e-07)
ROUND = 12582912.0
PI = 3.1415925


def filter_taps(nc, taps_by_start, features_dram, w1, b1_freq1, w2, b2_freq2, w3, b3_freq3, w_taps, decay_dram,
                bypass_dram):
    with ExitStack() as stack:
        s = Scope(nc, stack, "taps")
        features = s.sbuf("features", [3, FILTER])
        w = [s.sbuf(f"w{n}", [3 if n == 0 else ORDER, ORDER]) for n in range(3)]
        bf = [s.sbuf(f"bf{n}", [ORDER, 2]) for n in range(3)]
        w_last = s.sbuf("w_last", [ORDER, DIM])
        decay = s.sbuf("decay", [P, KT, FILTER])
        bypass = s.sbuf("bypass", [P, KT])
        arg = s.sbuf("arg", [ORDER, FILTER])
        turns = s.sbuf("turns", [ORDER, FILTER])
        h = s.sbuf("h", [ORDER, FILTER])
        taps = s.sbuf("taps", [P, KT, PADDED])
        by_start = s.sbuf("ordered", [P, KT, STARTS, SPANS])
        ps_h = s.psum("ps_h", [ORDER, 2, PSUM_F32])
        ps_k = s.psum("ps_k", [P, KT, 2, PSUM_F32])
        loaded, product, sined, step, final_ps, stored = [s.sem(n) for n in
                                                          ("loaded", "product", "sined", "step", "final_ps", "stored")]
        n_loads = 10
        LAYERS = 3

        with nc.Block() as block:

            @block.sync
            def _(sp):
                for dst, src in [(features[:, :], features_dram), (w[0][:, :], w1), (w[1][:, :], w2), (w[2][:, :], w3),
                                 (bf[0][:, :], b1_freq1), (bf[1][:, :], b2_freq2), (bf[2][:, :], b3_freq3),
                                 (w_last[:, :], w_taps), (decay[:, :, :], decay_dram), (bypass[:, :], bypass_dram)]:
                    sp.dma_start(dst, src).then_inc(loaded, DMA)
                sp.wait_ge(step, LAYERS * 7 + 6)
                sp.dma_start(taps_by_start.rearrange("(k p) t -> p k t", p=P),
                             by_start[:, :, :, :].rearrange("p k r j -> p k (r j)")).then_inc(stored, DMA)
                sp.wait_ge(stored, DMA)

            @block.tensor
            def _(pe):
                pe.wait_ge(loaded, n_loads * DMA)
                for n in range(LAYERS):
                    if n:
                        pe.wait_ge(sined, n)
                    for half in (0, 1):
                        cols = slice(half * PSUM_F32, (half + 1) * PSUM_F32)
                        mm = pe.matmul(ps_h[:, half, :], w[n][:, :], features[:, cols] if n == 0 else h[:, cols],
                                       start=True, stop=True)
                    mm.then_inc(product, 1)
                pe.wait_ge(sined, LAYERS)
                for k in range(KT):
                    for half in (0, 1):
                        mm = pe.matmul(ps_k[:, k, half, :], w_last[:, k * P:(k + 1) * P],
                                       h[:, half * PSUM_F32:(half + 1) * PSUM_F32], start=True, stop=True)
                mm.then_inc(final_ps, 1)

            @block.vector
            def _(dve):
                done = 0
                dve.memset(taps[:, :, :], 0.0).then_inc(step, 1)
                done += 1
                dve.wait_ge(loaded, n_loads * DMA)
                for n in range(LAYERS):
                    dve.wait_ge(product, n + 1)
                    if n:
                        dve.wait_ge(sined, n)
                    flat = ps_h[:, :, :].rearrange("p a b -> p (a b)")
                    dve.tensor_scalar(arg[:, :], flat, bf[n][:, 0:1], bf[n][:, 1:2], ALU.add, ALU.mult).then_inc(step, 1)
                    done += 1
                    dve.wait_ge(step, done)
                    dve.tensor_scalar(turns[:, :], arg[:, :], 1.0 / (2 * np.pi), ROUND, ALU.mult, ALU.add).then_inc(step, 1)
                    done += 1
                    dve.wait_ge(step, done)
                    dve.tensor_scalar(turns[:, :], turns[:, :], ROUND, None, ALU.subtract).then_inc(step, 1)
                    done += 1
                    for part in TWO_PI:
                        dve.wait_ge(step, done)
                        dve.scalar_tensor_tensor(out=arg[:, :], in0=turns[:, :], scalar=-part, in1=arg[:, :],
                                                 op0=ALU.mult, op1=ALU.add).then_inc(step, 1)
                        done += 1
                    dve.wait_ge(step, done)
                    dve.tensor_scalar(arg[:, :], arg[:, :], PI, -PI, ALU.min, ALU.max).then_inc(step, 1)
                    done += 1
                dve.wait_ge(final_ps, 1)
                for k in range(KT):
                    dve.tensor_tensor(taps[:, k, STEP - 1:STEP - 1 + FILTER], ps_k[:, k, :, :].rearrange("p a b -> p (a b)"),
                                      decay[:, k, :], ALU.mult).then_inc(step, 1)
                    done += 1
                dve.wait_ge(step, done)
                dve.tensor_tensor(taps[:, :, STEP - 1], taps[:, :, STEP - 1], bypass[:, :], ALU.add).then_inc(step, 1)
                done += 1
                dve.wait_ge(step, done)
                for first, n in ((0, P), (P, STARTS - P)):
                    spans = taps[:, :, first:first + SPANS * P].rearrange("p k (j r) -> p k r j", r=P)
                    dve.tensor_copy(by_start[:, :, first:first + n, :], spans[:, :, 0:n, :]).then_inc(step, 1)

            @block.scalar
            def _(act):
                for n in range(LAYERS):
                    act.wait_ge(step, 1 + 7 * (n + 1))
                    act.activation(h[:, :], arg[:, :], ACT.Sin).then_inc(sined, 1)


UP = 3 * DIM // P


def gated_input(nc, u_dram, w_in_dram, columns_dram, ident_dram, x0_tok, v_tok):
    with ExitStack() as stack:
        s = Scope(nc, stack, "gate")
        w_in = s.sbuf("w_in", [P, KT, 3 * DIM])
        ident = s.sbuf("ident", [P, P])
        col = s.sbuf("col", [P, 5, UP])
        x = [s.sbuf(f"x{u}", [P, GROUP, DIM]) for u in (0, 1)]
        xT = s.sbuf("xT", [P, KT, GT])
        up = [s.sbuf(f"up{u}", [P, UP, 2 + GT]) for u in (0, 1)]
        conv = s.sbuf("conv", [P, UP, GT])
        v_rev = s.sbuf("v_rev", [P, KT, GT + STEP])
        ps_T = s.psum("ps_T", [P, KT, GT])
        ps_up = s.psum("ps_up", [P, 2, GT])
        ps_tok = s.psum("ps_tok", [P, 4, GROUP, P])
        in_sem, consts_set = s.sem("const_in"), s.sem("consts_set")
        x_loaded = [s.sem(f"x_loaded{u}") for u in (0, 1)]
        c = lambda name, n=1: s.count(name, n)
        xT_ps, xT_sb, up_ps, up_sb = c("xT_ps"), c("xT_sb"), c("up_ps", UP), c("up_sb", UP)
        tap2, tap1, tap0, carried = c("tap2", UP), c("tap1", UP), c("tap0", UP), c("carried")
        kept = c("kept")
        gated, tok_ps, tok_sb = c("gated"), c("tok_ps", 8), c("tok_sb", 8)

        with nc.Block() as block:

            @block.sync
            def _(sp):
                def load(g, u):
                    sp.dma_start(x[u][:, :, :], u_dram[bass.ds(g * GT, GT), :].rearrange("(n p) d -> p n d", p=P))\
                        .then_inc(x_loaded[u], DMA)

                for u in (0, 1):
                    load(u, u)
                for dst, src in ((ident[:, :], ident_dram), (col[:, :, :], columns_dram),
                                 (w_in[:, :, :], w_in_dram.rearrange("(k p) n -> p k n", p=P))):
                    sp.dma_start(dst, src).then_inc(in_sem, DMA)
                with sp.Fori(0, GROUPS // 2 - 1) as i:
                    for u in (0, 1):
                        wait(sp, xT_ps, i * 2 + u)
                        load(i * 2 + u + 2, u)

            @block.scalar
            def _(act):
                for q in (xT_sb, up_sb, tok_sb):
                    q.prime(act)
                act.wait_ge(in_sem, 3 * DMA)
                with act.Fori(0, GROUPS // 2) as i:
                    for u in (0, 1):
                        g = i * 2 + u
                        wait(act, xT_ps, g)
                        wait(act, up_ps, g - 1)
                        act.copy(xT[:, :, :], ps_T[:, :, :]).then_inc(xT_sb.sem, 1)
                        wait(act, tap0, g - 2)
                        wait(act, carried, g - 2)
                        for f in range(UP):
                            wait(act, up_ps, g, f + 1)
                            act.activation(up[u][:, f, 2:2 + GT], ps_up[:, f % 2, :], ACT.Identity,
                                           bias=col[:, 0, f:f + 1]).then_inc(up_sb.sem, 1)
                        for n in range(8):
                            wait(act, tok_ps, g, n + 1)
                            kind, k, part = n // 4, n // 2 % 2, n % 2
                            rows = P if kind else STEP
                            dst = (v_tok if kind else x0_tok)[0:rows, k * P:(k + 1) * P, bass.ds(g * 2 * GROUP + part * GROUP, GROUP)]
                            act.activation(dst.rearrange("p c b -> p b c"), ps_tok[0:rows, n % 4, :, :], ACT.Copy)\
                                .then_inc(tok_sb.sem, 1)

            @block.vector
            def _(dve):
                for q in (tap2, tap1, tap0, carried, kept, gated):
                    q.prime(dve)
                for u in (0, 1):
                    dve.memset(up[u][:, :, 0:2], 0.0).then_inc(consts_set, 1)
                dve.memset(v_rev[:, :, 0:STEP], 0.0).then_inc(consts_set, 1)
                dve.wait_ge(in_sem, 3 * DMA)
                dve.wait_ge(consts_set, 3)
                with dve.Fori(0, GROUPS // 2) as i:
                    for u in (0, 1):
                        g = i * 2 + u
                        wait(dve, carried, g - 1)
                        wait(dve, tok_ps, g - 1, 4)
                        wait(dve, gated, g - 1)
                        for f in range(UP):
                            wait(dve, up_sb, g, f + 1)
                            dve.tensor_scalar(conv[:, f, :], up[u][:, f, 2:2 + GT], col[:, 3, f:f + 1], col[:, 4, f:f + 1],
                                              ALU.mult, ALU.add).then_inc(tap2.sem, 1)
                        for tap, count, before in ((2, tap1, tap2), (1, tap0, tap1)):
                            for f in range(UP):
                                wait(dve, before, g, f + 1)
                                dve.scalar_tensor_tensor(out=conv[:, f, :], in0=up[u][:, f, tap - 1:tap - 1 + GT],
                                                         scalar=col[:, tap, f:f + 1], in1=conv[:, f, :],
                                                         op0=ALU.mult, op1=ALU.add).then_inc(count.sem, 1)
                        wait(dve, tap0, g - 1)
                        dve.tensor_copy(up[1 - u][:, :, 0:2], up[u][:, :, GT:GT + 2]).then_inc(carried.sem, 1)
                        wait(dve, tap0, g)
                        wait(dve, tok_ps, g - 1)
                        dve.tensor_copy(v_rev[:, :, GT:GT + STEP], v_rev[:, :, 0:STEP]).then_inc(kept.sem, 1)
                        wait(dve, kept, g)
                        for k in range(KT):
                            last = dve.tensor_tensor(v_rev[:, k, 0:GT][:, ::-1], conv[:, 2 + k, :], conv[:, 4 + k, :], ALU.mult)
                        last.then_inc(gated.sem, 1)

            @block.tensor
            def _(pe):
                for q in (xT_ps, up_ps, tok_ps):
                    q.prime(pe)
                pe.wait_ge(in_sem, 3 * DMA)

                def project(g, u, i):
                    pe.wait_ge(x_loaded[u], (i + 1) * DMA)
                    wait(pe, xT_sb, g - 1)
                    for k in range(KT):
                        for n in range(GROUP):
                            mm = pe.transpose(ps_T[:, k, n * P:(n + 1) * P], x[u][:, n, k * P:(k + 1) * P], ident[:, :])
                    mm.then_inc(xT_ps.sem, 1)
                    wait(pe, xT_sb, g)
                    for f in range(UP):
                        if f < 2:
                            wait(pe, up_sb, g - 1, f + UP - 1)
                        else:
                            wait(pe, up_sb, g, f - 1)
                        for k in range(KT):
                            mm = pe.matmul(ps_up[:, f % 2, :], w_in[:, k, f * P:(f + 1) * P], xT[:, k, :],
                                           start=(k == 0), stop=(k == KT - 1))
                        mm.then_inc(up_ps.sem, 1)

                def to_tokens(g):
                    for n in range(8):
                        if n < 4:
                            wait(pe, tok_sb, g - 1, n + 5)
                        else:
                            wait(pe, tok_sb, g, n - 3)
                        if n == 0:
                            wait(pe, tap0, g, 2)
                        if n == 4:
                            wait(pe, gated, g)
                        k, part = n // 2 % 2, n % 2
                        if n < 4:
                            pe.matmul(ps_tok[:, n % 4, 0, 0:STEP], ident[:, :], ident[:, 0:STEP], start=True, stop=True)
                        for b in range(GROUP):
                            step = part * GROUP + b
                            if n < 4:
                                mm = pe.transpose(ps_tok[0:STEP, n % 4, b, :], conv[:, k, step * STEP:(step + 1) * STEP],
                                                  ident[:, :])
                            else:
                                first = GT - (step + 1) * STEP
                                mm = pe.transpose(ps_tok[:, n % 4, b, :], v_rev[:, k, first:first + P], ident[:, :])
                        mm.then_inc(tok_ps.sem, 1)

                project(0, 0, 0)

                def group(g, u, i, more):
                    to_tokens(g)
                    if more:
                        project(g + 1, 1 - u, i + u)

                tile_pairs(pe, GROUPS // 2, group)


RING = 4
CONV_GROUP = 8


def long_convolution(nc, taps_by_start, x0_tok, v_tok, prefetch=None):
    with ExitStack() as stack:
        s = Scope(nc, stack, "conv")
        toep = [s.sbuf(f"toep{r}", [P, STEP, SPANS]) for r in range(RING)]
        ps = s.psum("ps", [STEP, 2, CONV_GROUP, STEPS])
        loaded = [s.sem(f"loaded{r}") for r in range(RING)]
        used = s.count("used", CONV_GROUP)
        multiplied = s.count("multiplied")
        groups = DIM // CONV_GROUP
        turns = CONV_GROUP // RING
        row = STARTS * SPANS

        with nc.Block() as block:

            def load(queue, ch, r):
                rows = bass.AP(tensor=taps_by_start.tensor, offset=ch * row, ap=[[SPANS, P], [1, STEP * SPANS]])
                queue.dma_start(toep[r][:, :, :].rearrange("p q j -> p (q j)"), rows).then_inc(loaded[r], DMA)

            def load_share(queue, which):
                for r in range(which, RING, 2):
                    load(queue, r, r)
                if prefetch and which == 0:
                    prefetch(queue)
                with queue.Fori(0, groups - 1) as g:
                    for n in range(which, CONV_GROUP, 2):
                        wait(queue, used, g, n + 1)
                        load(queue, g * CONV_GROUP + n + RING, n % RING)
                for n in range(which, CONV_GROUP - RING, 2):
                    wait(queue, used, groups - 1, n + 1)
                    load(queue, DIM - CONV_GROUP + n + RING, n % RING)

            @block.sync
            def _(sp):
                load_share(sp, 0)

            @block.scalar
            def _(act):
                load_share(act, 1)

            @block.tensor
            def _(pe):
                used.prime(pe)
                with pe.Fori(0, groups // 2) as i:
                    for u in (0, 1):
                        g = i * 2 + u
                        wait(pe, multiplied, g - 2)
                        for n in range(CONV_GROUP):
                            pe.wait_ge(loaded[n % RING], (g * turns + n // RING + 1) * DMA)
                            for j in range(SPANS):
                                mm = pe.matmul(ps[:, u, n, 2 * j:STEPS], toep[n % RING][:, :, j],
                                               v_tok[:, g * CONV_GROUP + n, 0:STEPS - 2 * j],
                                               start=(j == 0), stop=(j == SPANS - 1))
                            mm.then_inc(used.sem, 1)

            @block.vector
            def _(dve):
                multiplied.prime(dve)
                with dve.Fori(0, groups // 2) as i:
                    for u in (0, 1):
                        g = i * 2 + u
                        wait(dve, used, g)
                        x0 = x0_tok[0:STEP, bass.ds(g * CONV_GROUP, CONV_GROUP), :]
                        dve.tensor_tensor(x0, ps[:, u, :, :], x0, ALU.mult).then_inc(multiplied.sem, 1)


def project_and_norm(nc, z_tok, u_dram, x_out, w_out_dram, b_out_dram, ident_dram, prefetch=None):
    with ExitStack() as stack:
        s = Scope(nc, stack, "out0")
        w_out = s.sbuf("w_out", [P, KT, DIM])
        b_out = s.sbuf("b_out", [P, DIM])
        ident = s.sbuf("ident", [P, P])
        minus_half = s.sbuf("minus_half", [P, 1])
        x = [s.sbuf(f"x{u}", [P, DIM]) for u in (0, 1)]
        z = [s.sbuf(f"z{u}", [STEP, 2, DIM]) for u in (0, 1)]
        zT = [s.sbuf(f"zT{u}", [P, KT, P]) for u in (0, 1)]
        res = [s.sbuf(f"res{u}", [P, DIM]) for u in (0, 1)]
        stats = s.sbuf("stats", [P, 6])
        mean_var = s.sbuf("mean_var", [P, 2, 2])
        var_eps = s.sbuf("var_eps", [P, 2])
        rstd = s.sbuf("rstd", [P, 2])
        spare = s.sbuf("spare", [P, 2])
        y = [s.sbuf(f"y{u}", [P, DIM]) for u in (0, 1)]
        ps_T = s.psum("ps_T", [P, 2, PSUM_F32])
        ps_y = s.psum("ps_y", [P, 2, PSUM_F32])
        in_sem, consts_set = s.sem("const_in"), s.sem("consts_set")
        x_loaded = [s.sem(f"x_loaded{u}") for u in (0, 1)]
        y_stored = [s.sem(f"y_stored{u}") for u in (0, 1)]
        c = lambda name, n=1: s.count(name, n)
        z_copied, z_ps, z_sb, y_ps, biased = c("z_copied"), c("z_ps"), c("z_sb"), c("y_ps"), c("biased")
        res_done, stats_done, mean_done, eps_done = c("res_done"), c("stats_done"), c("mean_done"), c("eps_done")
        rstd_done, y_done = c("rstd_done"), c("y_done")

        with nc.Block() as block:

            @block.sync
            def _(sp):
                def load(t, u):
                    sp.dma_start(x[u][:, :], u_dram[bass.ds(t * P, P), :]).then_inc(x_loaded[u], DMA)

                for u in (0, 1):
                    sp.sem_inc(y_stored[u], DMA)
                    load(u, u)
                for dst, src in ((ident[:, :], ident_dram), (b_out[:, :], b_out_dram.to_broadcast([P, DIM])),
                                 (w_out[:, :, :], w_out_dram.rearrange("(k p) n -> p k n", p=P))):
                    sp.dma_start(dst, src).then_inc(in_sem, DMA)
                if prefetch:
                    prefetch(sp)

                def store(t, u):
                    wait(sp, y_done, t)
                    sp.dma_start(x_out[bass.ds(t * P + 1, P), :], y[u][:, :]).then_inc(y_stored[u], DMA)

                with sp.Fori(0, TILES // 2 - 1) as i:
                    for u in (0, 1):
                        store(i * 2 + u, u)
                        load(i * 2 + u + 2, u)
                for u in (0, 1):
                    store(TILES - 2 + u, u)
                for u in (0, 1):
                    sp.wait_ge(y_stored[u], DMA * (TILES // 2 + 1))

            @block.gpsimd
            def _(pool):
                for q in (biased, rstd_done):
                    q.prime(pool)
                pool.memset(minus_half[:, :], -0.5).then_inc(consts_set, 1)
                pool.wait_ge(consts_set, 1)
                pool.wait_ge(in_sem, 3 * DMA)
                with pool.Fori(0, TILES // 2) as i:
                    for u in (0, 1):
                        t = i * 2 + u
                        pool.wait_ge(x_loaded[u], (i + 1) * DMA)
                        pool.tensor_tensor(x[u][:, :], x[u][:, :], b_out[:, :], ALU.add).then_inc(biased.sem, 1)
                        wait(pool, eps_done, t)
                        wait(pool, y_done, t - 2)
                        pool.tensor_tensor(rstd[:, u:u + 1], var_eps[:, u:u + 1], minus_half[:, :], ALU.pow)\
                            .then_inc(rstd_done.sem, 1)

            @block.scalar
            def _(act):
                for q in (z_copied, z_sb):
                    q.prime(act)

                def gather(t, u):
                    wait(act, z_ps, t - 2)
                    act.activation(z[u][:, :, :], z_tok[0:STEP, :, bass.ds(t * 2, 2)].rearrange("p c n -> p n c"), ACT.Copy)\
                        .then_inc(z_copied.sem, 1)

                gather(0, 0)

                def tile(t, u, i, more):
                    if more:
                        gather(t + 1, 1 - u)
                    wait(act, z_ps, t)
                    wait(act, y_ps, t - 2)
                    act.copy(zT[u][:, :, :], ps_T[:, u, 0:DIM].rearrange("p (k t) -> p k t", k=KT)).then_inc(z_sb.sem, 1)

                tile_pairs(act, TILES // 2, tile)

            @block.vector
            def _(dve):
                for q in (res_done, stats_done, mean_done, eps_done, y_done):
                    q.prime(dve)

                def normalise(t, u, i):
                    wait(dve, rstd_done, t)
                    dve.wait_ge(y_stored[u], (i + 1) * DMA)
                    dve.tensor_scalar(y[u][:, :], res[u][:, :], mean_var[:, u, 0:1], rstd[:, u:u + 1],
                                      ALU.subtract, ALU.mult).then_inc(y_done.sem, 1)

                def tile(t, u, i, more):
                    wait(dve, y_ps, t)
                    wait(dve, biased, t)
                    wait(dve, y_done, t - 2)
                    dve.tensor_tensor(res[u][:, :], ps_y[:, u, 0:DIM], x[u][:, :], ALU.add).then_inc(res_done.sem, 1)
                    wait(dve, res_done, t)
                    wait(dve, mean_done, t - 1)
                    dve.bn_stats(stats[:, :], res[u][:, :]).then_inc(stats_done.sem, 1)
                    wait(dve, stats_done, t)
                    dve.memset(spare[:, :], 0.0)
                    dve.bn_aggr(mean_var[:, u, :], stats[:, :]).then_inc(mean_done.sem, 1)
                    wait(dve, mean_done, t)
                    wait(dve, rstd_done, t - 2)
                    dve.tensor_scalar(var_eps[:, u:u + 1], mean_var[:, u, 1:2], EPS, None, ALU.add).then_inc(eps_done.sem, 1)
                    normalise(t, u, i)

                tile_pairs(dve, TILES // 2, tile)

            @block.tensor
            def _(pe):
                for q in (z_ps, y_ps):
                    q.prime(pe)
                pe.wait_ge(in_sem, 3 * DMA)
                with pe.Fori(0, TILES // 2) as i:
                    for u in (0, 1):
                        t = i * 2 + u
                        wait(pe, z_copied, t)
                        wait(pe, z_sb, t - 2)
                        pe.matmul(ps_T[:, u, 0:STEP], ident[:, :], ident[:, 0:STEP], start=True, stop=True)
                        for k in range(KT):
                            for n in (0, 1):
                                mm = pe.transpose(ps_T[:, u, k * P + n * STEP:k * P + (n + 1) * STEP],
                                                  z[u][:, n, k * P:(k + 1) * P], ident[0:STEP, 0:STEP])
                        mm.then_inc(z_ps.sem, 1)
                        wait(pe, z_sb, t)
                        wait(pe, res_done, t - 2)
                        for k in range(KT):
                            mm = pe.matmul(ps_y[:, u, 0:DIM], zT[u][:, k, :], w_out[:, k, :],
                                           start=(k == 0), stop=(k == KT - 1))
                        mm.then_inc(y_ps.sem, 1)
EXPERTS = 8
FF = 4 * DIM
FT = FF // P
TOP_K = 2
BLOCKS = TOKENS * TOP_K // P + EXPERTS
ROWS = BLOCKS * P


def route(nc, x_in, x_all, position, weight, block_expert, router_w_dram, router_b_dram, ident_dram, before_dram,
          numbers_dram, sorted_rows, scratch):
    with ExitStack() as stack:
        s = Scope(nc, stack, "route")
        TE = [P, TILES, EXPERTS]
        ident = s.sbuf("ident", [P, P])
        before = s.sbuf("before", [P, 2, P])
        numbers = s.sbuf("numbers", [P, BLOCKS])
        router_w = s.sbuf("router_w", [P, KT, EXPERTS])
        router_b = s.sbuf("router_b", [P, EXPERTS])
        xT = s.sbuf("xT", [P, 2, KT, P])
        logits = s.sbuf("logits", TE)
        best = s.sbuf("best", [P, TILES])
        probs = s.sbuf("probs", TE)
        norm = s.sbuf("norm", [P, TILES])
        same = s.sbuf("same", TE)
        first = s.sbuf("first", [P, TILES])
        chosen = s.sbuf("chosen", [P, TOP_K] + TE[1:])
        both = s.sbuf("both", TE)
        upto = [s.sbuf(f"upto{n}", TE) for n in (0, 1)]
        rank = s.sbuf("rank", TE)
        blocks = s.sbuf("blocks", [P, EXPERTS])
        ends = s.sbuf("ends", [P, EXPERTS + 1])
        place = s.sbuf("place", TE)
        pos_f = s.sbuf("pos_f", [P, TOP_K, TILES])
        passed = scratch[:, 0:BLOCKS * EXPERTS].rearrange("p (b e) -> p b e", e=EXPERTS)
        expert_f = s.sbuf("expert_f", [P, BLOCKS])
        ps_T = s.psum("ps_T", [P, 2, PSUM_F32])
        ps_l = s.psum("ps_l", [P, 2, PSUM_F32])
        ps_rank = s.psum("ps_rank", [P, 2, PSUM_F32])
        in_sem, x_sem = s.sem("const_in"), s.sem("x_loaded")
        c = lambda name, n=1: s.count(name, n)
        xT_ps, xT_sb, l_ps, l_sb = c("xT_ps"), c("xT_sb"), c("l_ps"), c("l_sb")
        step, shifted, exped, mask_ready, ranked, placed, scattered = [
            s.sem(n) for n in ("step", "shifted", "exped", "mask_ready", "ranked", "placed", "scattered")]
        Q = 4

        with nc.Block() as block:

            @block.sync
            def _(sp):
                for n in range(0, TILES, Q):
                    sp.dma_start(x_all[:, n:n + Q, :], x_in[1 + n * P:1 + (n + Q) * P, :].rearrange("(n p) d -> p n d", p=P))\
                        .then_inc(x_sem, DMA)
                for dst, src in ((ident[:, :], ident_dram), (before[:, :, :], before_dram), (numbers[:, :], numbers_dram),
                                 (router_w[:, :, :], router_w_dram.rearrange("(k p) e -> p k e", p=P)),
                                 (router_b[:, :], router_b_dram.to_broadcast([P, EXPERTS]))):
                    sp.dma_start(dst, src).then_inc(in_sem, DMA)

            @block.tensor
            def _(pe):
                xT_ps.prime(pe)
                l_ps.prime(pe)
                pe.wait_ge(in_sem, 5 * DMA)
                pe.wait_ge(x_sem, TILES // Q * DMA)
                for t in range(TILES):
                    u = t % 2
                    wait(pe, xT_sb, t - 2)
                    for k in range(KT):
                        mm = pe.transpose(ps_T[:, u, k * P:(k + 1) * P], x_all[:, t, k * P:(k + 1) * P], ident[:, :])
                    mm.then_inc(xT_ps.sem, 1)
                    wait(pe, xT_sb, t)
                    wait(pe, l_sb, t - 2)
                    for k in range(KT):
                        mm = pe.matmul(ps_l[:, u, 0:EXPERTS], xT[:, u, k, :], router_w[:, k, :],
                                       start=(k == 0), stop=(k == KT - 1))
                    mm.then_inc(l_ps.sem, 1)
                pe.wait_ge(mask_ready, 1)
                for n in (0, 1):
                    mm = pe.matmul(ps_rank[:, n, 0:TILES * EXPERTS], before[:, n, :],
                                   both[:, :, :].rearrange("p t e -> p (t e)"), start=True, stop=True)
                mm.then_inc(ranked, 1)

            @block.scalar
            def _(act):
                xT_sb.prime(act)
                for t in range(TILES):
                    wait(act, xT_ps, t)
                    wait(act, l_ps, t - 2)
                    act.copy(xT[:, t % 2, :, :], ps_T[:, t % 2, 0:DIM].rearrange("p (k t) -> p k t", k=KT))\
                        .then_inc(xT_sb.sem, 1)
                act.wait_ge(shifted, 1)
                act.activation(probs[:, :, :], logits[:, :, :], ACT.Exp).then_inc(exped, 1)

            @block.vector
            def _(dve):
                l_sb.prime(dve)
                dve.wait_ge(in_sem, 5 * DMA)
                for t in range(TILES):
                    wait(dve, l_ps, t)
                    dve.tensor_tensor(logits[:, t, :], ps_l[:, t % 2, 0:EXPERTS], router_b[:, :], ALU.add)\
                        .then_inc(l_sb.sem, 1)
                wait(dve, l_sb, TILES - 1)
                done = 0

                def then(ins):
                    nonlocal done
                    ins.then_inc(step, 1)
                    done += 1
                    dve.wait_ge(step, done)

                over_e = lambda a: a.unsqueeze(2).to_broadcast(TE)
                over_t = lambda a: a.unsqueeze(1).to_broadcast(TE)
                number = over_t(numbers[:, 0:EXPERTS])
                then(dve.reduce_max(best[:, :], logits[:, :, :], axis=AX_X))
                dve.tensor_tensor(logits[:, :, :], logits[:, :, :], over_e(best[:, :]), ALU.subtract).then_inc(shifted, 1)
                dve.wait_ge(exped, 1)
                then(dve.reduce_sum(norm[:, :], probs[:, :, :], axis=AX_X))
                then(dve.reciprocal(norm[:, :], norm[:, :]))
                then(dve.tensor_tensor(probs[:, :, :], probs[:, :, :], over_e(norm[:, :]), ALU.mult))
                for k in range(TOP_K):
                    then(dve.reduce_max(weight[:, k, :], probs[:, :, :], axis=AX_X))
                    then(dve.tensor_tensor(same[:, :, :], probs[:, :, :], over_e(weight[:, k, :]), ALU.is_ge))
                    then(dve.tensor_scalar(same[:, :, :], same[:, :, :], -float(EXPERTS), float(EXPERTS), ALU.mult, ALU.add))
                    then(dve.tensor_tensor(same[:, :, :], same[:, :, :], number, ALU.add))
                    then(dve.tensor_reduce(first[:, :], same[:, :, :], AX_X, ALU.min))
                    then(dve.tensor_tensor(chosen[:, k, :, :], number, over_e(first[:, :]), ALU.is_equal))
                    if k < TOP_K - 1:
                        then(dve.scalar_tensor_tensor(out=probs[:, :, :], in0=chosen[:, k, :, :], scalar=-2.0,
                                                      in1=probs[:, :, :], op0=ALU.mult, op1=ALU.add))
                dve.tensor_tensor(both[:, :, :], chosen[:, 0, :, :], chosen[:, 1, :, :], ALU.add).then_inc(mask_ready, 1)
                dve.wait_ge(ranked, 1)
                flat = lambda a: a.rearrange("p t e -> p (t e)")
                total = ps_rank[:, 1, 0:TILES * EXPERTS]
                then(dve.tensor_copy(flat(upto[0][:, :, :]), total))
                src, n = 0, 1
                while n < TILES:
                    a, b = upto[src], upto[1 - src]
                    then(dve.tensor_copy(b[:, 0:n, :], a[:, 0:n, :]))
                    then(dve.tensor_tensor(b[:, n:, :], a[:, n:, :], a[:, 0:TILES - n, :], ALU.add))
                    src, n = 1 - src, 2 * n
                upto_t = upto[src]
                then(dve.tensor_tensor(flat(rank[:, :, :]), flat(upto_t[:, :, :]), total, ALU.subtract))
                then(dve.tensor_tensor(flat(rank[:, :, :]), flat(rank[:, :, :]), ps_rank[:, 0, 0:TILES * EXPERTS], ALU.add))
                then(dve.tensor_scalar(blocks[:, :], upto_t[:, TILES - 1, :], 1.0 / P, (P - 1) / P - (P - 1) / (2 * P),
                                       ALU.mult, ALU.add))
                then(dve.tensor_scalar(blocks[:, :], blocks[:, :], ROUND, None, ALU.add))
                then(dve.tensor_scalar(blocks[:, :], blocks[:, :], ROUND, None, ALU.subtract))
                then(dve.memset(ends[:, 0:1], 0.0))
                for e in range(EXPERTS):
                    then(dve.tensor_tensor(ends[:, e + 1:e + 2], ends[:, e:e + 1], blocks[:, e:e + 1], ALU.add))
                then(dve.scalar_tensor_tensor(out=place[:, :, :], in0=over_t(ends[:, 0:EXPERTS]), scalar=float(P),
                                              in1=rank[:, :, :], op0=ALU.mult, op1=ALU.add))
                for k in range(TOP_K):
                    then(dve.tensor_tensor(same[:, :, :], chosen[:, k, :, :], place[:, :, :], ALU.mult))
                    then(dve.reduce_sum(pos_f[:, k, :], same[:, :, :], axis=AX_X))
                dve.tensor_copy(position[:, :, :], pos_f[:, :, :]).then_inc(placed, 1)
                wide = [P, BLOCKS, EXPERTS]
                then(dve.tensor_tensor(passed[:, :, :], ends[:, 1:].unsqueeze(1).to_broadcast(wide),
                                       numbers[:, :].unsqueeze(2).to_broadcast(wide), ALU.is_le))
                then(dve.reduce_sum(expert_f[:, :], passed[:, :, :], axis=AX_X))
                then(dve.tensor_scalar(expert_f[:, :], expert_f[:, :], float(EXPERTS - 1), None, ALU.min))
                then(dve.tensor_copy(block_expert[:, :], expert_f[0:1, :]))

            @block.gpsimd
            def _(pool):
                pool.wait_ge(placed, 1)
                pool.wait_ge(x_sem, TILES // Q * DMA)
                for t in range(TILES):
                    for k in range(TOP_K):
                        pool.indirect_dma_start(out=sorted_rows, out_offset=bass.IndirectOffsetOnAxis(
                            ap=position[:, k, t:t + 1], axis=0), in_=x_all[:, t, :], in_offset=None)\
                            .then_inc(scattered, DMA)
                pool.wait_ge(scattered, TILES * TOP_K * DMA)


def experts(nc, sorted_rows, expert_rows, block_expert, w_up, w_down, up_loaded, down_loaded, ident_dram):
    with ExitStack() as stack:
        s = Scope(nc, stack, "expert")
        ident = s.sbuf("ident", [P, P])
        x = [s.sbuf(f"x{u}", [P, DIM]) for u in (0, 1)]
        xT = s.sbuf("xT", [P, KT, P])
        h = [s.sbuf(f"h{n}", [P, FF // 2]) for n in (0, 1)]
        hT = s.sbuf("hT", [P, FT, P])
        y = [s.sbuf(f"y{u}", [P, DIM]) for u in (0, 1)]
        ps_x = s.psum("ps_x", [P, PSUM_F32])
        ps_h = s.psum("ps_h", [P, 2, PSUM_F32])
        ps_T = s.psum("ps_T", [P, 2, PSUM_F32])
        ps_y = s.psum("ps_y", [P, 2, PSUM_F32])
        in_sem = s.sem("const_in")
        x_loaded = [s.sem(f"x_loaded{u}") for u in (0, 1)]
        y_stored = [s.sem(f"y_stored{u}") for u in (0, 1)]
        c = lambda name, n=1: s.count(name, n)
        xT_ps, xT_sb, h_ps, gelu_done = c("xT_ps"), c("xT_sb"), c("h_ps", 2), c("gelu_done", 2)
        hT_ps, hT_sb0, hT_sb1, y_ps, y_done = c("hT_ps", 2), c("hT_sb0"), c("hT_sb1"), c("y_ps"), c("y_done")

        with nc.Block() as block:

            @block.sync
            def _(sp):
                def load(g, u):
                    sp.dma_start(x[u][:, :], sorted_rows[bass.ds(g * P, P), :]).then_inc(x_loaded[u], DMA)

                sp.dma_start(ident[:, :], ident_dram).then_inc(in_sem, DMA)
                for u in (0, 1):
                    sp.sem_inc(y_stored[u], DMA)
                    load(u, u)

                def store(g, u):
                    wait(sp, y_done, g)
                    sp.dma_start(expert_rows[bass.ds(g * P, P), :], y[u][:, :]).then_inc(y_stored[u], DMA)

                with sp.Fori(0, BLOCKS // 2 - 1) as i:
                    for u in (0, 1):
                        wait(sp, xT_ps, i * 2 + u)
                        load(i * 2 + u + 2, u)
                        store(i * 2 + u, u)
                for u in (0, 1):
                    store(BLOCKS - 2 + u, u)
                for u in (0, 1):
                    sp.wait_ge(y_stored[u], DMA * (BLOCKS // 2 + 1))

            @block.scalar
            def _(act):
                for q in (gelu_done, hT_sb1):
                    q.prime(act)

                def tile(g, u, i, more):
                    for n in (0, 1):
                        wait(act, h_ps, g, n + 1)
                        wait(act, hT_ps, g - 1, n + 1)
                        act.activation(h[n][:, :], ps_h[:, n, :], ACT.Gelu).then_inc(gelu_done.sem, 1)
                    wait(act, hT_ps, g, 2)
                    wait(act, y_ps, g - 1)
                    act.copy(hT[:, 4:8, :], ps_T[:, 1, :].rearrange("p (f t) -> p f t", f=4)).then_inc(hT_sb1.sem, 1)

                with act.Fori(0, BLOCKS // 2) as i:
                    for u in (0, 1):
                        tile(i * 2 + u, u, i, True)

            @block.vector
            def _(dve):
                for q in (xT_sb, hT_sb0, y_done):
                    q.prime(dve)

                def turned_x(g):
                    wait(dve, xT_ps, g)
                    wait(dve, h_ps, g - 1)
                    dve.tensor_copy(xT[:, :, :], ps_x[:, 0:DIM].rearrange("p (k t) -> p k t", k=KT)).then_inc(xT_sb.sem, 1)

                turned_x(0)

                def tile(g, u, i, more):
                    if more:
                        turned_x(g + 1)
                    wait(dve, hT_ps, g, 1)
                    wait(dve, y_ps, g - 1)
                    dve.tensor_copy(hT[:, 0:4, :], ps_T[:, 0, :].rearrange("p (f t) -> p f t", f=4)).then_inc(hT_sb0.sem, 1)
                    wait(dve, y_ps, g)
                    dve.wait_ge(y_stored[u], (i + 1) * DMA)
                    dve.tensor_copy(y[u][:, :], ps_y[:, u, 0:DIM]).then_inc(y_done.sem, 1)

                tile_pairs(dve, BLOCKS // 2, tile)

            @block.tensor
            def _(pe):
                for q in (xT_ps, h_ps, hT_ps, y_ps):
                    q.prime(pe)
                pe.wait_ge(in_sem, DMA)

                def up(g, u, i, expert):
                    wait(pe, xT_sb, g)
                    for n in (0, 1):
                        wait(pe, gelu_done, g - 1, n + 1)
                        for k in range(KT):
                            cols = bass.ds((expert * KT + k) * FF + n * PSUM_F32, PSUM_F32)
                            mm = pe.matmul(ps_h[:, n, :], xT[:, k, :], w_up[:, cols], start=(k == 0), stop=(k == KT - 1))
                        mm.then_inc(h_ps.sem, 1)

                def turn_x(g, u, i):
                    pe.wait_ge(x_loaded[u], (i + 1) * DMA)
                    wait(pe, xT_sb, g - 1)
                    for k in range(KT):
                        mm = pe.transpose(ps_x[:, k * P:(k + 1) * P], x[u][:, k * P:(k + 1) * P], ident[:, :])
                    mm.then_inc(xT_ps.sem, 1)

                turn_x(0, 0, 0)
                pe.wait_ge(up_loaded, EXPERTS * DMA)
                pe.wait_ge(down_loaded, EXPERTS * DMA)
                e0 = pe.value_load(block_expert[0:1, 0:1], min_val=0, max_val=EXPERTS - 1)
                up(0, 0, 0, e0)

                def tile(g, u, i, more):
                    if more:
                        turn_x(g + 1, 1 - u, i + u)
                    for n in (0, 1):
                        wait(pe, gelu_done, g, n + 1)
                        wait(pe, (hT_sb0, hT_sb1)[n], g - 1)
                        for f in range(4):
                            mm = pe.transpose(ps_T[:, n, f * P:(f + 1) * P], h[n][:, f * P:(f + 1) * P], ident[:, :])
                        mm.then_inc(hT_ps.sem, 1)
                    if more:
                        up(g + 1, 1 - u, i + u,
                           pe.value_load(block_expert[0:1, bass.ds(g + 1, 1)], min_val=0, max_val=EXPERTS - 1))
                    expert = pe.value_load(block_expert[0:1, bass.ds(g, 1)], min_val=0, max_val=EXPERTS - 1)
                    wait(pe, hT_sb0, g)
                    wait(pe, y_done, g - 2)
                    for f in range(FT):
                        if f == 4:
                            wait(pe, hT_sb1, g)
                        mm = pe.matmul(ps_y[:, u, 0:DIM], hT[:, f, :], w_down[:, bass.ds((expert * FT + f) * DIM, DIM)],
                                       start=(f == 0), stop=(f == FT - 1))
                    mm.then_inc(y_ps.sem, 1)

                tile_pairs(pe, BLOCKS // 2, tile)


GATHERS = 4


def combine(nc, expert_rows, x_all, position, weight, x_out):
    with ExitStack() as stack:
        s = Scope(nc, stack, "combine")
        rows = [[s.sbuf(f"rows{r}_{k}", [P, DIM]) for k in range(TOP_K)] for r in range(GATHERS)]
        res = [s.sbuf(f"res{u}", [P, DIM]) for u in (0, 1)]
        stats = s.sbuf("stats", [P, TILES, 6])
        mean_var = s.sbuf("mean_var", [P, TILES, 2])
        var_eps = s.sbuf("var_eps", [P, TILES])
        rstd = s.sbuf("rstd", [P, TILES])
        y = [s.sbuf(f"y{u}", [P, DIM]) for u in (0, 1)]
        gathered = [s.sem(f"gathered{r}") for r in range(GATHERS)]
        y_stored = [s.sem(f"y_stored{u}") for u in (0, 1)]
        added, summed, stats_done, mean_done, eps_done, std_done, rstd_done, y_done = [
            s.sem(n) for n in ("added", "summed", "stats_done", "mean_done", "eps_done", "std_done", "rstd_done", "y_done")]

        with nc.Block() as block:

            @block.gpsimd
            def _(pool):
                for t in range(TILES):
                    if t >= GATHERS:
                        pool.wait_ge(summed, t - GATHERS + 1)
                    for k in range(TOP_K):
                        pool.indirect_dma_start(out=rows[t % GATHERS][k][:, :], out_offset=None, in_=expert_rows,
                                                in_offset=bass.IndirectOffsetOnAxis(ap=position[:, k, t:t + 1], axis=0))\
                            .then_inc(gathered[t % GATHERS], DMA)

            @block.scalar
            def _(act):
                act.wait_ge(eps_done, 1)
                act.activation(rstd[:, :], var_eps[:, :], ACT.Sqrt).then_inc(std_done, 1)

            @block.vector
            def _(dve):
                for t in range(TILES):
                    dve.wait_ge(gathered[t % GATHERS], (t // GATHERS + 1) * TOP_K * DMA)
                    row = x_all[:, t, :]
                    dve.scalar_tensor_tensor(out=row, in0=rows[t % GATHERS][0][:, :], scalar=weight[:, 0, t:t + 1],
                                             in1=row, op0=ALU.mult, op1=ALU.add).then_inc(added, 1)
                    dve.wait_ge(added, t + 1)
                    dve.scalar_tensor_tensor(out=row, in0=rows[t % GATHERS][1][:, :], scalar=weight[:, 1, t:t + 1],
                                             in1=row, op0=ALU.mult, op1=ALU.add).then_inc(summed, 1)
                    dve.wait_ge(summed, t + 1)
                    dve.bn_stats(stats[:, t, :], row).then_inc(stats_done, 1)
                    dve.wait_ge(stats_done, t + 1)
                    dve.bn_aggr(mean_var[:, t, :], stats[:, t, :]).then_inc(mean_done, 1)
                dve.wait_ge(mean_done, TILES)
                dve.tensor_scalar(var_eps[:, :], mean_var[:, :, 1], EPS, None, ALU.add).then_inc(eps_done, 1)
                dve.wait_ge(std_done, 1)
                dve.reciprocal(rstd[:, :], rstd[:, :]).then_inc(rstd_done, 1)
                dve.wait_ge(rstd_done, 1)
                for t in range(TILES):
                    row = x_all[:, t, :]
                    dve.tensor_scalar(row, row, mean_var[:, t, 0:1], rstd[:, t:t + 1], ALU.subtract, ALU.mult)\
                        .then_inc(y_done, 1)

            @block.sync
            def _(sp):
                Q = 4
                for n in range(0, TILES, Q):
                    sp.wait_ge(y_done, n + Q)
                    sp.dma_start(x_out[1 + n * P:1 + (n + Q) * P, :].rearrange("(n p) d -> p n d", p=P), x_all[:, n:n + Q, :])\
                        .then_inc(y_stored[0], DMA)
                sp.wait_ge(y_stored[0], TILES // Q * DMA)


def load_experts(sp, w_up, w_down, up_dram, down_dram, up_loaded, down_loaded):
    for e in range(EXPERTS):
        if w_up is not None:
            sp.dma_start(w_up[:, e * KT * FF:(e + 1) * KT * FF].rearrange("p (k n) -> p k n", k=KT),
                         up_dram[e].rearrange("(k p) n -> p k n", p=P)).then_inc(up_loaded, DMA)
        if w_down is not None:
            sp.dma_start(w_down[:, e * FT * DIM:(e + 1) * FT * DIM].rearrange("p (f n) -> p f n", f=FT),
                         down_dram[e].rearrange("(f p) n -> p f n", p=P)).then_inc(down_loaded, DMA)


def rotary_tables():
    half = np.arange(0, HEAD_DIM, 2, dtype=np.float32)
    inv_freq = (1.0 / 10000.0 ** (half / HEAD_DIM)).astype(np.float32)
    t = np.arange(TOKENS, dtype=np.float32)
    angle = (t[:, None] * inv_freq[None, :]).astype(np.float32).astype(np.float64)
    base = (half + 0.4 * HEAD_DIM) / (1.4 * HEAD_DIM)
    power = (t - TOKENS // 2) / float(P // 2)
    scale = base[None, :].astype(np.float64) ** power[:, None].astype(np.float64)
    cos, sin = np.cos(angle), np.sin(angle)
    out = [np.concatenate([cos * g, cos * g], 1) if n % 2 == 0 else np.concatenate([-sin * g, sin * g], 1)
           for n, g in ((0, scale), (1, scale), (0, 1 / scale), (1, 1 / scale))]
    return np.stack(out, 1).astype(np.float32)


def window_masks():
    q, k = np.arange(P)[:, None], np.arange(P)[None, :]
    now = np.where(k <= q, 0.0, NEG)
    before = np.where(k >= q, 0.0, NEG)
    never = np.full((P, P), NEG)
    return np.stack([np.stack([now, before], 1), np.stack([before, now], 1), np.stack([now, never], 1)], 1)\
        .astype(np.float32)


def swapped_scales(qs, ks):
    swap = lambda a: np.concatenate([a[HEAD_DIM // 2:], a[:HEAD_DIM // 2]])
    return np.stack([qs, swap(qs), ks, swap(ks)])


def columns(a):
    out = np.zeros((-(-a.shape[0] // P), P), a.dtype)
    out.reshape(-1)[:a.shape[0]] = a
    return out.T


def chunk_constants():
    q, k = np.arange(P)[:, None] % CHUNK, np.arange(CHUNK)[None, :]
    causal = np.where(k > q, -65000.0, 0.0).astype(np.float32)
    own = (np.arange(P)[:, None] // C_DIM == np.arange(HH)[None, :]).astype(np.float32)
    every = np.full((P, P), 1.0 / (4 * CHUNK), np.float32)
    second = every * (np.arange(P)[None, :] >= CHUNK)
    pair = np.arange(P)[:, None, None] // CHUNK == np.arange(2)[None, :, None]
    pair = (pair * np.ones((1, 1, C_DIM))).astype(np.float32)
    return causal, np.stack([own, own / CHUNK], 1).astype(np.float32), np.stack([every, second], 1).astype(np.float32), pair


def filter_constants():
    t = np.linspace(0.0, 1.0, FILTER, dtype=np.float32)
    w = (2.0 * np.pi * np.linspace(0.0, FILTER - 1.0, FILTER, dtype=np.float32) / FILTER).astype(np.float32)
    fw = np.float32(1e-4) * w
    features = np.stack([t, np.cos(fw), -np.sin(fw)]).astype(np.float32)
    deltas = np.linspace(np.log(0.01) / 1.5, np.log(0.01) / 0.3, DIM, dtype=np.float32)
    decay = np.exp(-t[None, :] * np.abs(deltas)[:, None]) + np.float32(0.05)
    return features, np.ascontiguousarray(decay.astype(np.float32).reshape(KT, P, FILTER).transpose(1, 0, 2))


def routing_constants():
    before = np.arange(P)[:, None] < np.arange(P)[None, :]
    return (np.stack([before, np.ones((P, P))], 1).astype(np.float32),
            np.tile(np.arange(BLOCKS, dtype=np.float32), (P, 1)))
def clear(nc, sorted_rows, stages):
    with ExitStack() as stack:
        s = Scope(nc, stack, "clear")
        zeros = s.sbuf("zeros", [P, 8, DIM])
        set_, stored = s.sem("set"), s.sem("stored")
        n_blocks = ROWS // (8 * P)
        with nc.Block() as block:

            @block.vector
            def _(dve):
                dve.memset(zeros[:, :, :], 0.0).then_inc(set_, 1)

            @block.sync
            def _(sp):
                sp.wait_ge(set_, 1)
                for n in range(n_blocks):
                    sp.dma_start(sorted_rows[n * 8 * P:(n + 1) * 8 * P, :].rearrange("(n p) d -> p n d", p=P), zeros[:, :, :])\
                        .then_inc(stored, DMA)
                for x in stages:
                    sp.dma_start(x[0:1, :], zeros[0:1, 0, :]).then_inc(stored, DMA)
                sp.wait_ge(stored, DMA * (n_blocks + len(stages)))


def network(nc, a, out):
    dram = lambda name, rows, cols: nc.dram_tensor(name, (rows, cols), F32).ap()
    stage = [dram(f"stage{n}", TOKENS + 1, DIM) for n in range(3)]
    inner = [dram(f"inner{n}", TOKENS + 1, DIM) for n in range(3)]
    taps_by_start = dram("taps_by_start", DIM, STARTS * SPANS)
    sorted_rows, expert_rows = dram("sorted_rows", ROWS, DIM), dram("expert_rows", ROWS, DIM)

    clear(nc, sorted_rows, stage + inner)
    filter_taps(nc, taps_by_start, a["features"], a["f_w1"], a["b1_freq1"], a["f_w2"], a["b2_freq2"], a["f_w3"],
                a["b3_freq3"], a["f_wout"], a["decay"], a["filt_bias"])
    with ExitStack() as stack:
        s = Scope(nc, stack, "first")
        up_loaded, down_loaded = s.sem("up_loaded"), s.sem("down_loaded")
        half = DIM * STEPS
        low, high = s.sbuf("low", [P, half]), s.sbuf("high", [P, half])
        x0_tok = low[:, :].rearrange("p (c n) -> p c n", c=DIM)
        v_tok = high[:, :].rearrange("p (c n) -> p c n", c=DIM)
        x_all = low[:, 0:TILES * DIM].rearrange("p (t d) -> p t d", t=TILES)
        w_down = high[:, :]
        gated_input(nc, a["u"], a["w_in"], a["in_columns"], a["ident"], x0_tok, v_tok)
        w_up = s.sbuf("w_up", [P, EXPERTS * KT * FF])
        long_convolution(nc, taps_by_start, x0_tok, v_tok,
                         lambda queue: load_experts(queue, w_up, None, a["expert_up"], None, up_loaded, None))
        project_and_norm(nc, x0_tok, a["u"], stage[0], a["w_out"], a["b_out"], a["ident"],
                         lambda queue: load_experts(queue, None, w_down, None, a["expert_down"], None, down_loaded))
        position = s.sbuf("position", [P, TOP_K, TILES], U32)
        weight = s.sbuf("weight", [P, TOP_K, TILES])
        block_expert = s.sbuf("block_expert", [1, BLOCKS], I32)
        route(nc, stage[0], x_all, position, weight, block_expert, a["router_w"], a["router_b"], a["ident"],
              a["before"], a["numbers"], sorted_rows, low[:, TILES * DIM:])
        experts(nc, sorted_rows, expert_rows, block_expert, w_up, w_down, up_loaded, down_loaded, a["ident"])
        combine(nc, expert_rows, x_all, position, weight, stage[1])

    chunk_attention(nc, stage[1], stage[2], a["W_qkv"], a["W_out"], a["ident"], a["causal"], a["head_mask"],
                    a["cum_weights"], a["pair_mask"])
    x = stage[2]
    for l in range(2):
        window_attention(nc, l, x, inner[2 * l], a["wqkv"][l], a["qk_scale"][l], a["wo"][l], a["rotary"], a["ident"],
                         a["window_mask"])
        gated_ffn(nc, l, inner[2 * l], inner[1] if l == 0 else out, a["w1"][l], a["b1"][l], a["w2"][l], a["b2"][l],
                  a["ln_g"][l], a["ln_b"][l], a["ident"], None if l == 0 else stage[2])
        x = inner[1]


def kernel(**inputs):
    import concourse.bacc as bacc
    from concourse.bass_utils import run_bass_kernel_spmd

    i = {name: np.asarray(a) for name, a in inputs.items()}
    A, F, G, H = ({n[len(p):]: a for n, a in i.items() if n.startswith(p)} for p in
                  ("L0_attn_", "L0_ffn_", "L1_attn_", "L1_ffn_"))
    features, decay = filter_constants()
    before, numbers = routing_constants()
    causal, head_mask, cum_weights, pair_mask = chunk_constants()
    hid = H["w2"].shape[1]
    two = lambda a, b: np.stack([a, b], 1)
    layers = range(H["wqkv"].shape[0])
    arrays = {
        "ident": np.eye(P), "u": A["u"][0], "w_in": A["w_in"],
        "in_columns": np.stack([columns(A["b_in"])] + [columns(A["sf_w"][:, n]) for n in range(3)] + [columns(A["sf_b"])], 1),
        "features": features, "decay": decay, "f_w1": A["f_w1"], "b1_freq1": two(A["f_b1"], A["freq1"]),
        "f_w2": A["f_w2"], "b2_freq2": two(A["f_b2"], A["freq2"]), "f_w3": A["f_w3"],
        "b3_freq3": two(A["f_b3"], A["freq3"]), "f_wout": A["f_wout"], "filt_bias": columns(A["filt_bias"]),
        "w_out": A["w_out"], "b_out": A["b_out"][None],
        "router_w": F["router_w"], "router_b": F["router_b"][None], "before": before, "numbers": numbers,
        "expert_up": F["expert_up"].transpose(0, 2, 1), "expert_down": F["expert_down"].transpose(0, 2, 1),
        "W_qkv": G["W_qkv"], "W_out": G["W_out"], "causal": causal, "head_mask": head_mask,
        "cum_weights": cum_weights, "pair_mask": pair_mask,
        "rotary": rotary_tables(), "window_mask": window_masks(), "wqkv": H["wqkv"], "wo": H["wo"],
        "qk_scale": np.stack([swapped_scales(H["q_scale"][l], H["k_scale"][l]) for l in layers]),
        "w1": H["w1"], "b1": np.stack([two(columns(H["b1"][l][:hid]), columns(H["b1"][l][hid:])) for l in layers]),
        "w2": H["w2"], "b2": H["b2"], "ln_g": np.stack([columns(H["ln_g"][l]) for l in layers]),
        "ln_b": np.stack([columns(H["ln_b"][l]) for l in layers]),
    }
    arrays = {n: np.ascontiguousarray(a, dtype=np.float32) for n, a in arrays.items()}
    nc = bacc.Bacc("TRN2", target_bir_lowering=False, num_devices=1)
    drams = {n: nc.dram_tensor(n, a.shape, F32, kind="ExternalInput").ap() for n, a in arrays.items()}
    out = nc.dram_tensor("out", (TOKENS, DIM), F32, kind="ExternalOutput").ap()
    network(nc, drams, out)
    got = run_bass_kernel_spmd(nc, [arrays], core_ids=[0])
    return got.results[0]["out"].reshape(1, TOKENS, DIM)
```

```python
from contextlib import ExitStack

import numpy as np

import concourse.bass as bass
import concourse.mybir as mybir

F32 = mybir.dt.float32
I32 = mybir.dt.int32
U32 = mybir.dt.uint32
ALU = mybir.AluOpType
ACT = mybir.ActivationFunctionType
AX_X = mybir.AxisListType.X

P = 128
TOKENS = 4096
DIM = 256
TILES = TOKENS // P
KT = DIM // P
EPS = 1e-5
DMA = 16


class Count:

    def __init__(self, sem, per_tile=1, by=1):
        self.sem = sem
        self.n, self.by = per_tile, by

    def prime(self, engine):
        engine.sem_inc(self.sem, 2 * self.n * self.by)

    def at(self, tile, k=None):
        return ((tile + 2) * self.n + (self.n if k is None else k)) * self.by


def wait(engine, count, tile, k=None):
    engine.wait_ge(count.sem, count.at(tile, k))


class Scope:

    def __init__(self, nc, stack, phase):
        self.nc, self.stack, self.phase, self.sems = nc, stack, phase, []
        stack.callback(self.release)

    def release(self):
        self.nc.clear_and_free_semaphores(self.sems)
        self.nc.all_engine_barrier()

    def sbuf(self, name, shape, dtype=F32):
        return self.stack.enter_context(self.nc.sbuf_tensor(f"{self.phase}_{name}", shape, dtype))

    def psum(self, name, shape, dtype=F32):
        return self.stack.enter_context(self.nc.psum_tensor(f"{self.phase}_{name}", shape, dtype))

    def sem(self, name):
        self.sems.append(self.nc.alloc_semaphore(f"{self.phase}_{name}"))
        return self.sems[-1]

    def count(self, name, per_tile=1, by=1):
        return Count(self.sem(name), per_tile, by)


def tile_pairs(engine, pairs, body):
    for u in (0, 1):
        body(u, u, 0, True)
    with engine.Fori(1, pairs - 1) as i:
        for u in (0, 1):
            body(i * 2 + u, u, i, True)
    for u in (0, 1):
        body(2 * (pairs - 1) + u, u, pairs - 1, u == 0)


def first(tile):
    return isinstance(tile, int) and tile == 0


def last(tile):
    return isinstance(tile, int) and tile == TILES - 1
HEADS = 8
HEAD_DIM = 64
INNER = HEADS * HEAD_DIM
PAIRS = HEADS // 2
NEG = -1e25


def load_window_weights(queue, w_qkv, w_o, wqkv, wo, loaded):
    queue.dma_start(w_qkv[:, :, :], wqkv.rearrange("(k p) n -> p k n", p=P)).then_inc(loaded, DMA)
    queue.dma_start(w_o[:, :, :], wo.rearrange("(k p) n -> p k n", p=P)).then_inc(loaded, DMA)


def window_attention(nc, layer, x_in, x_out, w_qkv, w_o, weights_in, qk_scale, rotary, ident_dram, mask_dram,
                     prefetch=None):
    with ExitStack() as stack:
        s = Scope(nc, stack, f"win{layer}")
        ident = s.sbuf("ident", [P, P])
        mask = s.sbuf("mask", [P, 3, 2, P])
        scales = s.sbuf("scales", [P, 4, HEAD_DIM])
        minus_half = s.sbuf("minus_half", [P, HEADS])
        x = [s.sbuf(f"x{u}", [P, DIM]) for u in (0, 1)]
        x_res = [s.sbuf(f"x_res{u}", [P, DIM]) for u in (0, 1)]
        x_shift = [s.sbuf(f"x_shift{u}", [P, P]) for u in (0, 1)]
        rot = [s.sbuf(f"rot{u}", [P, 4, HEAD_DIM]) for u in (0, 1)]
        rot_s = [s.sbuf(f"rot_s{u}", [P, 4, HEAD_DIM]) for u in (0, 1)]
        hT = s.sbuf("hT", [P, KT, P])
        squares = s.sbuf("squares", [P, 2, INNER])
        norm2 = s.sbuf("norm2", [P, 2, HEADS])
        inv_norm = s.sbuf("inv_norm", [P, 2, HEADS])
        q_gain = [s.sbuf(f"q_gain{u}", [P, HEADS]) for u in (0, 1)]
        by_cos = s.sbuf("by_cos", [P, 2, HEADS, HEAD_DIM])
        by_sin = s.sbuf("by_sin", [P, 2, HEADS, HEAD_DIM])
        turned = s.sbuf("turned", [P, 2, HEADS, HEAD_DIM])
        k_turned = s.sbuf("k_turned", [P, HEADS, HEAD_DIM])
        qT = s.sbuf("qT", [P, PAIRS, P])
        kT = s.sbuf("kT", [P, PAIRS, 2, 2, P])
        v = s.sbuf("v", [P, 2, INNER])
        masked = s.sbuf("masked", [P, 2, 2, 2 * P])
        top = s.sbuf("top", [P, PAIRS, 2])
        bias = s.sbuf("bias", [P, PAIRS, 2])
        probs = s.sbuf("probs", [P, 2, 2, 2 * P])
        spare = s.sbuf("spare", [P, 2])
        total = s.sbuf("total", [P, HEADS])
        inv_total = s.sbuf("inv_total", [P, HEADS])
        pT = s.sbuf("pT", [P, 2, 4, P])
        o = s.sbuf("o", [P, INNER])
        oT = s.sbuf("oT", [P, INNER // P, P])
        y = [s.sbuf(f"y{u}", [P, DIM]) for u in (0, 1)]

        ps_qk = s.psum("ps_qk", [P, 2, INNER])
        ps_v = s.psum("ps_v", [P, INNER])
        ps_T = s.psum("ps_T", [P, 2, 4, P])
        ps_s = s.psum("ps_s", [P, 2, 2, 2 * P])
        ps_o = s.psum("ps_o", [P, INNER])

        ident_in, const_in = s.sem("ident_in"), s.sem("const_in")
        consts_set = s.sem("consts_set")
        x_loaded = [s.sem(f"x_loaded{u}") for u in (0, 1)]
        res_loaded = [s.sem(f"res_loaded{u}") for u in (0, 1)]
        y_stored = [s.sem(f"y_stored{u}") for u in (0, 1)]
        c = lambda name, n=1: s.count(name, n)
        hT_ps, hT_sb, qk_ps, v_ps, v_sb = c("hT_ps"), c("hT_sb"), c("qk_ps", 2), c("v_ps"), c("v_sb")
        rot_ready, squared, normed2 = c("rot_ready"), c("squared", 2), c("normed2")
        norm_floor, norm_inv, gain = c("norm_floor"), c("norm_inv", 2), c("gain")
        cos_done, sin_done, turned_done, k_done = c("cos_done", 2), c("sin_done", 4), c("turned_done", 2), c("k_done")
        qT_ps, kT_ps, qT_sb, kT_sb = c("qT_ps"), c("kT_ps"), c("qT_sb"), c("kT_sb", 2)
        s_ps, s_masked, bias_done = c("s_ps", PAIRS), c("s_masked", HEADS), c("bias_done", PAIRS)
        exp_done, pT_ps, pT_sb, pv_done = c("exp_done", HEADS), c("pT_ps", PAIRS), c("pT_sb", PAIRS), c("pv_done", PAIRS)
        inv_done, o_done, oT_ps, oT_sb = c("inv_done"), c("o_done"), c("oT_ps"), c("oT_sb")
        y_ps, y_done = c("y_ps"), c("y_done")

        with nc.Block() as block:

            @block.sync
            def _(sp):
                sp.dma_start(ident[:, :], ident_dram).then_inc(ident_in, DMA)

                def load(t, u):
                    sp.dma_start(x[u][:, :], x_in[bass.ds(t * P + 1, P), :]).then_inc(x_loaded[u], DMA)
                    sp.dma_start(x_shift[u][:, :], x_in[bass.ds(t * P, P), P:DIM]).then_inc(x_loaded[u], DMA)
                    sp.dma_start(rot[u][:, :, :], rotary[bass.ds(t * P, P), :, :]).then_inc(x_loaded[u], DMA)

                def load_res(t, u):
                    sp.dma_start(x_res[u][:, :], x_in[bass.ds(t * P + 1, P), :]).then_inc(res_loaded[u], DMA)

                for u in (0, 1):
                    sp.sem_inc(y_stored[u], DMA)
                    load(u, u)
                    if u == 0:
                        for n in range(4):
                            sp.dma_start(scales[:, n, :], qk_scale[n:n + 1, :].to_broadcast([P, HEAD_DIM]))\
                                .then_inc(const_in, DMA)
                sp.dma_start(mask[:, :, :, :], mask_dram).then_inc(const_in, DMA)
                for u in (0, 1):
                    load_res(u, u)
                if prefetch:
                    prefetch(sp)

                def store(t, u):
                    wait(sp, y_done, t)
                    sp.dma_start(x_out[bass.ds(t * P + 1, P), :], y[u][:, :]).then_inc(y_stored[u], DMA)

                with sp.Fori(0, TILES // 2 - 1) as i:
                    for u in (0, 1):
                        wait(sp, hT_ps, i * 2 + u)
                        wait(sp, rot_ready, i * 2 + u)
                        load(i * 2 + u + 2, u)
                        store(i * 2 + u, u)
                        load_res(i * 2 + u + 2, u)
                for u in (0, 1):
                    store(TILES - 2 + u, u)
                for u in (0, 1):
                    sp.wait_ge(y_stored[u], DMA * (TILES // 2 + 1))

            @block.gpsimd
            def _(pool):
                for q in (rot_ready, norm_inv):
                    q.prime(pool)
                pool.memset(minus_half[:, :], -0.5).then_inc(consts_set, 1)
                pool.memset(kT[:, :, :, :, :], 0.0).then_inc(consts_set, 1)
                pool.memset(v[:, :, :], 0.0).then_inc(consts_set, 1)
                pool.wait_ge(consts_set, 3)
                pool.wait_ge(const_in, 5 * DMA)
                with pool.Fori(0, TILES // 2) as i:
                    for u in (0, 1):
                        t = i * 2 + u
                        pool.wait_ge(x_loaded[u], (i + 1) * 3 * DMA)
                        wait(pool, sin_done, t - 2)
                        pool.tensor_tensor(rot_s[u][:, :, :], rot[u][:, :, :], scales[:, :, :], ALU.mult)\
                            .then_inc(rot_ready.sem, 1)
                        wait(pool, norm_floor, t)
                        wait(pool, k_done, t - 1)
                        wait(pool, gain, t - 1)
                        for a in (1, 0):
                            pool.tensor_tensor(inv_norm[:, a, :], norm2[:, a, :], minus_half[:, :], ALU.pow)\
                                .then_inc(norm_inv.sem, 1)

            @block.scalar
            def _(act):
                for q in (hT_sb, v_sb, squared, qT_sb, exp_done, pT_sb, oT_sb):
                    q.prime(act)

                def turned_h(t):
                    wait(act, hT_ps, t)
                    wait(act, v_ps, t - 1)
                    act.copy(hT[:, :, :], ps_T[:, 1, 0:KT, :]).then_inc(hT_sb.sem, 1)

                def square(t):
                    wait(act, normed2, t - 1)
                    for a in (0, 1):
                        wait(act, qk_ps, t, a + 1)
                        act.activation(squares[:, a, :], ps_qk[:, a, :], ACT.Square).then_inc(squared.sem, 1)

                def turned_q(t):
                    wait(act, qT_ps, t)
                    wait(act, s_ps, t - 1)
                    act.copy(qT[:, :, :], ps_T[:, 1, :, :]).then_inc(qT_sb.sem, 1)

                def turned_o(t):
                    wait(act, oT_ps, t)
                    wait(act, y_ps, t - 1)
                    act.copy(oT[:, :, :], ps_T[:, 0, :, :]).then_inc(oT_sb.sem, 1)

                def keep_v(t, u):
                    wait(act, v_ps, t)
                    wait(act, pv_done, t - 1)
                    act.copy(v[:, u, :], ps_v[:, :]).then_inc(v_sb.sem, 1)

                def exps(t, u, p):
                    wait(act, bias_done, t, p + 1)
                    if p < 2:
                        wait(act, pT_ps, t - 1, p + 3)
                    else:
                        wait(act, pT_ps, t, p - 1)
                    for j in (0, 1):
                        h = 2 * p + j
                        act.activation(probs[:, p % 2, j, :], masked[:, p % 2, j, :], ACT.Exp,
                                       bias=bias[:, p, j:j + 1], scale=q_gain[u][:, h:h + 1],
                                       accum_out=total[:, h:h + 1]).then_inc(exp_done.sem, 1)

                def pT_copy(t, p):
                    wait(act, pT_ps, t, p + 1)
                    if p < 2:
                        wait(act, pv_done, t - 1, p + 3)
                    else:
                        wait(act, pv_done, t, p - 1)
                    act.copy(pT[:, p % 2, :, :], ps_T[:, int(p == 1), :, :]).then_inc(pT_sb.sem, 1)

                act.wait_ge(consts_set, 3)
                turned_h(0)
                square(0)
                turned_q(0)
                keep_v(0, 0)

                def tile(t, u, i, more):
                    if not first(t):
                        turned_o(t - 1)
                    wait(act, inv_done, t - 1)
                    exps(t, u, 0)
                    if more:
                        turned_h(t + 1)
                    exps(t, u, 1)
                    pT_copy(t, 0)
                    exps(t, u, 2)
                    if more:
                        square(t + 1)
                    pT_copy(t, 1)
                    exps(t, u, 3)
                    pT_copy(t, 2)
                    if more:
                        turned_q(t + 1)
                    pT_copy(t, 3)
                    if more:
                        keep_v(t + 1, 1 - u)

                tile_pairs(act, TILES // 2, tile)
                turned_o(TILES - 1)

            @block.vector
            def _(dve):
                for q in (normed2, norm_floor, gain, cos_done, sin_done, turned_done, k_done, kT_sb, s_masked, bias_done,
                          inv_done, o_done, y_done):
                    q.prime(dve)
                dve.wait_ge(const_in, 5 * DMA)
                dve.wait_ge(consts_set, 3)

                def rotate(t, u, a):
                    wait(dve, squared, t, a + 1)
                    wait(dve, rot_ready, t)
                    wait(dve, turned_done, t - 1, a + 1)
                    q4 = ps_qk[:, a, :].rearrange("p (h d) -> p h d", h=HEADS)
                    H2 = HEAD_DIM // 2
                    tab = rot_s[u][:, :, :].rearrange("p (a b) d -> p a b d", a=2)
                    dve.tensor_tensor(by_cos[:, a, :, :], q4, tab[:, a, 0:1, :].to_broadcast([P, HEADS, HEAD_DIM]), ALU.mult)\
                        .then_inc(cos_done.sem, 1)
                    for n, (to, of) in enumerate(((0, H2), (H2, 0))):
                        dve.tensor_tensor(by_sin[:, a, :, to:to + H2], q4[:, :, of:of + H2],
                                          tab[:, a, 1:2, to:to + H2].to_broadcast([P, HEADS, H2]), ALU.mult)\
                            .then_inc(sin_done.sem, 1)
                    wait(dve, cos_done, t, a + 1)
                    wait(dve, sin_done, t, 2 * a + 2)
                    if a == 0:
                        wait(dve, qT_ps, t - 1)
                    else:
                        wait(dve, k_done, t - 1)
                    dve.tensor_tensor(turned[:, a, :, :], by_cos[:, a, :, :], by_sin[:, a, :, :], ALU.add)\
                        .then_inc(turned_done.sem, 1)

                def norms(t):
                    wait(dve, squared, t)
                    wait(dve, norm_inv, t - 1)
                    dve.reduce_sum(norm2[:, :, :].rearrange("p a h -> p (a h)"),
                                   squares[:, :, :].rearrange("p a (h d) -> p (a h) d", h=HEADS), axis=AX_X)\
                        .then_inc(normed2.sem, 1)
                    wait(dve, normed2, t)
                    dve.tensor_scalar(norm2[:, :, :], norm2[:, :, :], 1e-24, None, ALU.max).then_inc(norm_floor.sem, 1)

                def normalise_k(t, u):
                    wait(dve, norm_inv, t, 1)
                    wait(dve, turned_done, t)
                    wait(dve, kT_ps, t - 1)
                    dve.tensor_tensor(k_turned[:, :, :], turned[:, 1, :, :],
                                      inv_norm[:, 1, :].unsqueeze(2).to_broadcast([P, HEADS, HEAD_DIM]), ALU.mult)\
                        .then_inc(k_done.sem, 1)
                    wait(dve, norm_inv, t)
                    dve.tensor_scalar(q_gain[u][:, :], inv_norm[:, 0, :], 8.0, None, ALU.mult).then_inc(gain.sem, 1)

                def turned_k(t, u):
                    wait(dve, kT_ps, t)
                    wait(dve, s_ps, t - 1)
                    for j in (0, 1):
                        half = slice(j * HEAD_DIM, (j + 1) * HEAD_DIM)
                        dve.tensor_copy(kT[half, :, j, u, :], ps_T[half, 1, :, :]).then_inc(kT_sb.sem, 1)

                def mask_pair(t, u, i, p, which):
                    wait(dve, s_ps, t, p + 1)
                    if p < 2:
                        wait(dve, exp_done, t - 1, 2 * p + 6)
                    else:
                        wait(dve, exp_done, t, 2 * p - 2)
                    dve.memset(spare[:, :], 0.0)
                    for j in (0, 1):
                        dve.tensor_tensor_reduce(out=masked[:, p % 2, j, :], in0=ps_s[:, p % 2, j, :],
                                                 in1=mask[:, which, :, :].rearrange("p a k -> p (a k)"),
                                                 scale=1.0, scalar=-3e38, op0=ALU.add, op1=ALU.max,
                                                 accum_out=top[:, p, j:j + 1]).then_inc(s_masked.sem, 1)
                    wait(dve, s_masked, t, 2 * p + 2)
                    wait(dve, gain, t)
                    dve.scalar_tensor_tensor(out=bias[:, p, :], in0=top[:, p, :], scalar=-1.0,
                                             in1=q_gain[u][:, 2 * p:2 * p + 2], op0=ALU.mult, op1=ALU.mult)\
                        .then_inc(bias_done.sem, 1)

                def add_residual(t, u, pair):
                    wait(dve, y_ps, t)
                    dve.wait_ge(y_stored[u], (pair + 1) * DMA)
                    dve.wait_ge(res_loaded[u], (pair + 1) * DMA)
                    dve.tensor_tensor(y[u][:, :], ps_v[:, 0:DIM], x_res[u][:, :], ALU.add).then_inc(y_done.sem, 1)

                rotate(0, 0, 0)
                norms(0)
                rotate(0, 0, 1)
                normalise_k(0, 0)
                turned_k(0, 0)

                def tile(t, u, i, more):
                    which = 2 if first(t) else u
                    mask_pair(t, u, i, 0, which)
                    mask_pair(t, u, i, 1, which)
                    mask_pair(t, u, i, 2, which)
                    if not first(t):
                        add_residual(t - 1, 1 - u, i + u - 1)
                    mask_pair(t, u, i, 3, which)
                    if more:
                        rotate(t + 1, 1 - u, 0)
                    if more:
                        norms(t + 1)
                    if more:
                        rotate(t + 1, 1 - u, 1)
                    if more:
                        normalise_k(t + 1, 1 - u)
                    wait(dve, exp_done, t)
                    dve.reciprocal(inv_total[:, :], total[:, :]).then_inc(inv_done.sem, 1)
                    if more:
                        turned_k(t + 1, 1 - u)
                    wait(dve, inv_done, t)
                    wait(dve, pv_done, t)
                    wait(dve, oT_ps, t - 1)
                    dve.tensor_tensor(o[:, :].rearrange("p (h d) -> p h d", h=HEADS),
                                      ps_o[:, :].rearrange("p (h d) -> p h d", h=HEADS),
                                      inv_total[:, :].unsqueeze(2).to_broadcast([P, HEADS, HEAD_DIM]), ALU.mult)\
                        .then_inc(o_done.sem, 1)

                tile_pairs(dve, TILES // 2, tile)
                add_residual(TILES - 1, 1, TILES // 2 - 1)

            @block.tensor
            def _(pe):
                for q in (hT_ps, qk_ps, v_ps, qT_ps, kT_ps, s_ps, pT_ps, pv_done, oT_ps, y_ps):
                    q.prime(pe)
                pe.wait_ge(ident_in, DMA)

                def turn_x(t, u, i):
                    pe.wait_ge(x_loaded[u], (i + 1) * 3 * DMA)
                    wait(pe, kT_sb, t - 1)
                    pe.transpose(ps_T[:, 1, 0, :], x[u][:, 0:P], ident[:, :])
                    pe.transpose(ps_T[:, 1, 1, :], x_shift[u][:, :], ident[:, :]).then_inc(hT_ps.sem, 1)

                def project_qk(t):
                    wait(pe, hT_sb, t)
                    for a in (0, 1):
                        wait(pe, squared, t - 1, a + 1)
                        wait(pe, sin_done, t - 1, 2 * a + 2)
                        for k in range(KT):
                            mm = pe.matmul(ps_qk[:, a, :], hT[:, k, :], w_qkv[:, k, a * INNER:(a + 1) * INNER],
                                           start=(k == 0), stop=(k == KT - 1))
                        mm.then_inc(qk_ps.sem, 1)

                def project_v(t):
                    wait(pe, y_done, t - 2)
                    for k in range(KT):
                        mm = pe.matmul(ps_v[:, :], hT[:, k, :], w_qkv[:, k, 2 * INNER:3 * INNER],
                                       start=(k == 0), stop=(k == KT - 1))
                    mm.then_inc(v_ps.sem, 1)

                def turn_q(t):
                    wait(pe, turned_done, t, 1)
                    if not first(t):
                        wait(pe, pT_sb, t - 1, 2)
                    else:
                        wait(pe, hT_sb, t)
                    for n in range(PAIRS):
                        mm = pe.transpose(ps_T[:, 1, n, :],
                                          turned[:, 0, 2 * n:2 * n + 2, :].rearrange("p h d -> p (h d)"), ident[:, :])
                    mm.then_inc(qT_ps.sem, 1)

                def turn_k(t):
                    wait(pe, k_done, t)
                    wait(pe, qT_sb, t)
                    for n in range(PAIRS):
                        mm = pe.transpose(ps_T[:, 1, n, :],
                                          k_turned[:, 2 * n:2 * n + 2, :].rearrange("p h d -> p (h d)"), ident[:, :])
                    mm.then_inc(kT_ps.sem, 1)

                def turn_o(t):
                    wait(pe, o_done, t)
                    wait(pe, pT_sb, t)
                    for n in range(INNER // P):
                        mm = pe.transpose(ps_T[:, 0, n, :], o[:, n * P:(n + 1) * P], ident[:, :])
                    mm.then_inc(oT_ps.sem, 1)

                def project_out(t):
                    wait(pe, oT_sb, t)
                    if not last(t):
                        wait(pe, v_sb, t + 1)
                    for n in range(INNER // P):
                        mm = pe.matmul(ps_v[:, 0:DIM], oT[:, n, :], w_o[:, n, :],
                                       start=(n == 0), stop=(n == INNER // P - 1))
                    mm.then_inc(y_ps.sem, 1)

                def scores(t, p):
                    if p < 2:
                        wait(pe, s_masked, t - 1, 2 * p + 6)
                    else:
                        wait(pe, s_masked, t, 2 * p - 2)
                    pe.matmul(ps_s[:, p % 2, :, :].rearrange("q j k -> q (j k)"), qT[:, p, :],
                              kT[:, p, :, :, :].rearrange("d j a k -> d (j a k)"), start=True, stop=True)\
                        .then_inc(s_ps.sem, 1)

                def pT_pair(t, p, more):
                    wait(pe, exp_done, t, 2 * p + 2)
                    if p == 0:
                        wait(pe, oT_sb, t - 1)
                    elif p == 1:
                        if more:
                            wait(pe, hT_sb, t + 1)
                        else:
                            wait(pe, kT_sb, t)
                    else:
                        wait(pe, pT_sb, t, (1, 3)[p - 2])
                    for n in range(4):
                        mm = pe.transpose(ps_T[:, int(p == 1), n, :], probs[:, p % 2, n // 2, (n % 2) * P:(n % 2 + 1) * P],
                                          ident[:, :])
                    mm.then_inc(pT_ps.sem, 1)

                def values(t, p):
                    wait(pe, pT_sb, t, p + 1)
                    if p == 0:
                        wait(pe, v_sb, t)
                        wait(pe, o_done, t - 1)
                    for j in (0, 1):
                        h = 2 * p + j
                        cols = slice(h * HEAD_DIM, (h + 1) * HEAD_DIM)
                        for a in (0, 1):
                            mm = pe.matmul(ps_o[:, cols], pT[:, p % 2, 2 * j + a, :], v[:, a, cols],
                                           start=(a == 0), stop=(a == 1))
                    mm.then_inc(pv_done.sem, 1)

                pe.wait_ge(consts_set, 3)
                turn_x(0, 0, 0)
                pe.wait_ge(weights_in, 2 * (layer + 1) * DMA)
                project_qk(0)
                project_v(0)
                turn_q(0)
                turn_k(0)

                def tile(t, u, i, more):
                    wait(pe, qT_sb, t)
                    wait(pe, kT_sb, t)
                    scores(t, 0)
                    scores(t, 1)
                    if not first(t):
                        turn_o(t - 1)
                    scores(t, 2)
                    if more:
                        turn_x(t + 1, 1 - u, i + u)
                    if not first(t):
                        project_out(t - 1)
                    pT_pair(t, 0, more)
                    scores(t, 3)
                    if more:
                        project_qk(t + 1)
                    pT_pair(t, 1, more)
                    values(t, 0)
                    pT_pair(t, 2, more)
                    values(t, 1)
                    if more:
                        project_v(t + 1)
                    if more:
                        turn_q(t + 1)
                    pT_pair(t, 3, more)
                    if more:
                        turn_k(t + 1)
                    values(t, 2)
                    values(t, 3)

                tile_pairs(pe, TILES // 2, tile)
                turn_o(TILES - 1)
                project_out(TILES - 1)
HIDDEN = DIM * 4 * 2 // 3
HT = -(-HIDDEN // P)
GROUP = 4
GT = GROUP * P
GROUPS = TOKENS // GT
PSUM_F32 = 512


def load_ffn_weights(queue, w_up, w_down, w1, w2, loaded):
    whole = (HT - 1) * P
    queue.dma_start(w_up[:, :, :], w1.rearrange("(k p) n -> p k n", p=P)).then_inc(loaded, DMA)
    queue.dma_start(w_down[:, 0:HT - 1, :], w2[0:whole, :].rearrange("(f p) d -> p f d", p=P)).then_inc(loaded, DMA)
    queue.dma_start(w_down[0:HIDDEN - whole, HT - 1, :], w2[whole:HIDDEN, :]).then_inc(loaded, DMA)


def gated_ffn(nc, layer, x_in, x_out, w_up, w_down, weights_in, b1, b2, ln_gain, ln_bias, ident_dram, x_block=None,
              prefetch=None):
    final = x_block is not None
    loads = 3 if final else 2
    with ExitStack() as stack:
        s = Scope(nc, stack, f"ffn{layer}")
        ident = s.sbuf("ident", [P, P])
        bias_up = s.sbuf("bias_up", [P, 2, HT])
        bias_down = s.sbuf("bias_down", [P, DIM])
        gain = s.sbuf("gain", [P, KT])
        offset = s.sbuf("offset", [P, KT])
        minus_half = s.sbuf("minus_half", [P, GROUP])
        x = [s.sbuf(f"x{u}", [P, GROUP, DIM]) for u in (0, 1)]
        x_shift = [s.sbuf(f"x_shift{u}", [P, GROUP, P]) for u in (0, 1)]
        x_outer = [s.sbuf(f"x_outer{u}", [P, GROUP, DIM]) for u in (0, 1)] if final else None
        spare = s.sbuf("spare", [P, 2])
        stats = s.sbuf("stats", [P, GROUP, 2, 6])
        mean_var = s.sbuf("mean_var", [P, GROUP, 2])
        var_eps = s.sbuf("var_eps", [P, GROUP])
        rstd = s.sbuf("rstd", [P, GROUP])
        normed = s.sbuf("normed", [P, GROUP, DIM])
        hT = s.sbuf("hT", [P, KT, GT])
        act_g = s.sbuf("act_g", [P, 2, GT])
        hidden = s.sbuf("hidden", [P, HT, GT])
        y = [s.sbuf(f"y{u}", [P, GROUP, DIM]) for u in (0, 1)]
        y_stats = s.sbuf("y_stats", [P, GROUP, 6])
        y_mean_var = s.sbuf("y_mean_var", [P, GROUP, 2])
        y_var_eps = s.sbuf("y_var_eps", [P, GROUP])
        y_rstd = s.sbuf("y_rstd", [P, GROUP])

        ps_T = s.psum("ps_T", [P, KT, GT])
        ps_a = s.psum("ps_a", [P, 2, GT])
        ps_g = s.psum("ps_g", [P, 2, GT])
        ps_y = s.psum("ps_y", [P, 2, PSUM_F32])

        const_in = s.sem("const_in")
        consts_set = s.sem("consts_set")
        x_loaded = [s.sem(f"x_loaded{u}") for u in (0, 1)]
        y_stored = [s.sem(f"y_stored{u}") for u in (0, 1)]
        c = lambda name, n=1: s.count(name, n)
        stats_done, mean_done, eps_done, rstd_done = c("stats_done", 2 * GROUP), c("mean_done", GROUP), c("eps_done"), c("rstd_done")
        normed_done, hT_ps, hT_sb = c("normed_done", 2 * GROUP), c("hT_ps"), c("hT_sb", KT)
        up_ps, gelu_done, hidden_done = c("up_ps", HT), c("gelu_done", HT), c("hidden_done", HT)
        down_ps, y_done, x_biased = c("down_ps", 2), c("y_done", 2), c("x_biased", 2 if final else 1)
        y_stats_done, y_mean_done, y_eps_done = c("y_stats_done", GROUP), c("y_mean_done", GROUP), c("y_eps_done")
        y_rstd_done, y_normed = c("y_rstd_done"), c("y_normed", GROUP)

        def rows(f):
            return min(P, HIDDEN - f * P)

        with nc.Block() as block:

            @block.sync
            def _(sp):
                def load(g, u):
                    sp.dma_start(x[u][:, :, :], x_in[bass.ds(g * GT + 1, GT), :].rearrange("(n p) d -> p n d", p=P))\
                        .then_inc(x_loaded[u], DMA)
                    sp.dma_start(x_shift[u][:, :, :],
                                 x_in[bass.ds(g * GT, GT), P:DIM].rearrange("(n p) d -> p n d", p=P))\
                        .then_inc(x_loaded[u], DMA)
                    if final:
                        sp.dma_start(x_outer[u][:, :, :], x_block[bass.ds(g * GT + 1, GT), :].rearrange("(n p) d -> p n d", p=P))\
                            .then_inc(x_loaded[u], DMA)

                for u in (0, 1):
                    sp.sem_inc(y_stored[u], DMA)
                    load(u, u)
                sp.dma_start(ident[:, :], ident_dram).then_inc(const_in, DMA)
                sp.dma_start(gain[:, :], ln_gain).then_inc(const_in, DMA)
                sp.dma_start(offset[:, :], ln_bias).then_inc(const_in, DMA)
                sp.dma_start(bias_up[:, :, :], b1).then_inc(const_in, DMA)
                sp.dma_start(bias_down[:, :], b2.rearrange("(o d) -> o d", o=1).to_broadcast([P, DIM])).then_inc(const_in, DMA)
                if prefetch:
                    prefetch(sp)

                def store(g, u):
                    if final:
                        wait(sp, y_normed, g)
                        out = x_out[bass.ds(g * GT, GT), :]
                    else:
                        wait(sp, y_done, g)
                        out = x_out[bass.ds(g * GT + 1, GT), :]
                    sp.dma_start(out.rearrange("(n p) d -> p n d", p=P), y[u][:, :, :]).then_inc(y_stored[u], DMA)

                with sp.Fori(0, GROUPS // 2 - 1) as i:
                    for u in (0, 1):
                        if final:
                            wait(sp, y_done, i * 2 + u)
                            load(i * 2 + u + 2, u)
                            store(i * 2 + u, u)
                        else:
                            store(i * 2 + u, u)
                            load(i * 2 + u + 2, u)
                for u in (0, 1):
                    store(GROUPS - 2 + u, u)
                for u in (0, 1):
                    sp.wait_ge(y_stored[u], DMA * (GROUPS // 2 + 1))

            @block.gpsimd
            def _(pool):
                for q in (rstd_done, x_biased) + ((y_rstd_done,) if final else ()):
                    q.prime(pool)
                pool.memset(minus_half[:, :], -0.5).then_inc(consts_set, 1)
                pool.wait_ge(consts_set, 1)
                pool.wait_ge(const_in, 5 * DMA)

                def whole_block_rstd(g):
                    wait(pool, y_eps_done, g)
                    wait(pool, y_normed, g - 1)
                    pool.tensor_tensor(y_rstd[:, :], y_var_eps[:, :], minus_half[:, :], ALU.pow)\
                        .then_inc(y_rstd_done.sem, 1)

                def group_rstd(g):
                    wait(pool, eps_done, g)
                    wait(pool, normed_done, g - 1)
                    pool.tensor_tensor(rstd[:, :], var_eps[:, :], minus_half[:, :], ALU.pow)\
                        .then_inc(rstd_done.sem, 1)

                group_rstd(0)

                def group(g, u, i, more):
                    wait(pool, normed_done, g)
                    pool.tensor_tensor(x[u][:, :, :], x[u][:, :, :],
                                       bias_down[:, :].unsqueeze(1).to_broadcast([P, GROUP, DIM]), ALU.add)\
                        .then_inc(x_biased.sem, 1)
                    if final:
                        wait(pool, x_biased, g, 1)
                        pool.tensor_tensor(x[u][:, :, :], x[u][:, :, :], x_outer[u][:, :, :], ALU.add)\
                            .then_inc(x_biased.sem, 1)
                    if more:
                        group_rstd(g + 1)
                    if final and not first(g):
                        whole_block_rstd(g - 1)

                tile_pairs(pool, GROUPS // 2, group)
                if final:
                    whole_block_rstd(GROUPS - 1)

            @block.scalar
            def _(act):
                for q in (hT_sb, gelu_done):
                    q.prime(act)
                act.wait_ge(const_in, 5 * DMA)

                def norm_affine(g):
                    wait(act, hT_ps, g)
                    wait(act, up_ps, g - 1)
                    for k in range(KT):
                        act.activation(hT[:, k, :], ps_T[:, k, :], ACT.Identity,
                                       bias=offset[:, k:k + 1], scale=gain[:, k:k + 1]).then_inc(hT_sb.sem, 1)

                norm_affine(0)

                def group(g, u, i, more):
                    for f in range(HT):
                        n = rows(f)
                        wait(act, up_ps, g, f + 1)
                        if f < 2:
                            wait(act, hidden_done, g - 1, f + HT - 1)
                        else:
                            wait(act, hidden_done, g, f - 1)
                        act.activation(act_g[0:n, f % 2, :], ps_g[0:n, f % 2, :], ACT.Gelu,
                                       bias=bias_up[0:n, 1, f:f + 1]).then_inc(gelu_done.sem, 1)
                    if more:
                        norm_affine(g + 1)

                tile_pairs(act, GROUPS // 2, group)

            @block.vector
            def _(dve):
                for q in (stats_done, mean_done, eps_done, normed_done, hidden_done, y_done) + \
                        ((y_stats_done, y_mean_done, y_eps_done, y_normed) if final else ()):
                    q.prime(dve)

                def statistics(g, u, i):
                    dve.wait_ge(x_loaded[u], (i + 1) * loads * DMA)
                    wait(dve, mean_done, g - 1)
                    for n in range(GROUP):
                        dve.bn_stats(stats[:, n, 0, :], x[u][:, n, 0:P]).then_inc(stats_done.sem, 1)
                        dve.bn_stats(stats[:, n, 1, :], x_shift[u][:, n, :]).then_inc(stats_done.sem, 1)
                    wait(dve, stats_done, g)
                    wait(dve, normed_done, g - 1)
                    dve.memset(spare[:, :], 0.0)
                    for n in range(GROUP):
                        dve.bn_aggr(mean_var[:, n, :], stats[:, n, :, :].rearrange("p a b -> p (a b)"))\
                            .then_inc(mean_done.sem, 1)
                    wait(dve, mean_done, g)
                    wait(dve, rstd_done, g - 1)
                    dve.tensor_scalar(var_eps[:, :], mean_var[:, :, 1], EPS, None, ALU.add).then_inc(eps_done.sem, 1)

                def normalise(g, u):
                    wait(dve, rstd_done, g)
                    wait(dve, hT_ps, g - 1)
                    for n in range(GROUP):
                        for k, src in ((0, x[u][:, n, 0:P]), (1, x_shift[u][:, n, :])):
                            dve.tensor_scalar(normed[:, n, k * P:(k + 1) * P], src, mean_var[:, n, 0:1], rstd[:, n:n + 1],
                                              ALU.subtract, ALU.mult).then_inc(normed_done.sem, 1)

                statistics(0, 0, 0)
                normalise(0, 0)

                def y_statistics(g, u):
                    wait(dve, y_done, g)
                    wait(dve, y_mean_done, g - 1)
                    for n in range(GROUP):
                        dve.bn_stats(y_stats[:, n, :], y[u][:, n, :]).then_inc(y_stats_done.sem, 1)
                    wait(dve, y_stats_done, g)
                    wait(dve, y_normed, g - 1)
                    dve.memset(spare[:, :], 0.0)
                    for n in range(GROUP):
                        dve.bn_aggr(y_mean_var[:, n, :], y_stats[:, n, :]).then_inc(y_mean_done.sem, 1)
                    wait(dve, y_mean_done, g)
                    wait(dve, y_rstd_done, g - 1)
                    dve.tensor_scalar(y_var_eps[:, :], y_mean_var[:, :, 1], EPS, None, ALU.add)\
                        .then_inc(y_eps_done.sem, 1)

                def y_normalise(g, u):
                    wait(dve, y_rstd_done, g)
                    for n in range(GROUP):
                        dve.tensor_scalar(y[u][:, n, :], y[u][:, n, :], y_mean_var[:, n, 0:1], y_rstd[:, n:n + 1],
                                          ALU.subtract, ALU.mult).then_inc(y_normed.sem, 1)

                def group(g, u, i, more):
                    for f in range(HT):
                        n = rows(f)
                        wait(dve, gelu_done, g, f + 1)
                        wait(dve, down_ps, g - 1)
                        dve.scalar_tensor_tensor(out=hidden[0:n, f, :], in0=ps_a[0:n, f % 2, :],
                                                 scalar=bias_up[0:n, 0, f:f + 1], in1=act_g[0:n, f % 2, :],
                                                 op0=ALU.add, op1=ALU.mult).then_inc(hidden_done.sem, 1)
                        if f == 1 and final and not first(g):
                            y_statistics(g - 1, 1 - u)
                        if f == 2 and more:
                            statistics(g + 1, 1 - u, i + u)
                        if f == 3 and final and not first(g):
                            y_normalise(g - 1, 1 - u)
                        if f == 4 and more:
                            normalise(g + 1, 1 - u)
                    wait(dve, x_biased, g)
                    dve.wait_ge(y_stored[u], (i + 1) * DMA)
                    for b in (0, 1):
                        wait(dve, down_ps, g, b + 1)
                        dve.tensor_tensor(y[u][:, 2 * b:2 * b + 2, :],
                                          ps_y[:, b, :].rearrange("p (n d) -> p n d", n=2),
                                          x[u][:, 2 * b:2 * b + 2, :], ALU.add).then_inc(y_done.sem, 1)

                tile_pairs(dve, GROUPS // 2, group)
                if final:
                    y_statistics(GROUPS - 1, 1)
                    y_normalise(GROUPS - 1, 1)

            @block.tensor
            def _(pe):
                for q in (hT_ps, up_ps, down_ps):
                    q.prime(pe)
                pe.wait_ge(const_in, 5 * DMA)

                def transposed(g):
                    wait(pe, normed_done, g)
                    wait(pe, hT_sb, g - 1)
                    for k in range(KT):
                        for n in range(GROUP):
                            mm = pe.transpose(ps_T[:, k, n * P:(n + 1) * P], normed[:, n, k * P:(k + 1) * P], ident[:, :])
                    mm.then_inc(hT_ps.sem, 1)

                transposed(0)
                pe.wait_ge(weights_in, 3 * (layer + 1) * DMA)

                def group(g, u, i, more):
                    wait(pe, hT_sb, g)
                    for f in range(HT):
                        n = rows(f)
                        if f < 2:
                            wait(pe, hidden_done, g - 1, f + HT - 1)
                        else:
                            wait(pe, hidden_done, g, f - 1)
                        for a, bank in ((1, ps_g), (0, ps_a)):
                            for k in range(KT):
                                mm = pe.matmul(bank[0:n, f % 2, :], w_up[:, k, a * HIDDEN + f * P:a * HIDDEN + f * P + n],
                                               hT[:, k, :], start=(k == 0), stop=(k == KT - 1))
                        mm.then_inc(up_ps.sem, 1)
                    if more:
                        transposed(g + 1)
                    for b in (0, 1):
                        wait(pe, y_done, g - 1, b + 1)
                        for n in (2 * b, 2 * b + 1):
                            for f in range(HT):
                                wait(pe, hidden_done, g, f + 1)
                                mm = pe.matmul(ps_y[:, b, (n % 2) * DIM:(n % 2 + 1) * DIM],
                                               hidden[0:rows(f), f, n * P:(n + 1) * P], w_down[0:rows(f), f, :],
                                               start=(f == 0), stop=(f == HT - 1))
                        mm.then_inc(down_ps.sem, 1)

                tile_pairs(pe, GROUPS // 2, group)
C_HEADS = 16
C_DIM = 16
CHUNK = 64
CH = P // CHUNK
HH = P // C_DIM
C_SCALE = C_DIM ** -0.5


def chunk_attention(nc, x_in, x_out, w_qkv_dram, w_out_dram, ident_dram, causal_dram, head_mask_dram, cum_dram,
                    pair_dram, prefetch=None):
    with ExitStack() as stack:
        s = Scope(nc, stack, "chunk")
        w_qkv = s.sbuf("w_qkv", [P, KT, 3 * DIM])
        w_out = s.sbuf("w_out", [P, KT, DIM])
        ident = s.sbuf("ident", [P, P])
        causal = s.sbuf("causal", [P, CHUNK])
        head_mask = s.sbuf("head_mask", [P, 2, HH])
        cum_w = s.sbuf("cum_w", [P, 2, P])
        pair_mask = s.sbuf("pair_mask", [P, 2, C_DIM])
        zero = s.sbuf("zero", [P, KT])
        minus_half = s.sbuf("minus_half", [P, 1])
        x = [s.sbuf(f"x{u}", [P, DIM]) for u in (0, 1)]
        x_res = [s.sbuf(f"x_res{u}", [P, DIM]) for u in (0, 1)]
        xT = s.sbuf("xT", [P, KT, P])
        xT_twice = s.sbuf("xT_twice", [P, KT, CH, 2, CHUNK])
        qT = s.sbuf("qT", [P, KT, P])
        kx = s.sbuf("kx", [P, KT, CH, HH, CHUNK])
        k_sum = s.sbuf("k_sum", [P, KT, CH])
        k_cum = s.sbuf("k_cum", [P, CH + 1, KT])
        k_mean = s.sbuf("k_mean", [P, KT, CH, HH])
        v = [s.sbuf(f"v{u}", [P, CH, DIM]) for u in (0, 1)]
        v_pairs = [s.sbuf(f"v_pairs{u}", [P, CH, HH, 2, C_DIM]) for u in (0, 1)]
        v_sum = [s.sbuf(f"v_sum{u}", [P, DIM]) for u in (0, 1)]
        v_add = s.sbuf("v_add", [P, DIM])
        scores = s.sbuf("scores", [P, C_HEADS, CHUNK])
        top = s.sbuf("top", [P, C_HEADS])
        probs = s.sbuf("probs", [P, C_HEADS, CHUNK])
        total = s.sbuf("total", [P, C_HEADS])
        inv_total = s.sbuf("inv_total", [P, C_HEADS])
        cross_e = s.sbuf("cross_e", [P, C_HEADS])
        cross_d = s.sbuf("cross_d", [P, C_HEADS])
        cross = s.sbuf("cross", [P, C_HEADS])
        pT = s.sbuf("pT", [P, HH, P])
        o_local = s.sbuf("o_local", [P, DIM])
        o_cross = s.sbuf("o_cross", [P, DIM])
        o = s.sbuf("o", [P, DIM])
        oT = s.sbuf("oT", [P, KT, P])
        res = s.sbuf("res", [P, DIM])
        stats = s.sbuf("stats", [P, 6])
        mean_var = s.sbuf("mean_var", [P, 2])
        var_eps = s.sbuf("var_eps", [P, 1])
        rstd = s.sbuf("rstd", [P, 1])
        spare = s.sbuf("spare", [P, 2])
        y = [s.sbuf(f"y{u}", [P, DIM]) for u in (0, 1)]

        ps_T = s.psum("ps_T", [P, 2, 4, P])
        ps_f = s.psum("ps_f", [P, 4, P])
        ps_v = s.psum("ps_v", [P, CH, DIM])
        ps_s = s.psum("ps_s", [P, KT, HH, CHUNK])
        ps_c = s.psum("ps_c", [P, PSUM_F32])
        ps_o = s.psum("ps_o", [P, PSUM_F32])

        in_sem = s.sem("const_in")
        consts_set = s.sem("consts_set")
        x_loaded = [s.sem(f"x_loaded{u}") for u in (0, 1)]
        res_loaded = [s.sem(f"res_loaded{u}") for u in (0, 1)]
        y_stored = [s.sem(f"y_stored{u}") for u in (0, 1)]
        c = lambda name, n=1: s.count(name, n)
        xT_ps, xT_sb, qk_ps, qT_sb, v_ps, v_sb = c("xT_ps"), c("xT_sb", 2), c("qk_ps"), c("qT_sb"), c("v_ps"), c("v_sb")
        kx_done, ksum_done, kcum_done, kmean_done = c("kx_done", KT), c("ksum_done"), c("kcum_done", 3), c("kmean_done")
        pairs_done, vadd_done, vsum_done = c("pairs_done"), c("vadd_done"), c("vsum_done")
        s_ps, z_ps, added, max_done, shifted = c("s_ps"), c("z_ps"), c("added"), c("max_done"), c("shifted")
        exp_done, cross_exp, sum_done, inv_done = c("exp_done"), c("cross_exp"), c("sum_done"), c("inv_done")
        cross_plus, cross_done = c("cross_plus"), c("cross_done")
        pT_ps, pT_sb, pv_ps, cumv_ps = c("pT_ps", 2), c("pT_sb", 2), c("pv_ps"), c("cumv_ps")
        local_done, crossed, o_done, oT_ps, oT_sb = c("local_done"), c("crossed"), c("o_done"), c("oT_ps"), c("oT_sb")
        y_ps, res_done, stats_done, mean_done = c("y_ps"), c("res_done"), c("stats_done"), c("mean_done")
        eps_done, rstd_done, y_done = c("eps_done"), c("rstd_done"), c("y_done")

        with nc.Block() as block:

            @block.sync
            def _(sp):
                def load(t, u):
                    sp.dma_start(x[u][:, :], x_in[bass.ds(t * P + 1, P), :]).then_inc(x_loaded[u], DMA)

                def load_res(t, u):
                    sp.dma_start(x_res[u][:, :], x_in[bass.ds(t * P + 1, P), :]).then_inc(res_loaded[u], DMA)

                for u in (0, 1):
                    sp.sem_inc(y_stored[u], DMA)
                    load(u, u)
                for dst, src in ((ident[:, :], ident_dram), (causal[:, :], causal_dram),
                                 (head_mask[:, :, :], head_mask_dram), (cum_w[:, :, :], cum_dram), (pair_mask[:, :, :], pair_dram),
                                 (w_qkv[:, :, :], w_qkv_dram.rearrange("(k p) n -> p k n", p=P)),
                                 (w_out[:, :, :], w_out_dram.rearrange("(k p) n -> p k n", p=P))):
                    sp.dma_start(dst, src).then_inc(in_sem, DMA)

                for u in (0, 1):
                    load_res(u, u)
                if prefetch:
                    prefetch(sp)

                def store(t, u):
                    wait(sp, y_done, t)
                    sp.dma_start(x_out[bass.ds(t * P + 1, P), :], y[u][:, :]).then_inc(y_stored[u], DMA)

                with sp.Fori(0, TILES // 2 - 1) as i:
                    for u in (0, 1):
                        wait(sp, xT_ps, i * 2 + u)
                        load(i * 2 + u + 2, u)
                        store(i * 2 + u, u)
                        load_res(i * 2 + u + 2, u)
                for u in (0, 1):
                    store(TILES - 2 + u, u)
                for u in (0, 1):
                    sp.wait_ge(y_stored[u], DMA * (TILES // 2 + 1))

            @block.gpsimd
            def _(pool):
                for q in (kcum_done, kmean_done, pairs_done, vadd_done, vsum_done, rstd_done):
                    q.prime(pool)
                pool.memset(minus_half[:, :], -0.5).then_inc(consts_set, 1)
                pool.memset(k_cum[:, :, :], 0.0).then_inc(consts_set, 1)
                pool.memset(zero[:, :], 0.0).then_inc(consts_set, 1)
                for u in (0, 1):
                    pool.memset(v_sum[u][:, :], 0.0).then_inc(consts_set, 1)
                pool.wait_ge(consts_set, 5)
                pool.wait_ge(in_sem, 7 * DMA)

                def running_k(t):
                    wait(pool, kmean_done, t - 1)
                    pool.tensor_tensor(k_cum[:, 0, :], k_cum[:, CH, :], zero[:, :], ALU.add).then_inc(kcum_done.sem, 1)
                    wait(pool, ksum_done, t)
                    wait(pool, kcum_done, t, 1)
                    for n in range(CH):
                        pool.tensor_tensor(k_cum[:, n + 1, :], k_cum[:, n, :], k_sum[:, :, n], ALU.add)\
                            .then_inc(kcum_done.sem, 1)
                        wait(pool, kcum_done, t, n + 2)
                    wait(pool, z_ps, t - 1)
                    pool.tensor_tensor(k_mean[:, :, :, :],
                                       k_cum[:, 0:CH, :].rearrange("p c k -> p k c").unsqueeze(3)
                                       .to_broadcast([P, KT, CH, HH]),
                                       head_mask[:, 1:2, :].unsqueeze(1).to_broadcast([P, KT, CH, HH]), ALU.mult)\
                        .then_inc(kmean_done.sem, 1)

                def running_v(t, u):
                    wait(pool, v_sb, t)
                    wait(pool, pv_ps, t - 2)
                    pool.tensor_tensor(v_pairs[u][:, :, :, :, :].rearrange("p c n j d -> p (c n) j d"),
                                       v[u][:, :, :].rearrange("p c (n j d) -> p (c n) j d", j=2, d=C_DIM),
                                       pair_mask[:, :, :].unsqueeze(1).to_broadcast([P, CH * HH, 2, C_DIM]), ALU.mult)\
                        .then_inc(pairs_done.sem, 1)
                    wait(pool, vsum_done, t - 1)
                    pool.tensor_tensor(v_add[:, :], v[u][:, 0, :], v[u][:, 1, :], ALU.add).then_inc(vadd_done.sem, 1)
                    wait(pool, vadd_done, t)
                    wait(pool, cumv_ps, t - 1)
                    pool.tensor_tensor(v_sum[1 - u][:, :], v_sum[u][:, :], v_add[:, :], ALU.add)\
                        .then_inc(vsum_done.sem, 1)

                running_k(0)
                running_v(0, 0)

                def row_factor(t):
                    wait(pool, eps_done, t)
                    wait(pool, y_done, t - 1)
                    pool.tensor_tensor(rstd[:, :], var_eps[:, :], minus_half[:, :], ALU.pow).then_inc(rstd_done.sem, 1)

                def tile(t, u, i, more):
                    if not first(t):
                        row_factor(t - 1)
                    if more:
                        running_k(t + 1)
                    if more:
                        running_v(t + 1, 1 - u)

                tile_pairs(pool, TILES // 2, tile)
                row_factor(TILES - 1)

            @block.scalar
            def _(act):
                for q in (xT_sb, qT_sb, v_sb, exp_done, cross_exp, pT_sb, oT_sb):
                    q.prime(act)

                def turned_x(t):
                    wait(act, xT_ps, t)
                    wait(act, v_ps, t - 1)
                    act.copy(xT[:, :, :], ps_T[:, 0, 0:KT, :]).then_inc(xT_sb.sem, 1)
                    for k in range(KT):
                        last_copy = act.copy(xT_twice[:, k, :, :, :],
                                             ps_T[:, 0, k, :].rearrange("p (c t) -> p c t", c=CH).unsqueeze(2)
                                             .to_broadcast([P, CH, 2, CHUNK]))
                    last_copy.then_inc(xT_sb.sem, 1)

                def keep_q(t):
                    wait(act, qk_ps, t)
                    wait(act, z_ps, t - 1)
                    act.copy(qT[:, :, :], ps_f[:, 0:KT, :]).then_inc(qT_sb.sem, 1)

                def keep_v(t, u):
                    wait(act, v_ps, t)
                    wait(act, cumv_ps, t - 2)
                    wait(act, vadd_done, t - 2)
                    act.copy(v[u][:, :, :], ps_v[:, :, :]).then_inc(v_sb.sem, 1)

                def turned_o(t):
                    wait(act, oT_ps, t)
                    wait(act, y_ps, t - 1)
                    act.copy(oT[:, :, :], ps_T[:, 1, 0:KT, :]).then_inc(oT_sb.sem, 1)

                turned_x(0)
                keep_q(0)
                keep_v(0, 0)

                def gate_exp(t):
                    wait(act, z_ps, t)
                    wait(act, cross_plus, t - 1)
                    act.activation(cross_e[:, :], ps_c[:, 0:C_HEADS], ACT.Exp, scale=-C_SCALE).then_inc(cross_exp.sem, 1)

                def score_exp(t):
                    wait(act, shifted, t)
                    wait(act, pT_ps, t - 1)
                    wait(act, sum_done, t - 1)
                    act.activation(probs[:, :, :], scores[:, :, :], ACT.Exp, scale=C_SCALE).then_inc(exp_done.sem, 1)

                def turned_probs(t, b):
                    wait(act, pT_ps, t, b + 1)
                    wait(act, pv_ps, t - 1)
                    act.copy(pT[:, 4 * b:4 * b + 4, :], ps_T[:, b, :, :]).then_inc(pT_sb.sem, 1)

                def tile(t, u, i, more):
                    gate_exp(t)
                    if not first(t):
                        turned_o(t - 1)
                    if more:
                        turned_x(t + 1)
                    score_exp(t)
                    if more:
                        keep_q(t + 1)
                    if more:
                        keep_v(t + 1, 1 - u)
                    turned_probs(t, 0)
                    turned_probs(t, 1)

                tile_pairs(act, TILES // 2, tile)
                turned_o(TILES - 1)

            @block.vector
            def _(dve):
                for q in (kx_done, ksum_done, added, max_done, shifted, sum_done, inv_done, cross_plus, cross_done,
                          local_done, crossed, o_done, res_done, stats_done, mean_done, eps_done, y_done):
                    q.prime(dve)
                dve.wait_ge(in_sem, 7 * DMA)

                def spread_k(t):
                    wait(dve, qT_sb, t)
                    wait(dve, s_ps, t - 1)
                    for n in range(KT):
                        dve.tensor_tensor(kx[:, n, :, :, :],
                                          ps_f[:, KT + n, :].rearrange("p (c k) -> p c k", c=CH).unsqueeze(2)
                                          .to_broadcast([P, CH, HH, CHUNK]),
                                          head_mask[:, 0:1, :].unsqueeze(3).to_broadcast([P, CH, HH, CHUNK]), ALU.mult)\
                            .then_inc(kx_done.sem, 1)
                    wait(dve, kcum_done, t - 1)
                    dve.reduce_sum(k_sum[:, :, :].rearrange("p k c -> p (k c)"),
                                   ps_f[:, KT:2 * KT, :].rearrange("p k (c t) -> p (k c) t", c=CH), axis=AX_X)\
                        .then_inc(ksum_done.sem, 1)

                def statistics(t, u, pair):
                    wait(dve, y_ps, t)
                    dve.wait_ge(res_loaded[u], (pair + 1) * DMA)
                    dve.tensor_tensor(res[:, :], ps_o[:, DIM:2 * DIM], x_res[u][:, :], ALU.add).then_inc(res_done.sem, 1)
                    wait(dve, res_done, t)
                    dve.bn_stats(stats[:, :], res[:, :]).then_inc(stats_done.sem, 1)
                    wait(dve, stats_done, t)
                    dve.memset(spare[:, :], 0.0)
                    dve.bn_aggr(mean_var[:, :], stats[:, :]).then_inc(mean_done.sem, 1)
                    wait(dve, mean_done, t)
                    dve.tensor_scalar(var_eps[:, :], mean_var[:, 1:2], EPS, None, ALU.add).then_inc(eps_done.sem, 1)

                def normalise(t, u, pair):
                    wait(dve, rstd_done, t)
                    dve.wait_ge(y_stored[u], (pair + 1) * DMA)
                    dve.tensor_scalar(y[u][:, :], res[:, :], mean_var[:, 0:1], rstd[:, :], ALU.subtract, ALU.mult)\
                        .then_inc(y_done.sem, 1)

                spread_k(0)

                heads = lambda a: a.rearrange("p (h d) -> p h d", h=C_HEADS)
                wide = lambda a: a.unsqueeze(2).to_broadcast([P, C_HEADS, C_DIM])

                def mask_and_shift(t):
                    wait(dve, s_ps, t)
                    wait(dve, exp_done, t - 1)
                    dve.tensor_tensor(scores[:, :, :], ps_s[:, :, :, :].rearrange("p a h k -> p (a h) k"),
                                      causal[:, :].unsqueeze(1).to_broadcast([P, C_HEADS, CHUNK]), ALU.add)\
                        .then_inc(added.sem, 1)
                    wait(dve, added, t)
                    dve.reduce_max(top[:, :], scores[:, :, :], axis=AX_X).then_inc(max_done.sem, 1)
                    wait(dve, max_done, t)
                    dve.tensor_tensor(scores[:, :, :], scores[:, :, :],
                                      top[:, :].unsqueeze(2).to_broadcast([P, C_HEADS, CHUNK]), ALU.subtract)\
                        .then_inc(shifted.sem, 1)

                def sum_probs(t):
                    wait(dve, exp_done, t)
                    dve.reduce_sum(total[:, :], probs[:, :, :], axis=AX_X).then_inc(sum_done.sem, 1)
                    wait(dve, sum_done, t)
                    dve.reciprocal(inv_total[:, :], total[:, :]).then_inc(inv_done.sem, 1)

                def gates(t):
                    wait(dve, cross_exp, t)
                    dve.tensor_scalar(cross_d[:, :], cross_e[:, :], 1.0, None, ALU.add).then_inc(cross_plus.sem, 1)
                    wait(dve, cross_plus, t)
                    dve.reciprocal(cross[:, :], cross_d[:, :]).then_inc(cross_done.sem, 1)

                def local_part(t):
                    wait(dve, inv_done, t)
                    wait(dve, pv_ps, t)
                    dve.tensor_tensor(heads(o_local[:, :]), heads(ps_o[:, 0:DIM]), wide(inv_total[:, :]), ALU.mult)\
                        .then_inc(local_done.sem, 1)

                def cross_part(t):
                    wait(dve, cross_done, t)
                    wait(dve, cumv_ps, t)
                    dve.tensor_tensor(heads(o_cross[:, :]), heads(ps_c[:, DIM:2 * DIM]), wide(cross[:, :]), ALU.mult)\
                        .then_inc(crossed.sem, 1)

                def both_parts(t):
                    wait(dve, local_done, t)
                    wait(dve, crossed, t)
                    wait(dve, oT_ps, t - 1)
                    dve.tensor_tensor(o[:, :], o_local[:, :], o_cross[:, :], ALU.add).then_inc(o_done.sem, 1)

                def tile(t, u, i, more):
                    mask_and_shift(t)
                    if not first(t):
                        statistics(t - 1, 1 - u, i + u - 1)
                    sum_probs(t)
                    if not first(t):
                        normalise(t - 1, 1 - u, i + u - 1)
                    if more:
                        spread_k(t + 1)
                    gates(t)
                    local_part(t)
                    cross_part(t)
                    both_parts(t)

                tile_pairs(dve, TILES // 2, tile)
                statistics(TILES - 1, 1, TILES // 2 - 1)
                normalise(TILES - 1, 1, TILES // 2 - 1)

            @block.tensor
            def _(pe):
                for q in (xT_ps, qk_ps, v_ps, s_ps, z_ps, pT_ps, pv_ps, cumv_ps, oT_ps, y_ps):
                    q.prime(pe)
                pe.wait_ge(in_sem, 7 * DMA)

                def turn_x(t, u, i):
                    pe.wait_ge(x_loaded[u], (i + 1) * DMA)
                    wait(pe, pT_sb, t - 2, 1)
                    for k in range(KT):
                        mm = pe.transpose(ps_T[:, 0, k, :], x[u][:, k * P:(k + 1) * P], ident[:, :])
                    mm.then_inc(xT_ps.sem, 1)

                def project(t):
                    wait(pe, xT_sb, t)
                    wait(pe, ksum_done, t - 1)
                    for n in range(4):
                        for k in range(KT):
                            mm = pe.matmul(ps_f[:, n, :], w_qkv[:, k, n * P:(n + 1) * P], xT[:, k, :],
                                           start=(k == 0), stop=(k == KT - 1))
                    mm.then_inc(qk_ps.sem, 1)

                def project_v(t):
                    wait(pe, v_sb, t - 1)
                    for ch in range(CH):
                        for k in range(KT):
                            mm = pe.matmul(ps_v[:, ch, :], xT_twice[:, k, ch, :, :].rearrange("p a t -> p (a t)"),
                                           w_qkv[:, k, 2 * DIM:3 * DIM],
                                           start=(k == 0), stop=(k == KT - 1))
                    mm.then_inc(v_ps.sem, 1)

                def turn_o(t):
                    wait(pe, o_done, t)
                    for k in range(KT):
                        mm = pe.transpose(ps_T[:, 1, k, :], o[:, k * P:(k + 1) * P], ident[:, :])
                    mm.then_inc(oT_ps.sem, 1)

                def project_out(t):
                    wait(pe, oT_sb, t)
                    for k in range(KT):
                        mm = pe.matmul(ps_o[:, DIM:2 * DIM], oT[:, k, :], w_out[:, k, :],
                                       start=(k == 0), stop=(k == KT - 1))
                    mm.then_inc(y_ps.sem, 1)

                pe.wait_ge(consts_set, 5)
                turn_x(0, 0, 0)
                project(0)
                project_v(0)

                def score(t):
                    wait(pe, kx_done, t)
                    wait(pe, added, t - 1)
                    for n in range(KT):
                        for ch in range(CH):
                            q = slice(ch * CHUNK, (ch + 1) * CHUNK)
                            mm = pe.matmul(ps_s[q, n, :, :].rearrange("p h k -> p (h k)"), qT[:, n, q],
                                           kx[:, n, ch, :, :].rearrange("p h k -> p (h k)"), start=True, stop=True)
                    mm.then_inc(s_ps.sem, 1)

                def gate_args(t):
                    wait(pe, qT_sb, t)
                    wait(pe, kmean_done, t)
                    wait(pe, crossed, t - 1)
                    for n in range(KT):
                        for ch in range(CH):
                            q = slice(ch * CHUNK, (ch + 1) * CHUNK)
                            mm = pe.matmul(ps_c[q, n * HH:(n + 1) * HH], qT[:, n, q], k_mean[:, n, ch, :],
                                           start=True, stop=True)
                    mm.then_inc(z_ps.sem, 1)

                def turn_probs(t, b, more):
                    wait(pe, exp_done, t)
                    if b == 1:
                        wait(pe, oT_sb, t - 1)
                    elif more:
                        wait(pe, xT_sb, t + 1)
                    flat = probs[:, :, :].rearrange("p (n j) k -> p n (j k)", j=2)
                    for n in range(4):
                        mm = pe.transpose(ps_T[:, b, n, :], flat[:, 4 * b + n, :], ident[:, :])
                    mm.then_inc(pT_ps.sem, 1)

                def values(t, u, b):
                    wait(pe, pairs_done, t)
                    wait(pe, res_done, t - 1)
                    wait(pe, pT_sb, t, b + 1)
                    for n in range(4 * b, 4 * b + 4):
                        for ch in range(CH):
                            q = slice(ch * CHUNK, (ch + 1) * CHUNK)
                            mm = pe.matmul(ps_o[q, n * 2 * C_DIM:(n + 1) * 2 * C_DIM], pT[:, n, q],
                                           v_pairs[u][:, ch, n, :, :].rearrange("p j d -> p (j d)"), start=True, stop=True)
                    if b == 1:
                        mm.then_inc(pv_ps.sem, 1)

                def cumulated(t, u):
                    wait(pe, cross_exp, t)
                    wait(pe, v_sb, t)
                    wait(pe, vsum_done, t - 1)
                    pe.matmul(ps_c[:, DIM:2 * DIM], cum_w[:, 0, :], v_sum[u][:, :], start=True, stop=False)
                    pe.matmul(ps_c[:, DIM:2 * DIM], cum_w[:, 1, :], v[u][:, 0, :], start=False, stop=True)\
                        .then_inc(cumv_ps.sem, 1)

                def tile(t, u, i, more):
                    score(t)
                    gate_args(t)
                    if not first(t):
                        turn_o(t - 1)
                    if more:
                        turn_x(t + 1, 1 - u, i + u)
                    if not first(t):
                        project_out(t - 1)
                    if more:
                        project(t + 1)
                    if more:
                        project_v(t + 1)
                    turn_probs(t, 0, more)
                    turn_probs(t, 1, more)
                    values(t, u, 0)
                    values(t, u, 1)
                    cumulated(t, u)

                tile_pairs(pe, TILES // 2, tile)
                turn_o(TILES - 1)
                project_out(TILES - 1)
FILTER = 1024
ORDER = 64
STEP = 64
STEPS = TOKENS // STEP
SPANS = FILTER // P + 1
PADDED = FILTER + 2 * P
STARTS = P + STEP
TWO_PI = (6.28125, 0.0019350051879882812, 3.0199157663446385e-07)
ROUND = 12582912.0
PI = 3.1415925


def filter_taps(nc, taps_by_start, features_dram, w1, b1_freq1, w2, b2_freq2, w3, b3_freq3, w_taps, decay_dram,
                bypass_dram, stages):
    with ExitStack() as stack:
        s = Scope(nc, stack, "taps")
        features = s.sbuf("features", [3, FILTER])
        w = [s.sbuf(f"w{n}", [3 if n == 0 else ORDER, ORDER]) for n in range(3)]
        bf = [s.sbuf(f"bf{n}", [ORDER, 2]) for n in range(3)]
        w_last = s.sbuf("w_last", [ORDER, DIM])
        decay = s.sbuf("decay", [P, KT, FILTER])
        bypass = s.sbuf("bypass", [P, KT])
        arg = s.sbuf("arg", [ORDER, FILTER])
        turns = s.sbuf("turns", [ORDER, FILTER])
        h = s.sbuf("h", [ORDER, FILTER])
        taps = s.sbuf("taps", [P, KT, PADDED])
        by_start = s.sbuf("ordered", [P, KT, STARTS, SPANS])
        zeros = s.sbuf("zeros", [1, DIM])
        ps_h = s.psum("ps_h", [ORDER, 2, PSUM_F32])
        ps_k = s.psum("ps_k", [P, KT, 2, PSUM_F32])
        loaded, product, sined, step, final_ps, stored = [s.sem(n) for n in
                                                          ("loaded", "product", "sined", "step", "final_ps", "stored")]
        in_range = s.sem("in_range")
        decay_in = s.sem("decay_in")
        zeros_set, cleared = s.sem("zeros_set"), s.sem("cleared")
        n_loads = 8
        n_clears = len(stages)
        LAYERS = 3

        with nc.Block() as block:

            @block.sync
            def _(sp):
                for dst, src in [(features[:, :], features_dram), (w[0][:, :], w1), (w[1][:, :], w2), (w[2][:, :], w3),
                                 (bf[0][:, :], b1_freq1), (bf[1][:, :], b2_freq2), (bf[2][:, :], b3_freq3),
                                 (w_last[:, :], w_taps)]:
                    sp.dma_start(dst, src).then_inc(loaded, DMA)
                for dst, src in [(decay[:, :, :], decay_dram), (bypass[:, :], bypass_dram)]:
                    sp.dma_start(dst, src).then_inc(decay_in, DMA)
                sp.wait_ge(step, 2 * LAYERS * 6 + 6)
                sp.dma_start(taps_by_start.rearrange("(k p) t -> p k t", p=P),
                             by_start[:, :, :, :].rearrange("p k r j -> p k (r j)")).then_inc(stored, DMA)
                sp.wait_ge(stored, DMA)
                sp.wait_ge(cleared, n_clears * DMA)

            @block.tensor
            def _(pe):
                pe.wait_ge(loaded, n_loads * DMA)
                for n in range(LAYERS):
                    for half in (0, 1):
                        cols = slice(half * PSUM_F32, (half + 1) * PSUM_F32)
                        if n:
                            pe.wait_ge(sined, 2 * n + half - 1)
                        pe.matmul(ps_h[:, half, :], w[n][:, :], features[:, cols] if n == 0 else h[:, cols],
                                  start=True, stop=True).then_inc(product, 1)
                pe.wait_ge(sined, 2 * LAYERS)
                for k in range(KT):
                    for half in (0, 1):
                        mm = pe.matmul(ps_k[:, k, half, :], w_last[:, k * P:(k + 1) * P],
                                       h[:, half * PSUM_F32:(half + 1) * PSUM_F32], start=True, stop=True)
                mm.then_inc(final_ps, 1)

            @block.vector
            def _(dve):
                done = 0
                dve.memset(zeros[:, :], 0.0).then_inc(zeros_set, 1)
                dve.memset(taps[:, :, :], 0.0).then_inc(step, 1)
                done += 1
                dve.wait_ge(loaded, n_loads * DMA)
                for n in range(LAYERS):
                    for half in (0, 1):
                        dve.wait_ge(product, 2 * n + half + 1)
                        cols = slice(half * PSUM_F32, (half + 1) * PSUM_F32)
                        arg_h, turns_h = arg[:, cols], turns[:, cols]
                        dve.tensor_scalar(arg_h, ps_h[:, half, :], bf[n][:, 0:1], bf[n][:, 1:2], ALU.add, ALU.mult)\
                            .then_inc(step, 1)
                        done += 1
                        dve.wait_ge(step, done)
                        dve.tensor_scalar(turns_h, arg_h, 1.0 / (2 * np.pi), ROUND, ALU.mult, ALU.add).then_inc(step, 1)
                        done += 1
                        dve.wait_ge(step, done)
                        dve.tensor_scalar(turns_h, turns_h, ROUND, None, ALU.subtract).then_inc(step, 1)
                        done += 1
                        for part in TWO_PI:
                            dve.wait_ge(step, done)
                            dve.scalar_tensor_tensor(out=arg_h, in0=turns_h, scalar=-part, in1=arg_h,
                                                     op0=ALU.mult, op1=ALU.add).then_inc(step, 1)
                            done += 1
                        dve.wait_ge(step, done)
                        dve.tensor_scalar(arg_h, arg_h, PI, -PI, ALU.min, ALU.max).then_inc(in_range, 1)
                dve.wait_ge(decay_in, 2 * DMA)
                dve.wait_ge(final_ps, 1)
                for k in range(KT):
                    dve.tensor_tensor(taps[:, k, STEP - 1:STEP - 1 + FILTER], ps_k[:, k, :, :].rearrange("p a b -> p (a b)"),
                                      decay[:, k, :], ALU.mult).then_inc(step, 1)
                    done += 1
                dve.wait_ge(step, done)
                dve.tensor_tensor(taps[:, :, STEP - 1], taps[:, :, STEP - 1], bypass[:, :], ALU.add).then_inc(step, 1)
                done += 1
                dve.wait_ge(step, done)
                for first, n in ((0, P), (P, STARTS - P)):
                    spans = taps[:, :, first:first + SPANS * P].rearrange("p k (j r) -> p k r j", r=P)
                    dve.tensor_copy(by_start[:, :, first:first + n, :], spans[:, :, 0:n, :]).then_inc(step, 1)

            @block.scalar
            def _(act):
                act.wait_ge(zeros_set, 1)
                for x in stages:
                    act.dma_start(x[0:1, :], zeros[:, :]).then_inc(cleared, DMA)
                for n in range(LAYERS):
                    for half in (0, 1):
                        cols = slice(half * PSUM_F32, (half + 1) * PSUM_F32)
                        act.wait_ge(in_range, 2 * n + half + 1)
                        act.activation(h[:, cols], arg[:, cols], ACT.Sin).then_inc(sined, 1)


UP = 3 * DIM // P


def gated_input(nc, u_dram, w_in_dram, columns_dram, ident_dram, x0_tok, v_tok):
    with ExitStack() as stack:
        s = Scope(nc, stack, "gate")
        w_in = s.sbuf("w_in", [P, KT, 3 * DIM])
        ident = s.sbuf("ident", [P, P])
        col = s.sbuf("col", [P, 5, UP])
        x = [s.sbuf(f"x{u}", [P, GROUP, DIM]) for u in (0, 1)]
        xT = s.sbuf("xT", [P, KT, GT])
        up = [s.sbuf(f"up{u}", [P, UP, 2 + GT]) for u in (0, 1)]
        convs = [s.sbuf(f"conv{u}", [P, UP, GT]) for u in (0, 1)]
        v_rev = s.sbuf("v_rev", [P, KT, GT + STEP])
        ps_T = s.psum("ps_T", [P, KT, GT])
        ps_up = s.psum("ps_up", [P, 2, GT])
        ps_tok = s.psum("ps_tok", [P, 4, GROUP, P])
        in_sem, consts_set = s.sem("const_in"), s.sem("consts_set")
        x_loaded = [s.sem(f"x_loaded{u}") for u in (0, 1)]
        c = lambda name, n=1: s.count(name, n)
        xT_ps, xT_sb, up_ps, up_sb = c("xT_ps"), c("xT_sb"), c("up_ps", UP), c("up_sb", UP)
        tap2, tap1, tap0, carried = c("tap2", UP), c("tap1", UP), c("tap0", UP), c("carried")
        kept = c("kept")
        gated, tok_ps, tok_sb = c("gated"), c("tok_ps", 8), c("tok_sb", 8)

        with nc.Block() as block:

            @block.sync
            def _(sp):
                def load(g, u):
                    sp.dma_start(x[u][:, :, :], u_dram[bass.ds(g * GT, GT), :].rearrange("(n p) d -> p n d", p=P))\
                        .then_inc(x_loaded[u], DMA)

                for u in (0, 1):
                    load(u, u)
                for dst, src in ((ident[:, :], ident_dram), (col[:, :, :], columns_dram),
                                 (w_in[:, :, :], w_in_dram.rearrange("(k p) n -> p k n", p=P))):
                    sp.dma_start(dst, src).then_inc(in_sem, DMA)
                with sp.Fori(0, GROUPS // 2 - 1) as i:
                    for u in (0, 1):
                        wait(sp, xT_ps, i * 2 + u)
                        load(i * 2 + u + 2, u)

            @block.scalar
            def _(act):
                for q in (xT_sb, up_sb, tok_sb):
                    q.prime(act)
                act.wait_ge(in_sem, 3 * DMA)

                def projected(g, u):
                    wait(act, xT_ps, g)
                    wait(act, up_ps, g - 1)
                    act.copy(xT[:, :, :], ps_T[:, :, :]).then_inc(xT_sb.sem, 1)
                    wait(act, tap0, g - 2)
                    wait(act, carried, g - 2)
                    for f in range(UP):
                        wait(act, up_ps, g, f + 1)
                        act.activation(up[u][:, f, 2:2 + GT], ps_up[:, f % 2, :], ACT.Identity,
                                       bias=col[:, 0, f:f + 1]).then_inc(up_sb.sem, 1)

                projected(0, 0)

                def group(g, u, i, more):
                    if more:
                        projected(g + 1, 1 - u)
                    for n in range(8):
                        wait(act, tok_ps, g, n + 1)
                        kind, k, part = n // 4, n // 2 % 2, n % 2
                        rows = P if kind else STEP
                        dst = (v_tok if kind else x0_tok)[0:rows, k * P:(k + 1) * P, bass.ds(g * 2 * GROUP + part * GROUP, GROUP)]
                        act.activation(dst.rearrange("p c b -> p b c"), ps_tok[0:rows, n % 4, :, :], ACT.Copy)\
                            .then_inc(tok_sb.sem, 1)

                tile_pairs(act, GROUPS // 2, group)

            @block.vector
            def _(dve):
                for q in (tap2, tap1, tap0, carried, kept, gated):
                    q.prime(dve)
                for u in (0, 1):
                    dve.memset(up[u][:, :, 0:2], 0.0).then_inc(consts_set, 1)
                dve.memset(v_rev[:, :, 0:STEP], 0.0).then_inc(consts_set, 1)
                dve.wait_ge(in_sem, 3 * DMA)
                dve.wait_ge(consts_set, 3)
                with dve.Fori(0, GROUPS // 2) as i:
                    for u in (0, 1):
                        g = i * 2 + u
                        conv = convs[u]
                        wait(dve, carried, g - 1)
                        wait(dve, tok_ps, g - 2, 4)
                        wait(dve, gated, g - 2)
                        for f in range(UP):
                            wait(dve, up_sb, g, f + 1)
                            dve.tensor_scalar(conv[:, f, :], up[u][:, f, 2:2 + GT], col[:, 3, f:f + 1], col[:, 4, f:f + 1],
                                              ALU.mult, ALU.add).then_inc(tap2.sem, 1)
                        for tap, count, before in ((2, tap1, tap2), (1, tap0, tap1)):
                            for f in range(UP):
                                wait(dve, before, g, f + 1)
                                dve.scalar_tensor_tensor(out=conv[:, f, :], in0=up[u][:, f, tap - 1:tap - 1 + GT],
                                                         scalar=col[:, tap, f:f + 1], in1=conv[:, f, :],
                                                         op0=ALU.mult, op1=ALU.add).then_inc(count.sem, 1)
                        wait(dve, tap0, g - 1)
                        dve.tensor_copy(up[1 - u][:, :, 0:2], up[u][:, :, GT:GT + 2]).then_inc(carried.sem, 1)
                        wait(dve, tap0, g)
                        wait(dve, tok_ps, g - 1)
                        dve.tensor_copy(v_rev[:, :, GT:GT + STEP], v_rev[:, :, 0:STEP]).then_inc(kept.sem, 1)
                        wait(dve, kept, g)
                        for k in range(KT):
                            last = dve.tensor_tensor(v_rev[:, k, 0:GT][:, ::-1], conv[:, 2 + k, :], conv[:, 4 + k, :], ALU.mult)
                        last.then_inc(gated.sem, 1)

            @block.tensor
            def _(pe):
                for q in (xT_ps, up_ps, tok_ps):
                    q.prime(pe)
                pe.wait_ge(in_sem, 3 * DMA)

                def project(g, u, i):
                    pe.wait_ge(x_loaded[u], (i + 1) * DMA)
                    wait(pe, xT_sb, g - 1)
                    for k in range(KT):
                        for n in range(GROUP):
                            mm = pe.transpose(ps_T[:, k, n * P:(n + 1) * P], x[u][:, n, k * P:(k + 1) * P], ident[:, :])
                    mm.then_inc(xT_ps.sem, 1)
                    wait(pe, xT_sb, g)
                    for f in range(UP):
                        if f < 2:
                            wait(pe, up_sb, g - 1, f + UP - 1)
                        else:
                            wait(pe, up_sb, g, f - 1)
                        for k in range(KT):
                            mm = pe.matmul(ps_up[:, f % 2, :], w_in[:, k, f * P:(f + 1) * P], xT[:, k, :],
                                           start=(k == 0), stop=(k == KT - 1))
                        mm.then_inc(up_ps.sem, 1)

                def to_tokens(g, u):
                    conv = convs[u]
                    for n in range(8):
                        if n < 4:
                            wait(pe, tok_sb, g - 1, n + 5)
                        else:
                            wait(pe, tok_sb, g, n - 3)
                        if n == 0:
                            wait(pe, tap0, g, 2)
                        if n == 4:
                            wait(pe, gated, g)
                        k, part = n // 2 % 2, n % 2
                        if n < 4:
                            pe.matmul(ps_tok[:, n % 4, 0, 0:STEP], ident[:, :], ident[:, 0:STEP], start=True, stop=True)
                        for b in range(GROUP):
                            step = part * GROUP + b
                            if n < 4:
                                mm = pe.transpose(ps_tok[0:STEP, n % 4, b, :], conv[:, k, step * STEP:(step + 1) * STEP],
                                                  ident[:, :])
                            else:
                                first = GT - (step + 1) * STEP
                                mm = pe.transpose(ps_tok[:, n % 4, b, :], v_rev[:, k, first:first + P], ident[:, :])
                        mm.then_inc(tok_ps.sem, 1)

                project(0, 0, 0)

                def group(g, u, i, more):
                    if more:
                        project(g + 1, 1 - u, i + u)
                    to_tokens(g, u)

                tile_pairs(pe, GROUPS // 2, group)


RING = 4
CONV_GROUP = 8


def long_convolution(nc, taps_by_start, x0_tok, v_tok, prefetch=None):
    with ExitStack() as stack:
        s = Scope(nc, stack, "conv")
        toep = [s.sbuf(f"toep{r}", [P, STEP, SPANS]) for r in range(RING)]
        ps = s.psum("ps", [STEP, 2, CONV_GROUP, STEPS])
        loaded = [s.sem(f"loaded{r}") for r in range(RING)]
        used = s.count("used", CONV_GROUP)
        multiplied = s.count("multiplied")
        groups = DIM // CONV_GROUP
        turns = CONV_GROUP // RING
        row = STARTS * SPANS

        with nc.Block() as block:

            def load(queue, ch, r):
                rows = bass.AP(tensor=taps_by_start.tensor, offset=ch * row, ap=[[SPANS, P], [1, STEP * SPANS]])
                queue.dma_start(toep[r][:, :, :].rearrange("p q j -> p (q j)"), rows).then_inc(loaded[r], DMA)

            def load_share(queue, which):
                for r in range(which, RING, 2):
                    load(queue, r, r)
                if prefetch and which == 0:
                    prefetch(queue)
                with queue.Fori(0, groups - 1) as g:
                    for n in range(which, CONV_GROUP, 2):
                        wait(queue, used, g, n + 1)
                        load(queue, g * CONV_GROUP + n + RING, n % RING)
                for n in range(which, CONV_GROUP - RING, 2):
                    wait(queue, used, groups - 1, n + 1)
                    load(queue, DIM - CONV_GROUP + n + RING, n % RING)

            @block.sync
            def _(sp):
                load_share(sp, 0)

            @block.scalar
            def _(act):
                load_share(act, 1)

            @block.tensor
            def _(pe):
                used.prime(pe)
                with pe.Fori(0, groups // 2) as i:
                    for u in (0, 1):
                        g = i * 2 + u
                        wait(pe, multiplied, g - 2)
                        for n in range(CONV_GROUP):
                            pe.wait_ge(loaded[n % RING], (g * turns + n // RING + 1) * DMA)
                            for j in range(SPANS):
                                mm = pe.matmul(ps[:, u, n, 2 * j:STEPS], toep[n % RING][:, :, j],
                                               v_tok[:, g * CONV_GROUP + n, 0:STEPS - 2 * j],
                                               start=(j == 0), stop=(j == SPANS - 1))
                            mm.then_inc(used.sem, 1)

            @block.vector
            def _(dve):
                multiplied.prime(dve)
                with dve.Fori(0, groups // 2) as i:
                    for u in (0, 1):
                        g = i * 2 + u
                        wait(dve, used, g)
                        x0 = x0_tok[0:STEP, bass.ds(g * CONV_GROUP, CONV_GROUP), :]
                        dve.tensor_tensor(x0, ps[:, u, :, :], x0, ALU.mult).then_inc(multiplied.sem, 1)


QUAD = 4


def project_and_norm(nc, z_tok, u_dram, x_all, w_out_dram, b_out_dram, ident_dram):
    with ExitStack() as stack:
        s = Scope(nc, stack, "out0")
        w_out = s.sbuf("w_out", [P, KT, DIM])
        b_out = s.sbuf("b_out", [P, DIM])
        ident = s.sbuf("ident", [P, P])
        z = [s.sbuf(f"z{u}", [STEP, 2, DIM]) for u in (0, 1)]
        zT = [s.sbuf(f"zT{u}", [P, KT, P]) for u in (0, 1)]
        minus_half = s.sbuf("minus_half", [P, QUAD])
        res = s.sbuf("res", [P, QUAD, DIM])
        stats = s.sbuf("stats", [P, QUAD, 6])
        mean_var = s.sbuf("mean_var", [P, QUAD, 2])
        var_eps = s.sbuf("var_eps", [P, QUAD])
        rstd = s.sbuf("rstd", [P, QUAD])
        spare = s.sbuf("spare", [P, 2])
        ps_T = s.psum("ps_T", [P, 2, PSUM_F32])
        ps_y = s.psum("ps_y", [P, QUAD, PSUM_F32])
        in_sem, consts_set = s.sem("const_in"), s.sem("consts_set")
        x_loaded = [s.sem(f"x_loaded{n}") for n in range(TILES // QUAD)]
        c = lambda name, n=1: s.count(name, n)
        z_copied, z_ps, z_sb, y_ps, biased = c("z_copied"), c("z_ps"), c("z_sb"), c("y_ps"), c("biased")
        res_done, stats_done, mean_done = c("res_done", QUAD), c("stats_done", QUAD), c("mean_done", QUAD)
        eps_done, rstd_done, normed = c("eps_done"), c("rstd_done"), c("normed", QUAD)

        with nc.Block() as block:

            @block.sync
            def _(sp):
                for dst, src in ((ident[:, :], ident_dram), (b_out[:, :], b_out_dram.to_broadcast([P, DIM])),
                                 (w_out[:, :, :], w_out_dram.rearrange("(k p) n -> p k n", p=P))):
                    sp.dma_start(dst, src).then_inc(in_sem, DMA)
                for n in range(0, TILES, QUAD):
                    sp.dma_start(x_all[:, n:n + QUAD, :], u_dram[n * P:(n + QUAD) * P, :].rearrange("(n p) d -> p n d", p=P))\
                        .then_inc(x_loaded[n // QUAD], DMA)

            @block.gpsimd
            def _(pool):
                for q in (biased, rstd_done):
                    q.prime(pool)
                pool.memset(minus_half[:, :], -0.5).then_inc(consts_set, 1)
                pool.wait_ge(consts_set, 1)
                pool.wait_ge(in_sem, 3 * DMA)

                def add_bias(i):
                    pool.wait_ge(x_loaded[i], DMA)
                    rows = x_all[:, i * QUAD:(i + 1) * QUAD, :]
                    pool.tensor_tensor(rows, rows, b_out[:, :].unsqueeze(1).to_broadcast([P, QUAD, DIM]), ALU.add)\
                        .then_inc(biased.sem, 1)

                add_bias(0)
                for i in range(TILES // QUAD):
                    if i < TILES // QUAD - 1:
                        add_bias(i + 1)
                    wait(pool, eps_done, i)
                    wait(pool, normed, i - 1)
                    pool.tensor_tensor(rstd[:, :], var_eps[:, :], minus_half[:, :], ALU.pow).then_inc(rstd_done.sem, 1)

            @block.scalar
            def _(act):
                for q in (z_copied, z_sb):
                    q.prime(act)

                def gather(t, u):
                    wait(act, z_ps, t - 2)
                    act.activation(z[u][:, :, :], z_tok[0:STEP, :, bass.ds(t * 2, 2)].rearrange("p c n -> p n c"), ACT.Copy)\
                        .then_inc(z_copied.sem, 1)

                gather(0, 0)

                def tile(t, u, i, more):
                    if more:
                        gather(t + 1, 1 - u)
                    wait(act, z_ps, t)
                    wait(act, y_ps, t - 2)
                    act.copy(zT[u][:, :, :], ps_T[:, u, 0:DIM].rearrange("p (k t) -> p k t", k=KT)).then_inc(z_sb.sem, 1)

                tile_pairs(act, TILES // 2, tile)

            @block.vector
            def _(dve):
                for q in (res_done, stats_done, mean_done, eps_done, normed):
                    q.prime(dve)
                with dve.Fori(0, TILES // QUAD) as i:
                    row = lambda n: x_all[:, bass.ds(i * QUAD + n, 1), :].rearrange("p a d -> p (a d)")
                    wait(dve, biased, i)
                    wait(dve, normed, i - 1)
                    for n in range(QUAD):
                        wait(dve, y_ps, i * QUAD + n)
                        dve.tensor_tensor(res[:, n, :], ps_y[:, n, 0:DIM], row(n), ALU.add).then_inc(res_done.sem, 1)
                    for n in range(QUAD):
                        wait(dve, res_done, i, n + 1)
                        dve.bn_stats(stats[:, n, :], res[:, n, :]).then_inc(stats_done.sem, 1)
                    wait(dve, stats_done, i)
                    dve.memset(spare[:, :], 0.0)
                    for n in range(QUAD):
                        dve.bn_aggr(mean_var[:, n, :], stats[:, n, :]).then_inc(mean_done.sem, 1)
                    wait(dve, mean_done, i)
                    dve.tensor_scalar(var_eps[:, :], mean_var[:, :, 1], EPS, None, ALU.add).then_inc(eps_done.sem, 1)
                    wait(dve, rstd_done, i)
                    for n in range(QUAD):
                        dve.tensor_scalar(row(n), res[:, n, :], mean_var[:, n, 0:1], rstd[:, n:n + 1],
                                          ALU.subtract, ALU.mult).then_inc(normed.sem, 1)

            @block.tensor
            def _(pe):
                for q in (z_ps, y_ps):
                    q.prime(pe)
                pe.wait_ge(in_sem, 3 * DMA)

                def turn_z(t, u):
                    wait(pe, z_copied, t)
                    wait(pe, z_sb, t - 2)
                    pe.matmul(ps_T[:, u, 0:STEP], ident[:, :], ident[:, 0:STEP], start=True, stop=True)
                    for k in range(KT):
                        for n in (0, 1):
                            mm = pe.transpose(ps_T[:, u, k * P + n * STEP:k * P + (n + 1) * STEP],
                                              z[u][:, n, k * P:(k + 1) * P], ident[0:STEP, 0:STEP])
                    mm.then_inc(z_ps.sem, 1)

                def project(t, n, i, more):
                    if more:
                        turn_z(t + 1, (n + 1) % 2)
                    wait(pe, z_sb, t)
                    wait(pe, res_done, i - 1, n + 1)
                    for k in range(KT):
                        mm = pe.matmul(ps_y[:, n, 0:DIM], zT[n % 2][:, k, :], w_out[:, k, :],
                                       start=(k == 0), stop=(k == KT - 1))
                    mm.then_inc(y_ps.sem, 1)

                turn_z(0, 0)
                with pe.Fori(0, TILES // QUAD - 1) as i:
                    for n in range(QUAD):
                        project(i * QUAD + n, n, i, True)
                for n in range(QUAD):
                    project(TILES - QUAD + n, n, TILES // QUAD - 1, n < QUAD - 1)
EXPERTS = 8
FF = 4 * DIM
FT = FF // P
TOP_K = 2
BLOCKS = TOKENS * TOP_K // P + EXPERTS
ROWS = BLOCKS * P
CHOICES = 16


def route(nc, x_all, x_rows, weight, block_expert, token_of, choice_of, router_w_dram, router_b_dram, ident_dram,
          before_dram, numbers_dram, scratch, prefetch=None):
    with ExitStack() as stack:
        s = Scope(nc, stack, "route")
        TE = [P, TILES, EXPERTS]
        ident = s.sbuf("ident", [P, P])
        before = s.sbuf("before", [P, 2, P])
        numbers = s.sbuf("numbers", [P, P + TOP_K * TILES])
        router_w = s.sbuf("router_w", [P, KT, EXPERTS])
        router_b = s.sbuf("router_b", [P, EXPERTS])
        xT = s.sbuf("xT", [P, 2, 2 * KT, P])
        logits = s.sbuf("logits", TE)
        best = s.sbuf("best", [P, TILES])
        probs = s.sbuf("probs", TE)
        norm = s.sbuf("norm", [P, TILES])
        same = s.sbuf("same", TE)
        first = s.sbuf("first", [P, TILES])
        chosen = s.sbuf("chosen", [P, TOP_K] + TE[1:])
        upto = [s.sbuf(f"upto{n}", TE) for n in (0, 1)]
        blocks = s.sbuf("blocks", [P, EXPERTS])
        ends = s.sbuf("ends", [P, EXPERTS + 1])
        passed = scratch[:, 0:BLOCKS * EXPERTS].rearrange("p (b e) -> p b e", e=EXPERTS)
        taken = BLOCKS * EXPERTS

        def carve(n, inner):
            nonlocal taken
            taken += n * inner
            return scratch[:, taken - n * inner:taken].rearrange("p (n i) -> p n i", i=inner)

        pos_f = carve(TOP_K, TILES)
        expert_f = carve(1, BLOCKS)[:, 0, :]
        both = carve(TILES, EXPERTS)
        rank, place = carve(TILES, EXPERTS), carve(TILES, EXPERTS)
        block_of, row_of = carve(TOP_K, TILES), carve(TOP_K, TILES)
        is_row = [carve(CHOICES, P) for _ in (0, 1)]
        is_block = [carve(CHOICES, BLOCKS) for _ in (0, 1)]
        ps_T = s.psum("ps_T", [P, 2, PSUM_F32])
        ps_l = s.psum("ps_l", [P, 2, PSUM_F32])
        ps_rank = s.psum("ps_rank", [P, 2, PSUM_F32])
        ps_token = s.psum("ps_token", [P, PSUM_F32])
        in_sem = s.sem("const_in")
        c = lambda name, n=1: s.count(name, n)
        xT_ps, xT_sb, l_ps, l_sb = c("xT_ps"), c("xT_sb"), c("l_ps"), c("l_sb")
        step, shifted, exped, mask_ready, ranked, placed, summed, stored = [
            s.sem(n) for n in ("step", "shifted", "exped", "mask_ready", "ranked", "placed", "summed", "stored")]
        with nc.Block() as block:

            @block.sync
            def _(sp):
                for dst, src in ((ident[:, :], ident_dram), (before[:, :, :], before_dram), (numbers[:, :], numbers_dram),
                                 (router_w[:, :, :], router_w_dram.rearrange("(k p) e -> p k e", p=P)),
                                 (router_b[:, :], router_b_dram.to_broadcast([P, EXPERTS]))):
                    sp.dma_start(dst, src).then_inc(in_sem, DMA)
                for n in range(0, TILES, QUAD):
                    sp.dma_start(x_rows[n * P:(n + QUAD) * P, :].rearrange("(n p) d -> p n d", p=P), x_all[:, n:n + QUAD, :])\
                        .then_inc(stored, DMA)
                if prefetch:
                    prefetch(sp)
                sp.wait_ge(stored, TILES // QUAD * DMA)

            @block.tensor
            def _(pe):
                xT_ps.prime(pe)
                l_ps.prime(pe)
                pe.wait_ge(in_sem, 5 * DMA)
                pairs = TILES // 2

                def turn_pair(n):
                    wait(pe, xT_sb, n - 2)
                    for j in (0, 1):
                        for k in range(KT):
                            mm = pe.transpose(ps_T[:, n % 2, (j * KT + k) * P:(j * KT + k + 1) * P],
                                              x_all[:, 2 * n + j, k * P:(k + 1) * P], ident[:, :])
                    mm.then_inc(xT_ps.sem, 1)

                turn_pair(0)
                for n in range(pairs):
                    if n < pairs - 1:
                        turn_pair(n + 1)
                    wait(pe, xT_sb, n)
                    wait(pe, l_sb, n - 2)
                    for j in (0, 1):
                        for k in range(KT):
                            mm = pe.matmul(ps_l[:, n % 2, j * EXPERTS:(j + 1) * EXPERTS], xT[:, n % 2, j * KT + k, :],
                                           router_w[:, k, :], start=(k == 0), stop=(k == KT - 1))
                    mm.then_inc(l_ps.sem, 1)
                pe.wait_ge(mask_ready, 1)
                for n in (0, 1):
                    mm = pe.matmul(ps_rank[:, n, 0:TILES * EXPERTS], before[:, n, :],
                                   both[:, :, :].rearrange("p t e -> p (t e)"), start=True, stop=True)
                mm.then_inc(ranked, 1)
                chunks = TOP_K * TILES // CHOICES
                for n in range(chunks):
                    pe.wait_ge(placed, n + 1)
                    for j in range(CHOICES):
                        mm = pe.matmul(ps_token[:, 0:BLOCKS], is_row[n % 2][:, j, :], is_block[n % 2][:, j, :],
                                       start=(n == 0 and j == 0), stop=(n == chunks - 1 and j == CHOICES - 1))
                    mm.then_inc(summed, 1)

            @block.scalar
            def _(act):
                xT_sb.prime(act)
                for n in range(TILES // 2):
                    wait(act, xT_ps, n)
                    wait(act, l_ps, n - 2)
                    act.copy(xT[:, n % 2, :, :], ps_T[:, n % 2, :].rearrange("p (k t) -> p k t", t=P)).then_inc(xT_sb.sem, 1)
                act.wait_ge(shifted, 1)
                act.activation(probs[:, :, :], logits[:, :, :], ACT.Exp).then_inc(exped, 1)

            @block.vector
            def _(dve):
                l_sb.prime(dve)
                dve.wait_ge(in_sem, 5 * DMA)
                for n in range(TILES // 2):
                    wait(dve, l_ps, n)
                    dve.tensor_tensor(logits[:, 2 * n:2 * n + 2, :],
                                      ps_l[:, n % 2, 0:2 * EXPERTS].rearrange("p (j e) -> p j e", j=2),
                                      router_b[:, :].unsqueeze(1).to_broadcast([P, 2, EXPERTS]), ALU.add).then_inc(l_sb.sem, 1)
                wait(dve, l_sb, TILES // 2 - 1)
                done = 0

                def then(ins):
                    nonlocal done
                    ins.then_inc(step, 1)
                    done += 1
                    dve.wait_ge(step, done)

                over_e = lambda a: a.unsqueeze(2).to_broadcast(TE)
                over_t = lambda a: a.unsqueeze(1).to_broadcast(TE)
                number = over_t(numbers[:, 0:EXPERTS])
                then(dve.reduce_max(best[:, :], logits[:, :, :], axis=AX_X))
                dve.tensor_tensor(logits[:, :, :], logits[:, :, :], over_e(best[:, :]), ALU.subtract).then_inc(shifted, 1)
                dve.wait_ge(exped, 1)
                then(dve.reduce_sum(norm[:, :], probs[:, :, :], axis=AX_X))
                then(dve.reciprocal(norm[:, :], norm[:, :]))
                then(dve.tensor_tensor(probs[:, :, :], probs[:, :, :], over_e(norm[:, :]), ALU.mult))
                for k in range(TOP_K):
                    then(dve.reduce_max(weight[:, k, :], probs[:, :, :], axis=AX_X))
                    then(dve.tensor_tensor(same[:, :, :], probs[:, :, :], over_e(weight[:, k, :]), ALU.is_ge))
                    then(dve.tensor_scalar(same[:, :, :], same[:, :, :], -float(EXPERTS), float(EXPERTS), ALU.mult, ALU.add))
                    then(dve.tensor_tensor(same[:, :, :], same[:, :, :], number, ALU.add))
                    then(dve.tensor_reduce(first[:, :], same[:, :, :], AX_X, ALU.min))
                    then(dve.tensor_tensor(chosen[:, k, :, :], number, over_e(first[:, :]), ALU.is_equal))
                    if k < TOP_K - 1:
                        then(dve.scalar_tensor_tensor(out=probs[:, :, :], in0=chosen[:, k, :, :], scalar=-2.0,
                                                      in1=probs[:, :, :], op0=ALU.mult, op1=ALU.add))
                dve.tensor_tensor(both[:, :, :], chosen[:, 0, :, :], chosen[:, 1, :, :], ALU.add).then_inc(mask_ready, 1)
                dve.wait_ge(ranked, 1)
                flat = lambda a: a.rearrange("p t e -> p (t e)")
                total = ps_rank[:, 1, 0:TILES * EXPERTS]
                then(dve.tensor_copy(flat(upto[0][:, :, :]), total))
                src, n = 0, 1
                while n < TILES:
                    a, b = upto[src], upto[1 - src]
                    then(dve.tensor_copy(b[:, 0:n, :], a[:, 0:n, :]))
                    then(dve.tensor_tensor(b[:, n:, :], a[:, n:, :], a[:, 0:TILES - n, :], ALU.add))
                    src, n = 1 - src, 2 * n
                upto_t = upto[src]
                then(dve.tensor_tensor(flat(rank[:, :, :]), flat(upto_t[:, :, :]), total, ALU.subtract))
                then(dve.tensor_tensor(flat(rank[:, :, :]), flat(rank[:, :, :]), ps_rank[:, 0, 0:TILES * EXPERTS], ALU.add))
                then(dve.tensor_scalar(blocks[:, :], upto_t[:, TILES - 1, :], 1.0 / P, (P - 1) / P - (P - 1) / (2 * P),
                                       ALU.mult, ALU.add))
                then(dve.tensor_scalar(blocks[:, :], blocks[:, :], ROUND, None, ALU.add))
                then(dve.tensor_scalar(blocks[:, :], blocks[:, :], ROUND, None, ALU.subtract))
                then(dve.memset(ends[:, 0:1], 0.0))
                for e in range(EXPERTS):
                    then(dve.tensor_tensor(ends[:, e + 1:e + 2], ends[:, e:e + 1], blocks[:, e:e + 1], ALU.add))
                then(dve.scalar_tensor_tensor(out=place[:, :, :], in0=over_t(ends[:, 0:EXPERTS]), scalar=float(P),
                                              in1=rank[:, :, :], op0=ALU.mult, op1=ALU.add))
                for k in range(TOP_K):
                    then(dve.tensor_tensor(same[:, :, :], chosen[:, k, :, :], place[:, :, :], ALU.mult))
                    then(dve.reduce_sum(pos_f[:, k, :], same[:, :, :], axis=AX_X))
                then(dve.tensor_scalar(block_of, pos_f[:, :, :], 1.0 / P, -(P - 1) / (2 * P), ALU.mult, ALU.add))
                then(dve.tensor_scalar(block_of, block_of, ROUND, None, ALU.add))
                then(dve.tensor_scalar(block_of, block_of, ROUND, None, ALU.subtract))
                then(dve.scalar_tensor_tensor(out=row_of, in0=block_of, scalar=-float(P), in1=pos_f[:, :, :],
                                              op0=ALU.mult, op1=ALU.add))
                for n in range(TOP_K * TILES // CHOICES):
                    k, t = n * CHOICES // TILES, n * CHOICES % TILES
                    if n >= 2:
                        dve.wait_ge(summed, n - 1)
                    wide = lambda a, inner: a.unsqueeze(2).to_broadcast([P, CHOICES, inner])
                    count_to = lambda inner: numbers[:, 0:inner].unsqueeze(1).to_broadcast([P, CHOICES, inner])
                    is_b = is_block[n % 2]
                    then(dve.tensor_tensor(is_b, count_to(BLOCKS), wide(block_of[:, k, t:t + CHOICES], BLOCKS), ALU.is_equal))
                    then(dve.tensor_tensor(is_row[n % 2], count_to(P), wide(row_of[:, k, t:t + CHOICES], P), ALU.is_equal))
                    dve.tensor_tensor(is_b, is_b, wide(numbers[:, P + n * CHOICES:P + (n + 1) * CHOICES], BLOCKS), ALU.mult).then_inc(placed, 1)
                wide = [P, BLOCKS, EXPERTS]
                then(dve.tensor_tensor(passed[:, :, :], ends[:, 1:].unsqueeze(1).to_broadcast(wide),
                                       numbers[:, 0:BLOCKS].unsqueeze(2).to_broadcast(wide), ALU.is_le))
                then(dve.reduce_sum(expert_f[:, :], passed[:, :, :], axis=AX_X))
                then(dve.tensor_scalar(expert_f[:, :], expert_f[:, :], float(EXPERTS - 1), None, ALU.min))
                then(dve.tensor_copy(block_expert[:, :], expert_f[0:1, :]))
                dve.wait_ge(summed, TOP_K * TILES // CHOICES)
                number_of = ps_token[:, 0:BLOCKS]
                a_blocks, b_blocks = expert_f, passed[:, :, 0]
                then(dve.tensor_scalar(a_blocks, number_of, TOKENS + 0.5, -float(TOKENS), ALU.is_ge, ALU.mult))
                then(dve.tensor_tensor(a_blocks, a_blocks, number_of, ALU.add))
                then(dve.tensor_scalar(a_blocks, a_blocks, -1.0, 0.0, ALU.add, ALU.max))
                then(dve.tensor_copy(token_of[:, :], a_blocks))
                then(dve.tensor_scalar(a_blocks, numbers[:, 0:BLOCKS], float(P), numbers[:, P:P + 1], ALU.mult, ALU.add))
                then(dve.tensor_scalar(b_blocks, number_of, 0.5, None, ALU.is_lt))
                then(dve.scalar_tensor_tensor(out=a_blocks, in0=a_blocks, scalar=float(TOP_K * TOKENS), in1=b_blocks,
                                              op0=ALU.add, op1=ALU.mult))
                then(dve.scalar_tensor_tensor(out=a_blocks, in0=number_of, scalar=-1.0, in1=a_blocks,
                                              op0=ALU.add, op1=ALU.add))
                then(dve.tensor_copy(choice_of[:, :], a_blocks))


def experts(nc, x_rows, token_of, choice_of, out_rows, block_expert, w_up, w_down, up_loaded, down_loaded, ident_dram):
    with ExitStack() as stack:
        s = Scope(nc, stack, "expert")
        ident = s.sbuf("ident", [P, P])
        x = [s.sbuf(f"x{u}", [P, DIM]) for u in (0, 1)]
        xT = s.sbuf("xT", [P, KT, P])
        h = [s.sbuf(f"h{n}", [P, FF // 2]) for n in (0, 1)]
        hT = s.sbuf("hT", [P, FT, P])
        y = [s.sbuf(f"y{u}", [P, DIM]) for u in (0, 1)]
        ps_x = s.psum("ps_x", [P, PSUM_F32])
        ps_h = s.psum("ps_h", [P, 2, PSUM_F32])
        ps_T = s.psum("ps_T", [P, 2, PSUM_F32])
        ps_y = s.psum("ps_y", [P, 2, PSUM_F32])
        in_sem = s.sem("const_in")
        x_loaded = [s.sem(f"x_loaded{u}") for u in (0, 1)]
        y_stored = [s.sem(f"y_stored{u}") for u in (0, 1)]
        c = lambda name, n=1: s.count(name, n)
        xT_ps, xT_sb, h_ps, gelu_done = c("xT_ps"), c("xT_sb"), c("h_ps", 2), c("gelu_done", 2)
        hT_ps, hT_sb0, hT_sb1, y_ps, y_done = c("hT_ps", 2), c("hT_sb0"), c("hT_sb1"), c("y_ps"), c("y_done")

        def near_end(g):
            return isinstance(g, int) and g >= BLOCKS - 2

        with nc.Block() as block:

            @block.sync
            def _(sp):
                sp.dma_start(ident[:, :], ident_dram).then_inc(in_sem, DMA)

            @block.gpsimd
            def _(pool):
                def gather(g):
                    wait(pool, xT_ps, g - 2)
                    pool.indirect_dma_start(out=x[g % 2][:, :], out_offset=None, in_=x_rows,
                                            in_offset=bass.IndirectOffsetOnAxis(ap=token_of[:, g:g + 1], axis=0))\
                        .then_inc(x_loaded[g % 2], DMA)

                def scatter(g):
                    wait(pool, y_done, g)
                    pool.indirect_dma_start(out=out_rows, out_offset=bass.IndirectOffsetOnAxis(
                        ap=choice_of[:, g:g + 1], axis=0), in_=y[g % 2][:, :], in_offset=None)\
                        .then_inc(y_stored[g % 2], DMA)

                for g in (0, 1):
                    gather(g)
                for g in range(BLOCKS + 1):
                    if g < BLOCKS - 2:
                        gather(g + 2)
                    if g:
                        scatter(g - 1)
                for u in (0, 1):
                    pool.wait_ge(y_stored[u], BLOCKS // 2 * DMA)

            @block.scalar
            def _(act):
                for q in (gelu_done, hT_sb1):
                    q.prime(act)

                def tile(g, u, i, more):
                    for n in (0, 1):
                        wait(act, h_ps, g, n + 1)
                        wait(act, hT_ps, g - 1, n + 1)
                        act.activation(h[n][:, :], ps_h[:, n, :], ACT.Gelu).then_inc(gelu_done.sem, 1)
                    wait(act, hT_ps, g, 2)
                    wait(act, y_ps, g - 1)
                    act.copy(hT[:, 4:8, :], ps_T[:, 1, :].rearrange("p (f t) -> p f t", f=4)).then_inc(hT_sb1.sem, 1)

                with act.Fori(0, BLOCKS // 2) as i:
                    for u in (0, 1):
                        tile(i * 2 + u, u, i, True)

            @block.vector
            def _(dve):
                for q in (xT_sb, hT_sb0, y_done):
                    q.prime(dve)

                def turned_x(g):
                    wait(dve, xT_ps, g)
                    wait(dve, h_ps, g - 1)
                    dve.tensor_copy(xT[:, :, :], ps_x[:, 0:DIM].rearrange("p (k t) -> p k t", k=KT)).then_inc(xT_sb.sem, 1)

                turned_x(0)
                turned_x(1)

                def tile(g, u, i, more):
                    wait(dve, hT_ps, g, 1)
                    wait(dve, y_ps, g - 1)
                    dve.tensor_copy(hT[:, 0:4, :], ps_T[:, 0, :].rearrange("p (f t) -> p f t", f=4)).then_inc(hT_sb0.sem, 1)
                    if not near_end(g):
                        turned_x(g + 2)
                    wait(dve, y_ps, g)
                    if not (isinstance(i, int) and i == 0):
                        dve.wait_ge(y_stored[u], i * DMA)
                    dve.tensor_copy(y[u][:, :], ps_y[:, u, 0:DIM]).then_inc(y_done.sem, 1)

                tile_pairs(dve, BLOCKS // 2, tile)

            @block.tensor
            def _(pe):
                for q in (xT_ps, h_ps, hT_ps, y_ps):
                    q.prime(pe)
                pe.wait_ge(in_sem, DMA)

                def up(g, u, i, expert):
                    wait(pe, xT_sb, g)
                    for n in (0, 1):
                        wait(pe, gelu_done, g - 1, n + 1)
                        for k in range(KT):
                            cols = bass.ds((expert * KT + k) * FF + n * PSUM_F32, PSUM_F32)
                            mm = pe.matmul(ps_h[:, n, :], xT[:, k, :], w_up[:, cols], start=(k == 0), stop=(k == KT - 1))
                        mm.then_inc(h_ps.sem, 1)

                def turn_x(g, u, i):
                    pe.wait_ge(x_loaded[u], (i + 1) * DMA)
                    wait(pe, xT_sb, g - 1)
                    for k in range(KT):
                        mm = pe.transpose(ps_x[:, k * P:(k + 1) * P], x[u][:, k * P:(k + 1) * P], ident[:, :])
                    mm.then_inc(xT_ps.sem, 1)

                turn_x(0, 0, 0)
                pe.wait_ge(up_loaded, EXPERTS * DMA)
                pe.wait_ge(down_loaded, EXPERTS * DMA)
                e0 = pe.value_load(block_expert[0:1, 0:1], min_val=0, max_val=EXPERTS - 1)
                up(0, 0, 0, e0)
                turn_x(1, 1, 0)

                def tile(g, u, i, more):
                    for n in (0, 1):
                        wait(pe, gelu_done, g, n + 1)
                        wait(pe, (hT_sb0, hT_sb1)[n], g - 1)
                        for f in range(4):
                            mm = pe.transpose(ps_T[:, n, f * P:(f + 1) * P], h[n][:, f * P:(f + 1) * P], ident[:, :])
                        mm.then_inc(hT_ps.sem, 1)
                    if more:
                        up(g + 1, 1 - u, i + u,
                           pe.value_load(block_expert[0:1, bass.ds(g + 1, 1)], min_val=0, max_val=EXPERTS - 1))
                    if not near_end(g):
                        turn_x(g + 2, u, i + 1)
                    expert = pe.value_load(block_expert[0:1, bass.ds(g, 1)], min_val=0, max_val=EXPERTS - 1)
                    wait(pe, hT_sb0, g)
                    wait(pe, y_done, g - 2)
                    for f in range(FT):
                        if f == 4:
                            wait(pe, hT_sb1, g)
                        mm = pe.matmul(ps_y[:, u, 0:DIM], hT[:, f, :], w_down[:, bass.ds((expert * FT + f) * DIM, DIM)],
                                       start=(f == 0), stop=(f == FT - 1))
                    mm.then_inc(y_ps.sem, 1)

                tile_pairs(pe, BLOCKS // 2, tile)


def combine(nc, out_rows, rows, x_all, weight, x_out):
    with ExitStack() as stack:
        s = Scope(nc, stack, "combine")
        stats = s.sbuf("stats", [P, TILES, 6])
        mean_var = s.sbuf("mean_var", [P, TILES, 2])
        var_eps = s.sbuf("var_eps", [P, TILES])
        rstd = s.sbuf("rstd", [P, TILES])
        loaded = [s.sem(f"loaded{n}") for n in range(TILES // QUAD)]
        shift = s.sbuf("shift", [P, TILES])
        y_stored, shift_done = s.sem("y_stored"), s.sem("shift_done")
        added, summed, stats_done, mean_done, eps_done, std_done, rstd_done, y_done = [
            s.sem(n) for n in ("added", "summed", "stats_done", "mean_done", "eps_done", "std_done", "rstd_done", "y_done")]

        with nc.Block() as block:

            @block.scalar
            def _(act):
                def normalise(n):
                    act.wait_ge(shift_done, n + 1)
                    for t in range(n * QUAD, (n + 1) * QUAD):
                        act.activation(x_all[:, t, :], x_all[:, t, :], ACT.Identity, bias=shift[:, t:t + 1],
                                       scale=rstd[:, t:t + 1]).then_inc(y_done, 1)

                for n in range(TILES // QUAD):
                    act.wait_ge(eps_done, n + 1)
                    act.activation(rstd[:, n * QUAD:(n + 1) * QUAD], var_eps[:, n * QUAD:(n + 1) * QUAD], ACT.Sqrt)\
                        .then_inc(std_done, 1)
                    if n:
                        normalise(n - 1)
                normalise(TILES // QUAD - 1)

            @block.vector
            def _(dve):
                def factors(n):
                    quad = slice(n * QUAD, (n + 1) * QUAD)
                    dve.wait_ge(std_done, n + 1)
                    dve.reciprocal(rstd[:, quad], rstd[:, quad]).then_inc(rstd_done, 1)
                    dve.wait_ge(rstd_done, n + 1)
                    dve.scalar_tensor_tensor(out=shift[:, quad], in0=mean_var[:, quad, 0], scalar=-1.0, in1=rstd[:, quad],
                                             op0=ALU.mult, op1=ALU.mult).then_inc(shift_done, 1)

                for n in range(TILES // QUAD):
                    tiles = range(n * QUAD, (n + 1) * QUAD)
                    dve.wait_ge(loaded[n], TOP_K * DMA)
                    for k, before, now in ((0, None, added), (1, added, summed)):
                        for t in tiles:
                            if before:
                                dve.wait_ge(before, t + 1)
                            dve.scalar_tensor_tensor(out=x_all[:, t, :], in0=rows[:, k, t, :], scalar=weight[:, k, t:t + 1],
                                                     in1=x_all[:, t, :], op0=ALU.mult, op1=ALU.add).then_inc(now, 1)
                    for t in tiles:
                        dve.wait_ge(summed, t + 1)
                        dve.bn_stats(stats[:, t, :], x_all[:, t, :]).then_inc(stats_done, 1)
                    if n:
                        factors(n - 1)
                    for t in tiles:
                        dve.wait_ge(stats_done, t + 1)
                        dve.bn_aggr(mean_var[:, t, :], stats[:, t, :]).then_inc(mean_done, 1)
                    dve.wait_ge(mean_done, (n + 1) * QUAD)
                    quad = slice(n * QUAD, (n + 1) * QUAD)
                    dve.tensor_scalar(var_eps[:, quad], mean_var[:, quad, 1], EPS, None, ALU.add).then_inc(eps_done, 1)
                factors(TILES // QUAD - 1)

            @block.sync
            def _(sp):
                for n in range(0, TILES, QUAD):
                    for k in range(TOP_K):
                        first_row = k * TOKENS + n * P
                        sp.dma_start(rows[:, k, n:n + QUAD, :],
                                     out_rows[first_row:first_row + QUAD * P, :].rearrange("(n p) d -> p n d", p=P))\
                            .then_inc(loaded[n // QUAD], DMA)
                for n in range(0, TILES, QUAD):
                    sp.wait_ge(y_done, n + QUAD)
                    sp.dma_start(x_out[1 + n * P:1 + (n + QUAD) * P, :].rearrange("(n p) d -> p n d", p=P),
                                 x_all[:, n:n + QUAD, :]).then_inc(y_stored, DMA)
                sp.wait_ge(y_stored, TILES // QUAD * DMA)


def load_experts(sp, w_up, w_down, up_dram, down_dram, up_loaded, down_loaded):
    for e in range(EXPERTS):
        if w_up is not None:
            sp.dma_start(w_up[:, e * KT * FF:(e + 1) * KT * FF].rearrange("p (k n) -> p k n", k=KT),
                         up_dram[e].rearrange("(k p) n -> p k n", p=P)).then_inc(up_loaded, DMA)
        if w_down is not None:
            sp.dma_start(w_down[:, e * FT * DIM:(e + 1) * FT * DIM].rearrange("p (f n) -> p f n", f=FT),
                         down_dram[e].rearrange("(f p) n -> p f n", p=P)).then_inc(down_loaded, DMA)


def rotary_tables():
    half = np.arange(0, HEAD_DIM, 2, dtype=np.float32)
    inv_freq = (1.0 / 10000.0 ** (half / HEAD_DIM)).astype(np.float32)
    t = np.arange(TOKENS, dtype=np.float32)
    angle = (t[:, None] * inv_freq[None, :]).astype(np.float32).astype(np.float64)
    base = (half + 0.4 * HEAD_DIM) / (1.4 * HEAD_DIM)
    power = (t - TOKENS // 2) / float(P // 2)
    scale = base[None, :].astype(np.float64) ** power[:, None].astype(np.float64)
    cos, sin = np.cos(angle), np.sin(angle)
    out = [np.concatenate([cos * g, cos * g], 1) if n % 2 == 0 else np.concatenate([-sin * g, sin * g], 1)
           for n, g in ((0, scale), (1, scale), (0, 1 / scale), (1, 1 / scale))]
    return np.stack(out, 1).astype(np.float32)


def window_masks():
    q, k = np.arange(P)[:, None], np.arange(P)[None, :]
    now = np.where(k <= q, 0.0, NEG)
    before = np.where(k >= q, 0.0, NEG)
    never = np.full((P, P), NEG)
    return np.stack([np.stack([now, before], 1), np.stack([before, now], 1), np.stack([now, never], 1)], 1)\
        .astype(np.float32)


def swapped_scales(qs, ks):
    swap = lambda a: np.concatenate([a[HEAD_DIM // 2:], a[:HEAD_DIM // 2]])
    return np.stack([qs, swap(qs), ks, swap(ks)])


def columns(a):
    out = np.zeros((-(-a.shape[0] // P), P), a.dtype)
    out.reshape(-1)[:a.shape[0]] = a
    return out.T


def chunk_constants():
    q, k = np.arange(P)[:, None] % CHUNK, np.arange(CHUNK)[None, :]
    causal = np.where(k > q, -65000.0, 0.0).astype(np.float32)
    own = (np.arange(P)[:, None] // C_DIM == np.arange(HH)[None, :]).astype(np.float32)
    every = np.full((P, P), 1.0 / (4 * CHUNK), np.float32)
    second = every * (np.arange(P)[None, :] >= CHUNK)
    pair = np.arange(P)[:, None, None] // CHUNK == np.arange(2)[None, :, None]
    pair = (pair * np.ones((1, 1, C_DIM))).astype(np.float32)
    return causal, np.stack([own, own / CHUNK], 1).astype(np.float32), np.stack([every, second], 1).astype(np.float32), pair


def filter_constants():
    t = np.linspace(0.0, 1.0, FILTER, dtype=np.float32)
    w = (2.0 * np.pi * np.linspace(0.0, FILTER - 1.0, FILTER, dtype=np.float32) / FILTER).astype(np.float32)
    fw = np.float32(1e-4) * w
    features = np.stack([t, np.cos(fw), -np.sin(fw)]).astype(np.float32)
    deltas = np.linspace(np.log(0.01) / 1.5, np.log(0.01) / 0.3, DIM, dtype=np.float32)
    decay = np.exp(-t[None, :] * np.abs(deltas)[:, None]) + np.float32(0.05)
    return features, np.ascontiguousarray(decay.astype(np.float32).reshape(KT, P, FILTER).transpose(1, 0, 2))


def routing_constants():
    before = np.arange(P)[:, None] < np.arange(P)[None, :]
    return (np.stack([before, np.ones((P, P))], 1).astype(np.float32),
            np.concatenate([np.tile(np.arange(P), (P, 1)), 1 + np.arange(TOP_K * TOKENS).reshape(TOP_K * TILES, P).T], 1).astype(np.float32))
def network(nc, a, out):
    dram = lambda name, rows, cols: nc.dram_tensor(name, (rows, cols), F32).ap()
    stage = [dram(f"stage{n}", TOKENS + 1, DIM) for n in (0, 1)]
    inner = [dram(f"inner{n}", TOKENS + 1, DIM) for n in range(3)]
    taps_by_start = dram("taps_by_start", DIM, STARTS * SPANS)
    x_rows, out_rows = dram("x_rows", TOKENS, DIM), dram("out_rows", TOP_K * TOKENS + ROWS, DIM)

    filter_taps(nc, taps_by_start, a["features"], a["f_w1"], a["b1_freq1"], a["f_w2"], a["b2_freq2"], a["f_w3"],
                a["b3_freq3"], a["f_wout"], a["decay"], a["filt_bias"], stage + inner)
    with ExitStack() as stack:
        s = Scope(nc, stack, "first")
        up_loaded, down_loaded = s.sem("up_loaded"), s.sem("down_loaded")
        half = DIM * STEPS
        low, high = s.sbuf("low", [P, half]), s.sbuf("high", [P, half])
        x0_tok = low[:, :].rearrange("p (c n) -> p c n", c=DIM)
        v_tok = high[:, :].rearrange("p (c n) -> p c n", c=DIM)
        w_down = low[:, :]
        x_all = high[:, 0:TILES * DIM].rearrange("p (t d) -> p t d", t=TILES)
        gated_input(nc, a["u"], a["w_in"], a["in_columns"], a["ident"], x0_tok, v_tok)
        w_up = s.sbuf("w_up", [P, EXPERTS * KT * FF])
        long_convolution(nc, taps_by_start, x0_tok, v_tok,
                         lambda queue: load_experts(queue, w_up, None, a["expert_up"], None, up_loaded, None))
        project_and_norm(nc, x0_tok, a["u"], x_all, a["w_out"], a["b_out"], a["ident"])
        weight = s.sbuf("weight", [P, TOP_K, TILES])
        block_expert = s.sbuf("block_expert", [1, BLOCKS], I32)
        token_of = s.sbuf("token_of", [P, BLOCKS], U32)
        choice_of = s.sbuf("choice_of", [P, BLOCKS], U32)
        route(nc, x_all, x_rows, weight, block_expert, token_of, choice_of, a["router_w"], a["router_b"], a["ident"],
              a["before"], a["numbers"], high[:, TILES * DIM:],
              lambda queue: load_experts(queue, None, w_down, None, a["expert_down"], None, down_loaded))
        experts(nc, x_rows, token_of, choice_of, out_rows, block_expert, w_up, w_down, up_loaded, down_loaded, a["ident"])
        combine(nc, out_rows, low[:, :].rearrange("p (k t d) -> p k t d", k=TOP_K, t=TILES), x_all, weight, stage[0])

    with ExitStack() as stack:
        s = Scope(nc, stack, "last")
        win_loaded, ffn_loaded = s.sem("win_loaded"), s.sem("ffn_loaded")
        w_qkv = s.sbuf("w_qkv", [P, KT, 3 * INNER])
        w_o = s.sbuf("w_o", [P, INNER // P, DIM])
        w_up = s.sbuf("w_up", [P, KT, 2 * HIDDEN])
        w_down = s.sbuf("w_down", [P, HT, DIM])

        def load_window(l):
            return lambda queue: load_window_weights(queue, w_qkv, w_o, a["wqkv"][l], a["wo"][l], win_loaded)

        def load_ffn(l):
            return lambda queue: load_ffn_weights(queue, w_up, w_down, a["w1"][l], a["w2"][l], ffn_loaded)

        chunk_attention(nc, stage[0], stage[1], a["W_qkv"], a["W_out"], a["ident"], a["causal"], a["head_mask"],
                        a["cum_weights"], a["pair_mask"], load_window(0))
        x = stage[1]
        for l in range(2):
            window_attention(nc, l, x, inner[2 * l], w_qkv, w_o, win_loaded, a["qk_scale"][l], a["rotary"], a["ident"],
                             a["window_mask"], load_ffn(l))
            gated_ffn(nc, l, inner[2 * l], inner[1] if l == 0 else out, w_up, w_down, ffn_loaded, a["b1"][l],
                      a["b2"][l], a["ln_g"][l], a["ln_b"][l], a["ident"], *((None, load_window(1)) if l == 0 else (stage[1],)))
            x = inner[1]


def kernel(**inputs):
    import concourse.bacc as bacc
    from concourse.bass_utils import run_bass_kernel_spmd

    i = {name: np.asarray(a) for name, a in inputs.items()}
    A, F, G, H = ({n[len(p):]: a for n, a in i.items() if n.startswith(p)} for p in
                  ("L0_attn_", "L0_ffn_", "L1_attn_", "L1_ffn_"))
    features, decay = filter_constants()
    before, numbers = routing_constants()
    causal, head_mask, cum_weights, pair_mask = chunk_constants()
    hid = H["w2"].shape[1]
    two = lambda a, b: np.stack([a, b], 1)
    layers = range(H["wqkv"].shape[0])
    arrays = {
        "ident": np.eye(P), "u": A["u"][0], "w_in": A["w_in"],
        "in_columns": np.stack([columns(A["b_in"])] + [columns(A["sf_w"][:, n]) for n in range(3)] + [columns(A["sf_b"])], 1),
        "features": features, "decay": decay, "f_w1": A["f_w1"], "b1_freq1": two(A["f_b1"], A["freq1"]),
        "f_w2": A["f_w2"], "b2_freq2": two(A["f_b2"], A["freq2"]), "f_w3": A["f_w3"],
        "b3_freq3": two(A["f_b3"], A["freq3"]), "f_wout": A["f_wout"], "filt_bias": columns(A["filt_bias"]),
        "w_out": A["w_out"], "b_out": A["b_out"][None],
        "router_w": F["router_w"], "router_b": F["router_b"][None], "before": before, "numbers": numbers,
        "expert_up": F["expert_up"].transpose(0, 2, 1), "expert_down": F["expert_down"].transpose(0, 2, 1),
        "W_qkv": G["W_qkv"], "W_out": G["W_out"], "causal": causal, "head_mask": head_mask,
        "cum_weights": cum_weights, "pair_mask": pair_mask,
        "rotary": rotary_tables(), "window_mask": window_masks(), "wqkv": H["wqkv"], "wo": H["wo"],
        "qk_scale": np.stack([swapped_scales(H["q_scale"][l], H["k_scale"][l]) for l in layers]),
        "w1": H["w1"], "b1": np.stack([two(columns(H["b1"][l][:hid]), columns(H["b1"][l][hid:])) for l in layers]),
        "w2": H["w2"], "b2": H["b2"], "ln_g": np.stack([columns(H["ln_g"][l]) for l in layers]),
        "ln_b": np.stack([columns(H["ln_b"][l]) for l in layers]),
    }
    arrays = {n: np.ascontiguousarray(a, dtype=np.float32) for n, a in arrays.items()}
    nc = bacc.Bacc("TRN2", target_bir_lowering=False, num_devices=1)
    drams = {n: nc.dram_tensor(n, a.shape, F32, kind="ExternalInput").ap() for n, a in arrays.items()}
    out = nc.dram_tensor("out", (TOKENS, DIM), F32, kind="ExternalOutput").ap()
    network(nc, drams, out)
    got = run_bass_kernel_spmd(nc, [arrays], core_ids=[0])
    return got.results[0]["out"].reshape(1, TOKENS, DIM)
```
